# Optimizing a Trainium2 kernel written in Bass

```python
import numpy as np
import jax
import jax.numpy as jnp

def _softmax(x, axis=-1):
    return jax.nn.softmax(x, axis=axis)

def _gelu(x):
    return jax.nn.gelu(x, approximate=True)

def _silu(x):
    return jax.nn.silu(x)

def _sigmoid(x):
    return jax.nn.sigmoid(x)

def _layernorm(x, axis=-1, eps=1e-05):
    m = jnp.mean(x, axis=axis, keepdims=True)
    v = jnp.var(x, axis=axis, keepdims=True)
    return (x - m) / jnp.sqrt(v + eps)

def _scatter_add(tgt, idx, src, axis=0):
    return tgt.at[idx].add(src)

def _segment_sum(src, seg, n):
    return jax.ops.segment_sum(src, seg, n)
kernel_name = 'mk_flamingo_gated_d4_seqx_r8_1e69f1'

def setup_inputs(seed: int=0):
    np.random.seed(seed)
    _w = jnp.asarray

    def _rec_inputs():
        import jax
        import jax.numpy as jnp
        _rk = jax.random.key(seed)
        x = 7.22e-05 + 1 * jax.random.normal(jax.random.fold_in(_rk, 1), (16, 128, 128), jnp.float32)
        _lenS = 128 - jax.random.randint(jax.random.fold_in(_rk, 7), (16,), 0, max(1, 128 // 4) + 1, jnp.int32)
        _lenS2 = 128 - jax.random.randint(jax.random.fold_in(_rk, 8), (16,), 0, max(1, 128 // 4) + 1, jnp.int32)
        _ctx_1024P = jax.random.normal(jax.random.fold_in(_rk, 11), (16, 16, 128), jnp.float32)
        _ctx_1024c = jax.random.dirichlet(jax.random.fold_in(_rk, 511), 0.3 * jnp.ones((16,), jnp.float32), (16, 128))
        _ctx_1024t = jnp.einsum('bsk,bkd->bsd', _ctx_1024c, _ctx_1024P)
        _ctx_1024t = _ctx_1024t * jax.lax.rsqrt(jnp.mean(jnp.square(_ctx_1024t)) + 1e-12) * 0.953939
        ctx_1024 = 4.13588e-05 + 0.999923 * (_ctx_1024t + 0.3 * jax.random.normal(jax.random.fold_in(_rk, 611), (16, 128, 128), jnp.float32))
        _validS = jnp.arange(128)[None, :] < _lenS[:, None]
        _validS2 = jnp.arange(128)[None, :] < _lenS2[:, None]
        _causal = jnp.tril(jnp.ones((128, 128), dtype=bool))
        mask_BxS2_if1 = jnp.where(jnp.ones((16, 128), dtype=bool), 1, 0).astype(jnp.int32)
        mask_BxSxS2_if1 = jnp.where(jnp.ones((16, 128, 128), dtype=bool), 1, 0).astype(jnp.int32)
        mask_BxS2_bk1 = jnp.broadcast_to(_validS2[:, :], (16, 128))
        _g = jax.random.normal(jax.random.fold_in(_rk, 9001), (2, 4), jnp.float32)
        _g = jnp.sign(_g) * jnp.maximum(jnp.abs(_g), 1.0) + (_g == 0) * 1.0
        g_xattn = _g[0]
        g_ffn = _g[1]
        return (x, ctx_1024, mask_BxS2_if1, mask_BxSxS2_if1, mask_BxS2_bk1, g_xattn, g_ffn)
    x, ctx_1024, mask_BxS2_if1, mask_BxSxS2_if1, mask_BxS2_bk1, g_xattn, g_ffn = _rec_inputs()

    def _L0_xattn_setup():
        import jax, jax.numpy as jnp
        import numpy as np
        D_MODEL = 128
        N_HEADS = 16
        D_K = D_MODEL // N_HEADS
        key = jax.random.key(seed)
        ks = jax.random.split(key, 12)
        B, S, D = (4, 256, D_MODEL)
        scale = 1.0 / np.sqrt(D)
        inp = {'query': jax.random.normal(ks[0], (B, S, D), jnp.float32), 'key': jax.random.normal(ks[1], (B, S, D), jnp.float32), 'value': jax.random.normal(ks[2], (B, S, D), jnp.float32), 'Wq': jax.random.normal(ks[3], (D, D), jnp.float32) * scale, 'bq': jax.random.normal(ks[4], (D,), jnp.float32) * 0.02, 'Wk': jax.random.normal(ks[5], (D, D), jnp.float32) * scale, 'bk': jax.random.normal(ks[6], (D,), jnp.float32) * 0.02, 'Wv': jax.random.normal(ks[7], (D, D), jnp.float32) * scale, 'bv': jax.random.normal(ks[8], (D,), jnp.float32) * 0.02, 'Wo': jax.random.normal(ks[9], (D, D), jnp.float32) * scale, 'bo': jax.random.normal(ks[10], (D,), jnp.float32) * 0.02}
        return inp
    _L0_xattn_all = _L0_xattn_setup()
    _L0_xattn_in = {k: v for k, v in _L0_xattn_all.items() if k in ('Wq', 'bq', 'Wk', 'bk', 'Wv', 'bv', 'Wo', 'bo')}
    del _L0_xattn_all

    def _L0_ffn_setup():
        import jax, jax.numpy as jnp
        import numpy as np
        H = 128
        I = 4 * H
        E = 8
        K = 2
        B, S = (2, 128)
        STD = 0.02 / np.sqrt(H)
        key = jax.random.key(seed)
        ks = jax.random.split(key, 8)
        x = jax.random.normal(ks[0], (B, S, H), dtype=jnp.float32)
        gate_w = jax.random.normal(ks[1], (H, E), dtype=jnp.float32) * STD
        bias = jnp.zeros((E,), dtype=jnp.float32)
        up_w = jax.random.normal(ks[2], (E, H, I), dtype=jnp.float32) * STD
        up_b = jnp.zeros((E, I), dtype=jnp.float32)
        down_w = jax.random.normal(ks[3], (E, I, H), dtype=jnp.float32) * STD
        down_b = jnp.zeros((E, H), dtype=jnp.float32)
        sw_up = jax.random.normal(ks[4], (H, I), dtype=jnp.float32) * STD
        sb_up = jnp.zeros((I,), dtype=jnp.float32)
        sw_down = jax.random.normal(ks[5], (I, H), dtype=jnp.float32) * STD
        sb_down = jnp.zeros((H,), dtype=jnp.float32)
        return {'x': x, 'gate_w': gate_w, 'bias': bias, 'up_w': up_w, 'up_b': up_b, 'down_w': down_w, 'down_b': down_b, 'sw_up': sw_up, 'sb_up': sb_up, 'sw_down': sw_down, 'sb_down': sb_down}
    _L0_ffn_all = _L0_ffn_setup()
    _L0_ffn_in = {k: v for k, v in _L0_ffn_all.items() if k in ('gate_w', 'bias', 'up_w', 'up_b', 'down_w', 'down_b', 'sw_up', 'sb_up', 'sw_down', 'sb_down')}
    del _L0_ffn_all

    def _L1_xattn_setup():
        import jax, jax.numpy as jnp
        import numpy as np
        D_MODEL = 128
        N_HEADS = 16
        HEAD_DIM = D_MODEL // N_HEADS
        key = jax.random.key(seed)
        ks = jax.random.split(key, 10)
        B, LQ, LKV = (4, 128, 256)
        inv = 1.0 / np.sqrt(D_MODEL)
        inp = {'query': jax.random.normal(ks[0], (B, LQ, D_MODEL), dtype=jnp.float32), 'key_value': jax.random.normal(ks[1], (B, LKV, D_MODEL), dtype=jnp.float32), 'attention_mask': jnp.ones((B, LKV), dtype=jnp.int32), 'Wq': jax.random.normal(ks[2], (D_MODEL, D_MODEL), dtype=jnp.float32) * inv, 'bq': jnp.zeros((D_MODEL,), dtype=jnp.float32), 'Wk': jax.random.normal(ks[3], (D_MODEL, D_MODEL), dtype=jnp.float32) * inv, 'bk': jnp.zeros((D_MODEL,), dtype=jnp.float32), 'Wv': jax.random.normal(ks[4], (D_MODEL, D_MODEL), dtype=jnp.float32) * inv, 'bv': jnp.zeros((D_MODEL,), dtype=jnp.float32), 'Wo': jax.random.normal(ks[5], (D_MODEL, D_MODEL), dtype=jnp.float32) * inv, 'bo': jnp.zeros((D_MODEL,), dtype=jnp.float32)}
        return inp
    _L1_xattn_all = _L1_xattn_setup()
    _L1_xattn_in = {k: v for k, v in _L1_xattn_all.items() if k in ('Wq', 'bq', 'Wk', 'bk', 'Wv', 'bv', 'Wo', 'bo')}
    del _L1_xattn_all

    def _L1_ffn_setup():
        import jax, jax.numpy as jnp
        import numpy as np
        B, S, H, F, G = (8, 256, 128, 512, 128)
        EPS = 1e-05

        def _dequant(q, scales, g):
            K, N = q.shape
            w = (q.astype(jnp.float32) - 128.0).reshape(K // g, g, N) * scales[:, None, :]
            return w.reshape(K, N)
        key = jax.random.key(seed)
        ks = jax.random.split(key, 8)
        x = jax.random.normal(ks[0], (B, S, H), dtype=jnp.float32)
        ln_gamma = jnp.ones((H,), jnp.float32)
        ln_beta = jnp.zeros((H,), jnp.float32)
        fc1_q = jax.random.randint(ks[1], (H, F), 0, 32, dtype=jnp.int32)
        fc2_q = jax.random.randint(ks[2], (F, H), 0, 32, dtype=jnp.int32)
        fc1_scales = jax.random.uniform(ks[3], (H // G, F), jnp.float32) * 0.02 + 0.001
        fc2_scales = jax.random.uniform(ks[4], (F // G, H), jnp.float32) * 0.02 + 0.001
        fc1_bias = jax.random.normal(ks[5], (F,), jnp.float32) * 0.02
        fc2_bias = jax.random.normal(ks[6], (H,), jnp.float32) * 0.02
        return {'x': x, 'ln_gamma': ln_gamma, 'ln_beta': ln_beta, 'fc1_q': fc1_q, 'fc1_scales': fc1_scales, 'fc1_bias': fc1_bias, 'fc2_q': fc2_q, 'fc2_scales': fc2_scales, 'fc2_bias': fc2_bias}
    _L1_ffn_all = _L1_ffn_setup()
    _L1_ffn_in = {k: v for k, v in _L1_ffn_all.items() if k in ('ln_gamma', 'ln_beta', 'fc1_q', 'fc1_scales', 'fc1_bias', 'fc2_q', 'fc2_scales', 'fc2_bias')}
    del _L1_ffn_all

    def _L2_xattn_setup():
        import jax, jax.numpy as jnp
        import numpy as np
        H = 16
        key = jax.random.key(seed)
        ks = jax.random.split(key, 8)
        B, S, D = (2, 256, 128)
        q = jax.random.normal(ks[0], (B, S, D), dtype=jnp.float32)
        k = jax.random.normal(ks[1], (B, S, D), dtype=jnp.float32)
        v = jax.random.normal(ks[2], (B, S, D), dtype=jnp.float32)
        mask = jnp.ones((B, S, S), dtype=jnp.int32)
        scale = 1.0 / np.sqrt(D)
        Wq = jax.random.normal(ks[3], (D, D), dtype=jnp.float32) * scale
        Wk = jax.random.normal(ks[4], (D, D), dtype=jnp.float32) * scale
        Wv = jax.random.normal(ks[5], (D, D), dtype=jnp.float32) * scale
        Wo = jax.random.normal(ks[6], (D, D), dtype=jnp.float32) * scale
        return {'q': q, 'k': k, 'v': v, 'mask': mask, 'Wq': Wq, 'Wk': Wk, 'Wv': Wv, 'Wo': Wo}
    _L2_xattn_all = _L2_xattn_setup()
    _L2_xattn_in = {k: v for k, v in _L2_xattn_all.items() if k in ('Wq', 'Wk', 'Wv', 'Wo')}
    del _L2_xattn_all

    def _L2_ffn_setup():
        import jax, jax.numpy as jnp
        import numpy as np
        BLOCK = 32
        W_BITS = 4
        ACT_BITS = 16

        def act_qdq(x):
            qmax = 2.0 ** (ACT_BITS - 1) - 1.0
            scale = jnp.maximum(jnp.max(jnp.abs(x)) / qmax, 1e-12)
            return jnp.clip(jnp.round(x / scale), -qmax - 1.0, qmax) * scale

        def fixed_qdq_u16(x):
            scale = 1.0 / 65536.0
            return jnp.clip(jnp.round(x / scale), 0.0, 65535.0) * scale

        def lpbq_dequant(w):
            O, I = w.shape
            qmax = 2.0 ** (W_BITS - 1) - 1.0
            wb = w.reshape(O, I // BLOCK, BLOCK)
            s = jnp.maximum(jnp.max(jnp.abs(wb), axis=-1, keepdims=True) / qmax, 1e-12)
            wq = jnp.clip(jnp.round(wb / s), -qmax - 1.0, qmax) * s
            return wq.reshape(O, I)
        key = jax.random.key(seed)
        k1, k2, k3, k4 = jax.random.split(key, 4)
        B, S, H, I = (2, 512, 128, 384)
        x = jax.random.normal(k1, (B, S, H), jnp.float32)
        w_gate = jax.random.normal(k2, (I, H), jnp.float32) * 0.02
        w_up = jax.random.normal(k3, (I, H), jnp.float32) * 0.02
        w_down = jax.random.normal(k4, (H, I), jnp.float32) * 0.02
        return {'x': x, 'w_gate': w_gate, 'w_up': w_up, 'w_down': w_down}
    _L2_ffn_all = _L2_ffn_setup()
    _L2_ffn_in = {k: v for k, v in _L2_ffn_all.items() if k in ('w_gate', 'w_up', 'w_down')}
    del _L2_ffn_all

    def _L3_xattn_setup():
        import jax, jax.numpy as jnp
        import numpy as np
        B, S, T, D, H = (4, 256, 256, 128, 16)
        HD = D // H
        key = jax.random.key(seed)
        ks = jax.random.split(key, 7)
        src = jax.random.normal(ks[0], (B, S, D), dtype=jnp.float32)
        tgt = jax.random.normal(ks[1], (B, T, D), dtype=jnp.float32)
        attention_mask = jax.random.bernoulli(ks[2], 0.9, (B, S))
        scale = 1.0 / np.sqrt(D)
        Wq = jax.random.normal(ks[3], (D, D), dtype=jnp.float32) * scale
        Wk = jax.random.normal(ks[4], (D, D), dtype=jnp.float32) * scale
        Wv = jax.random.normal(ks[5], (D, D), dtype=jnp.float32) * scale
        Wo = jax.random.normal(ks[6], (D, D), dtype=jnp.float32) * scale
        return {'src': src, 'tgt': tgt, 'attention_mask': attention_mask, 'Wq': Wq, 'Wk': Wk, 'Wv': Wv, 'Wo': Wo}
    _L3_xattn_all = _L3_xattn_setup()
    _L3_xattn_in = {k: v for k, v in _L3_xattn_all.items() if k in ('Wq', 'Wk', 'Wv', 'Wo')}
    del _L3_xattn_all

    def _L3_ffn_setup():
        import jax, jax.numpy as jnp
        import numpy as np
        INT8_MAX = 127.0

        def _absmax_scale(x, axes):
            amax = jnp.max(jnp.abs(x), axis=axes, keepdims=True)
            return jnp.maximum(amax, 1e-12) / INT8_MAX
        key = jax.random.key(seed)
        k1, k2 = jax.random.split(key)
        lhs = jax.random.normal(k1, (4, 1024, 128), dtype=jnp.float32)
        rhs = jax.random.normal(k2, (128, 128), dtype=jnp.float32)
        return {'lhs': lhs, 'rhs': rhs}
    _L3_ffn_all = _L3_ffn_setup()
    _L3_ffn_in = {k: v for k, v in _L3_ffn_all.items() if k in ('rhs',)}
    del _L3_ffn_all
    return {'x': x, 'ctx_1024': ctx_1024, 'mask_BxS2_if1': mask_BxS2_if1, 'mask_BxSxS2_if1': mask_BxSxS2_if1, 'mask_BxS2_bk1': mask_BxS2_bk1, 'g_xattn': g_xattn, 'g_ffn': g_ffn, 'L0_xattn_Wq': _L0_xattn_in['Wq'], 'L0_xattn_bq': _L0_xattn_in['bq'], 'L0_xattn_Wk': _L0_xattn_in['Wk'], 'L0_xattn_bk': _L0_xattn_in['bk'], 'L0_xattn_Wv': _L0_xattn_in['Wv'], 'L0_xattn_bv': _L0_xattn_in['bv'], 'L0_xattn_Wo': _L0_xattn_in['Wo'], 'L0_xattn_bo': _L0_xattn_in['bo'], 'L0_ffn_gate_w': _L0_ffn_in['gate_w'], 'L0_ffn_bias': _L0_ffn_in['bias'], 'L0_ffn_up_w': _L0_ffn_in['up_w'], 'L0_ffn_up_b': _L0_ffn_in['up_b'], 'L0_ffn_down_w': _L0_ffn_in['down_w'], 'L0_ffn_down_b': _L0_ffn_in['down_b'], 'L0_ffn_sw_up': _L0_ffn_in['sw_up'], 'L0_ffn_sb_up': _L0_ffn_in['sb_up'], 'L0_ffn_sw_down': _L0_ffn_in['sw_down'], 'L0_ffn_sb_down': _L0_ffn_in['sb_down'], 'L1_xattn_Wq': _L1_xattn_in['Wq'], 'L1_xattn_bq': _L1_xattn_in['bq'], 'L1_xattn_Wk': _L1_xattn_in['Wk'], 'L1_xattn_bk': _L1_xattn_in['bk'], 'L1_xattn_Wv': _L1_xattn_in['Wv'], 'L1_xattn_bv': _L1_xattn_in['bv'], 'L1_xattn_Wo': _L1_xattn_in['Wo'], 'L1_xattn_bo': _L1_xattn_in['bo'], 'L1_ffn_ln_gamma': _L1_ffn_in['ln_gamma'], 'L1_ffn_ln_beta': _L1_ffn_in['ln_beta'], 'L1_ffn_fc1_q': _L1_ffn_in['fc1_q'], 'L1_ffn_fc1_scales': _L1_ffn_in['fc1_scales'], 'L1_ffn_fc1_bias': _L1_ffn_in['fc1_bias'], 'L1_ffn_fc2_q': _L1_ffn_in['fc2_q'], 'L1_ffn_fc2_scales': _L1_ffn_in['fc2_scales'], 'L1_ffn_fc2_bias': _L1_ffn_in['fc2_bias'], 'L2_xattn_Wq': _L2_xattn_in['Wq'], 'L2_xattn_Wk': _L2_xattn_in['Wk'], 'L2_xattn_Wv': _L2_xattn_in['Wv'], 'L2_xattn_Wo': _L2_xattn_in['Wo'], 'L2_ffn_w_gate': _L2_ffn_in['w_gate'], 'L2_ffn_w_up': _L2_ffn_in['w_up'], 'L2_ffn_w_down': _L2_ffn_in['w_down'], 'L3_xattn_Wq': _L3_xattn_in['Wq'], 'L3_xattn_Wk': _L3_xattn_in['Wk'], 'L3_xattn_Wv': _L3_xattn_in['Wv'], 'L3_xattn_Wo': _L3_xattn_in['Wo'], 'L3_ffn_rhs': _L3_ffn_in['rhs']}

def reference(x, ctx_1024, mask_BxS2_if1, mask_BxSxS2_if1, mask_BxS2_bk1, g_xattn, g_ffn, L0_xattn_Wq, L0_xattn_bq, L0_xattn_Wk, L0_xattn_bk, L0_xattn_Wv, L0_xattn_bv, L0_xattn_Wo, L0_xattn_bo, L0_ffn_gate_w, L0_ffn_bias, L0_ffn_up_w, L0_ffn_up_b, L0_ffn_down_w, L0_ffn_down_b, L0_ffn_sw_up, L0_ffn_sb_up, L0_ffn_sw_down, L0_ffn_sb_down, L1_xattn_Wq, L1_xattn_bq, L1_xattn_Wk, L1_xattn_bk, L1_xattn_Wv, L1_xattn_bv, L1_xattn_Wo, L1_xattn_bo, L1_ffn_ln_gamma, L1_ffn_ln_beta, L1_ffn_fc1_q, L1_ffn_fc1_scales, L1_ffn_fc1_bias, L1_ffn_fc2_q, L1_ffn_fc2_scales, L1_ffn_fc2_bias, L2_xattn_Wq, L2_xattn_Wk, L2_xattn_Wv, L2_xattn_Wo, L2_ffn_w_gate, L2_ffn_w_up, L2_ffn_w_down, L3_xattn_Wq, L3_xattn_Wk, L3_xattn_Wv, L3_xattn_Wo, L3_ffn_rhs):
    import jax
    import jax.numpy as jnp

    def _L0_xattn_ref(query, key, value, Wq, bq, Wk, bk, Wv, bv, Wo, bo):
        import jax, jax.numpy as jnp
        import numpy as np
        D_MODEL = 128
        N_HEADS = 16
        D_K = D_MODEL // N_HEADS
        B, S, D = query.shape

        def proj(x, W, b):
            y = jnp.einsum('bsd,ed->bse', x, W) + b
            return y.reshape(B, S, N_HEADS, D_K).transpose(0, 2, 1, 3)
        q = proj(query, Wq, bq)
        k = proj(key, Wk, bk)
        v = proj(value, Wv, bv)
        scores = jnp.einsum('bhqd,bhkd->bhqk', q, k) / jnp.sqrt(jnp.float32(D_K))
        attn = jax.nn.softmax(scores, axis=-1)
        out = jnp.einsum('bhqk,bhkd->bhqd', attn, v)
        out = out.transpose(0, 2, 1, 3).reshape(B, S, D)
        return jnp.einsum('bsd,ed->bse', out, Wo) + bo

    def _L0_ffn_ref(x, gate_w, bias, up_w, up_b, down_w, down_b, sw_up, sb_up, sw_down, sb_down):
        import jax, jax.numpy as jnp
        import numpy as np
        H = 128
        I = 4 * H
        E = 8
        K = 2
        B, S = (2, 128)
        STD = 0.02 / np.sqrt(H)
        b, s, h = x.shape
        xf = x.reshape(-1, h)
        T = xf.shape[0]
        scores = jax.nn.sigmoid(xf @ gate_w + bias)
        top_scores, top_idx = jax.lax.top_k(scores, K)
        top_scores = top_scores / (jnp.sum(top_scores, axis=-1, keepdims=True) + 1e-06)
        w = jnp.zeros((T, E), dtype=xf.dtype).at[jnp.arange(T)[:, None], top_idx].add(top_scores)
        up = jnp.einsum('th,ehi->tei', xf, up_w) + up_b
        hact = jax.nn.gelu(up, approximate=False)
        eo = jnp.einsum('tei,eih->teh', hact, down_w) + down_b
        combined = jnp.einsum('teh,te->th', eo * 0.1, w)
        shared = (jax.nn.gelu(xf @ sw_up + sb_up, approximate=False) @ sw_down + sb_down) * 0.1
        out = (shared + combined).reshape(b, s, h)
        out = out / (jnp.max(jnp.abs(out), axis=-1, keepdims=True) + 1e-06)
        return out

    def _L1_xattn_ref(query, key_value, attention_mask, Wq, bq, Wk, bk, Wv, bv, Wo, bo):
        import jax, jax.numpy as jnp
        import numpy as np
        D_MODEL = 128
        N_HEADS = 16
        HEAD_DIM = D_MODEL // N_HEADS
        B, LQ, _ = query.shape
        LKV = key_value.shape[1]
        scale = HEAD_DIM ** (-0.5)
        q = (query @ Wq + bq).reshape(B, LQ, N_HEADS, HEAD_DIM).transpose(0, 2, 1, 3)
        k = (key_value @ Wk + bk).reshape(B, LKV, N_HEADS, HEAD_DIM).transpose(0, 2, 1, 3)
        v = (key_value @ Wv + bv).reshape(B, LKV, N_HEADS, HEAD_DIM).transpose(0, 2, 1, 3)
        scores = jnp.einsum('bhqd,bhkd->bhqk', q, k) * scale
        mask = (attention_mask != 0)[:, None, None, :]
        scores = jnp.where(mask, scores, -jnp.inf)
        attn = jax.nn.softmax(scores, axis=-1)
        context = jnp.einsum('bhqk,bhkd->bhqd', attn, v)
        context = context.transpose(0, 2, 1, 3).reshape(B, LQ, D_MODEL)
        return context @ Wo + bo

    def _L1_ffn_ref(x, ln_gamma, ln_beta, fc1_q, fc1_scales, fc1_bias, fc2_q, fc2_scales, fc2_bias):
        import jax, jax.numpy as jnp
        import numpy as np
        B, S, H, F, G = (8, 256, 128, 512, 128)
        EPS = 1e-05

        def _dequant(q, scales, g):
            K, N = q.shape
            w = (q.astype(jnp.float32) - 128.0).reshape(K // g, g, N) * scales[:, None, :]
            return w.reshape(K, N)
        residual = x
        mu = jnp.mean(x, axis=-1, keepdims=True)
        var = jnp.mean(jnp.square(x - mu), axis=-1, keepdims=True)
        h = (x - mu) * jax.lax.rsqrt(var + EPS) * ln_gamma + ln_beta
        hf = h.reshape(-1, H)
        w1 = _dequant(fc1_q, fc1_scales, G)
        y = hf @ w1 + fc1_bias
        y = jax.nn.silu(y)
        w2 = _dequant(fc2_q, fc2_scales, G)
        z = y @ w2 + fc2_bias
        return residual + 0.5 * z.reshape(residual.shape)

    def _L2_xattn_ref(q, k, v, mask, Wq, Wk, Wv, Wo):
        import jax, jax.numpy as jnp
        import numpy as np
        H = 16
        B, S, D = q.shape
        dk = D // H
        query = (q @ Wq.T).reshape(B, S, H, dk).transpose(0, 2, 1, 3)
        key_ = (k @ Wk.T).reshape(B, S, H, dk).transpose(0, 2, 1, 3)
        value = (v @ Wv.T).reshape(B, S, H, dk).transpose(0, 2, 1, 3)
        scores = jnp.einsum('bhqd,bhkd->bhqk', query, key_) / jnp.sqrt(jnp.float32(dk))
        scores = jnp.where(mask[:, None, :, :] == 0, jnp.float32(-1000000000.0), scores)
        attn = jax.nn.softmax(scores, axis=-1)
        x = jnp.einsum('bhqk,bhkd->bhqd', attn, value)
        x = x.transpose(0, 2, 1, 3).reshape(B, S, D)
        return x @ Wo.T

    def _L2_ffn_ref(x, w_gate, w_up, w_down):
        import jax, jax.numpy as jnp
        import numpy as np
        BLOCK = 32
        W_BITS = 4
        ACT_BITS = 16

        def act_qdq(x):
            qmax = 2.0 ** (ACT_BITS - 1) - 1.0
            scale = jnp.maximum(jnp.max(jnp.abs(x)) / qmax, 1e-12)
            return jnp.clip(jnp.round(x / scale), -qmax - 1.0, qmax) * scale

        def fixed_qdq_u16(x):
            scale = 1.0 / 65536.0
            return jnp.clip(jnp.round(x / scale), 0.0, 65535.0) * scale

        def lpbq_dequant(w):
            O, I = w.shape
            qmax = 2.0 ** (W_BITS - 1) - 1.0
            wb = w.reshape(O, I // BLOCK, BLOCK)
            s = jnp.maximum(jnp.max(jnp.abs(wb), axis=-1, keepdims=True) / qmax, 1e-12)
            wq = jnp.clip(jnp.round(wb / s), -qmax - 1.0, qmax) * s
            return wq.reshape(O, I)
        x = act_qdq(x)
        up = act_qdq(x @ lpbq_dequant(w_up).T)
        gate = act_qdq(x @ lpbq_dequant(w_gate).T)
        sig = fixed_qdq_u16(jax.nn.sigmoid(gate))
        gate = act_qdq(gate * sig)
        o = act_qdq(gate * up)
        return o @ lpbq_dequant(w_down).T

    def _L3_xattn_ref(src, tgt, attention_mask, Wq, Wk, Wv, Wo):
        import jax, jax.numpy as jnp
        import numpy as np
        B, S, T, D, H = (4, 256, 256, 128, 16)
        HD = D // H
        b, s, d = src.shape
        t = tgt.shape[1]
        q = (tgt @ Wq.T).reshape(b, t, H, HD).transpose(0, 2, 1, 3)
        k = (src @ Wk.T).reshape(b, s, H, HD).transpose(0, 2, 1, 3)
        v = (src @ Wv.T).reshape(b, s, H, HD).transpose(0, 2, 1, 3)
        scores = jnp.einsum('bhtd,bhsd->bhts', q, k) / np.sqrt(HD)
        mask = attention_mask[:, None, None, :]
        scores = jnp.where(mask, scores, -jnp.inf)
        attn = jax.nn.softmax(scores, axis=-1)
        out = jnp.einsum('bhts,bhsd->bhtd', attn, v)
        out = out.transpose(0, 2, 1, 3).reshape(b, t, d)
        return out @ Wo.T

    def _L3_ffn_ref(lhs, rhs):
        import jax, jax.numpy as jnp
        import numpy as np
        INT8_MAX = 127.0

        def _absmax_scale(x, axes):
            amax = jnp.max(jnp.abs(x), axis=axes, keepdims=True)
            return jnp.maximum(amax, 1e-12) / INT8_MAX
        lhs_scale = _absmax_scale(lhs, (2,))
        rhs_scale = _absmax_scale(rhs, (0,))
        q_lhs = jnp.clip(jnp.round(lhs / lhs_scale), -INT8_MAX, INT8_MAX).astype(jnp.int8)
        q_rhs = jnp.clip(jnp.round(rhs / rhs_scale), -INT8_MAX, INT8_MAX).astype(jnp.int8)
        acc = jax.lax.dot_general(q_lhs, q_rhs, (((2,), (0,)), ((), ())), preferred_element_type=jnp.int32)
        return acc.astype(jnp.float32) * lhs_scale * rhs_scale
    x = x + jnp.tanh(g_xattn[0]) * _L0_xattn_ref(_layernorm(x, axis=-1), ctx_1024, ctx_1024, L0_xattn_Wq, L0_xattn_bq, L0_xattn_Wk, L0_xattn_bk, L0_xattn_Wv, L0_xattn_bv, L0_xattn_Wo, L0_xattn_bo)
    x = x + jnp.tanh(g_ffn[0]) * _L0_ffn_ref(_layernorm(x, axis=-1), L0_ffn_gate_w, L0_ffn_bias, L0_ffn_up_w, L0_ffn_up_b, L0_ffn_down_w, L0_ffn_down_b, L0_ffn_sw_up, L0_ffn_sb_up, L0_ffn_sw_down, L0_ffn_sb_down)
    x = x + jnp.tanh(g_xattn[1]) * _L1_xattn_ref(_layernorm(x, axis=-1), ctx_1024, mask_BxS2_if1, L1_xattn_Wq, L1_xattn_bq, L1_xattn_Wk, L1_xattn_bk, L1_xattn_Wv, L1_xattn_bv, L1_xattn_Wo, L1_xattn_bo)
    x = x + jnp.tanh(g_ffn[1]) * _L1_ffn_ref(_layernorm(x, axis=-1), L1_ffn_ln_gamma, L1_ffn_ln_beta, L1_ffn_fc1_q, L1_ffn_fc1_scales, L1_ffn_fc1_bias, L1_ffn_fc2_q, L1_ffn_fc2_scales, L1_ffn_fc2_bias)
    x = x + jnp.tanh(g_xattn[2]) * _L2_xattn_ref(_layernorm(x, axis=-1), ctx_1024, ctx_1024, mask_BxSxS2_if1, L2_xattn_Wq, L2_xattn_Wk, L2_xattn_Wv, L2_xattn_Wo)
    x = x + jnp.tanh(g_ffn[2]) * _L2_ffn_ref(_layernorm(x, axis=-1), L2_ffn_w_gate, L2_ffn_w_up, L2_ffn_w_down)
    x = x + jnp.tanh(g_xattn[3]) * _L3_xattn_ref(ctx_1024, _layernorm(x, axis=-1), mask_BxS2_bk1, L3_xattn_Wq, L3_xattn_Wk, L3_xattn_Wv, L3_xattn_Wo)
    x = x + jnp.tanh(g_ffn[3]) * _L3_ffn_ref(_layernorm(x, axis=-1), L3_ffn_rhs)
    return x

_drawn_inputs = setup_inputs


def setup_inputs(seed=0):
    import zlib

    import numpy as np

    out = dict(_drawn_inputs(seed))
    spreads = {'L0_ffn_bias': (0.0, 0.1),
     'L0_ffn_up_b': (0.0, 0.8),
     'L0_ffn_down_b': (0.0, 0.1),
     'L0_ffn_sb_up': (0.0, 0.8),
     'L0_ffn_sb_down': (0.0, 0.1),
     'L1_xattn_bq': (0.0, 0.669),
     'L1_xattn_bk': (0.0, 2.0),
     'L1_xattn_bv': (0.0, 0.1),
     'L1_xattn_bo': (0.0, 0.1),
     'L1_ffn_ln_gamma': (1.0, 0.2),
     'L1_ffn_ln_beta': (0.0, 0.1)}
    factors = {'L0_xattn_bq': 25.335,
     'L0_xattn_bk': 200.0,
     'L0_xattn_bv': 3.229,
     'L0_xattn_bo': 3.063,
     'L0_ffn_up_w': 23.866,
     'L0_ffn_down_w': 8.0,
     'L0_ffn_sw_up': 8.0,
     'L0_ffn_sw_down': 8.0,
     'L1_ffn_fc1_scales': 20.749,
     'L1_ffn_fc1_bias': 200.0,
     'L1_ffn_fc2_bias': 200.0,
     'L2_xattn_Wq': 55.02,
     'L2_xattn_Wk': 56.551,
     'L2_xattn_Wv': 49.774,
     'L2_xattn_Wo': 51.227,
     'L2_ffn_w_gate': 64.0,
     'L2_ffn_w_up': 64.0,
     'L2_ffn_w_down': 64.0,
     'L3_xattn_Wq': 59.796,
     'L3_xattn_Wk': 61.137,
     'L3_xattn_Wv': 53.522,
     'L3_xattn_Wo': 54.628,
     'L3_ffn_rhs': 177.782}
    for name, (base, spread) in spreads.items():
        noise = np.random.default_rng([zlib.crc32(name.encode()), seed]).standard_normal(out[name].shape)
        drawn = base * np.exp(spread * noise) if base else spread * noise
        out[name] = jnp.asarray(drawn.astype(out[name].dtype))
    for name, factor in factors.items():
        out[name] = (out[name] * factor).astype(out[name].dtype)
    return out
```

```python
from contextlib import ExitStack

import numpy as np

import concourse.bass as bass
from concourse import mybir

F32 = mybir.dt.float32
F16 = mybir.dt.float16
I32 = mybir.dt.int32
U8 = mybir.dt.uint8
ACT = mybir.ActivationFunctionType
ALU = mybir.AluOpType
AX = mybir.AxisListType
ABSMAX = bass.bass_isa.ReduceOp.absmax

P = 128
NB = 16
NL = 4
NH = 16
DK = 8
NC = 4
CT = 512
BC = NB // NC
NG = 4
NE = 9
NI = 4
BIG = 32768.0
MASK_ROW, MAX_ROW = 3, 7
ROUND = 12582912.0
EPS = 1e-5

R_GATES, R_GBIAS, R_PRIO, R_BV, R_BO = 0, 8, 16, 24, 536
R_B2, R_S2, R_N = 1048, 1176, 1688
C_BQ, C_BK, C_UB, C_S1, C_B1, C_GAMMA, C_BETA, C_GW, C_N = 0, 4, 8, 44, 48, 52, 53, 54, 62
A_Q, A_K, A_V, A_CTX, A_UP, A_DN, A_GW, A_UB, A_N = 0, 4, 8, 9, 10, 19, 28, 29, 38

UNITS = NB * 4
VA_N = NB * NL * NH * (DK + 1)
ST_LAG, PV_LAG = 9, 10
NT_LAG, L_LAG = 5, 6
OC_LAG, T_LAG, REC_LAG, ON_LAG, OT_LAG, Y_LAG, X_LAG, STAT_LAG = 13, 15, 15, 16, 18, 19, 20, 21
STEPS = 4 * (NB - 1) + STAT_LAG + 1
T_STEP = {c: 4 * BC * c - 15 for c in range(2, NC)}
Q_STEP = {c: 4 * BC * c - 11 for c in range(2, NC)}


def chunk_at(steps, n):
    return next((c for c, at in steps.items() if at == n), None)


def due(n, lag):
    b, off = divmod(n - lag, 4)
    return b if off == 0 and 0 <= b < NB else None


def live(lo, v, hi):
    return lo <= v < hi if isinstance(v, int) else True


def earlier(L):
    return UNITS * L, NB * L, NC * L


class SelfOrder:

    def __init__(self, engine, sem):
        self.engine, self.sem, self.n, self.base = engine, sem, 0, 0

    def __call__(self, ins):
        self.n += 1
        ins.then_inc(self.sem, 1)
        self.engine.wait_ge(self.sem, self.base + self.n)

    def loop(self, i, per):
        self.base, self.start = i * per, self.n
        self.per = per

    def end(self, trips):
        assert self.n - self.start == self.per, (self.n - self.start, self.per)
        self.base, self.n = 0, self.start + trips * self.per


def flamingo(nc, a, out):
    with ExitStack() as ctx:
        def sb(name, shape, dt=F32):
            return ctx.enter_context(nc.sbuf_tensor(name, shape, dt))

        def sem(name):
            return ctx.enter_context(nc.semaphore(name))

        def sems(name, n=NL):
            return [sem(f"{name}{i}") for i in range(n)]

        bank = [ctx.enter_context(nc.psum_tensor(f"bank{i}", [P, CT], F32)) for i in range(8)]

        X = sb("X", [P, NB, P])
        XN = sb("XN", [P, NB, P])
        XT = sb("XT", [P, 2, NB, P], F16)
        XTH, XTL = XT[:, 0], XT[:, 1]
        XT32 = XT[:].rearrange("p s b t -> p (s b t)").bitcast(F32)
        CTH = sb("CTH", [P, NB, P], F16)
        CTL = sb("CTL", [P, NB, P], F16)
        WAH = sb("WAH", [P, 12, P], F16)
        WAL = sb("WAL", [P, 12, P], F16)
        WO = sb("WO", [P, NL, P])
        VAF = sb("VAF", [P, VA_N + 32])
        VA = VAF[:, 0:VA_N].rearrange("p (b h d) -> p b h d", b=NB, h=NL * NH)
        STK = sb("STK", [P, 2, 4, CT], F16)
        PR = sb("PR", [P, 4, CT])
        ROWS = sb("ROWS", [P, R_N])
        COLS = sb("COLS", [P, C_N])
        DB = sb("DB", [NE, P])
        PJ = sb("PJ", [P, 2, CT])
        PJH = sb("PJH", [P, 2, CT], F16)
        PJL = sb("PJL", [P, 2, CT], F16)
        FC1 = sb("FC1", [P, CT], F16)
        FC2 = sb("FC2", [P, NI, P])
        WL2T = sb("WL2T", [P, 9, P])
        ID = sb("ID", [P, P])
        IDH = sb("IDH", [P, P], F16)
        IDB = sb("IDB", [P, P], F16)
        MV = sb("MV", [P, NB, 2])
        ST6 = sb("ST6", [P, NB, 6])
        RSTD = sb("RSTD", [P, NB])
        NM = sb("NM", [P, 2, NH])
        NHL = sb("NHL", [NH, 2, 2, P], F16)
        REC = sb("REC", [P, 2, NH])
        OC = sb("OC", [P, 2, CT])
        ON = sb("ON", [P, 2, P])
        OT = sb("OT", [P, 2, P])
        AM = sb("AM", [P, A_N])
        AMR = sb("AMR", [P, A_N])
        SC = sb("SC", [P, A_N])
        DS = sb("DS", [P, A_N])
        SMALL = sb("SMALL", [P, 320])
        GWH = sb("GWH", [P, 8], F16)
        GWL = sb("GWL", [P, 8], F16)
        LG = sb("LG", [P, NB, 8])
        SIG = sb("SIG", [P, NB, 8])
        W9 = sb("W9", [P, NB, NE])
        WF = sb("WF", [P, NB, NE])
        DK_ = sb("DK_", [P, 8])
        HS = sb("HS", [P, 2, NE])
        EXPERTS = sb("EXPERTS", [P, NE, NI + 1])
        EXPERT = sb("EXPERT", [P, 2, NI + 1])
        TG = sb("TG", [P, 8])
        SCAL = sb("SCAL", [P, 32])
        RT = sb("RT", [P, P])
        MV2 = sb("MV2", [P, NB, 2])
        MKH = sb("MKH", [NB, 2, P], F16)
        MK8W = sb("MK8", [NB, P // 4], I32)
        MK8 = MK8W[:].bitcast(U8)
        MKI = sb("MKI", [NB, P], I32)
        REGION = sb("REGION", [P, 19456])

        def region(at, n, dt=F32):
            v = REGION[:, at:at + n]
            return v if dt == F32 else v.bitcast(dt)

        UPH = region(0, 2304, F16).rearrange("p (e i) -> p e i", e=NE)
        UPL = region(2304, 2304, F16).rearrange("p (e i) -> p e i", e=NE)
        DNH = region(4608, 2304, F16).rearrange("p (e i) -> p e i", e=NE)
        DNL = region(6912, 2304, F16).rearrange("p (e i) -> p e i", e=NE)
        G = region(9216, 4096).rearrange("p (s i t) -> p s i t", s=2, i=NI)
        GH = region(13312, 2048, F16).rearrange("p (s i t) -> p s i t", s=2, i=NI)
        GL = region(15360, 2048, F16).rearrange("p (s i t) -> p s i t", s=2, i=NI)
        ACC = region(17408, 2048).rearrange("p (b h) -> p b h", b=NB)
        W9T = region(9216, 1024)
        UPRAW = region(9216, 4608).rearrange("p (e i) -> p e i", e=NE)
        DNRAW = region(13824, 4608).rearrange("p (e i) -> p e i", e=NE)
        FC1I = region(0, 512, I32)
        FC2I = region(512, 512, I32)
        MRAW = region(1024, 2048, I32).rearrange("p (b k) -> p b k", b=NB)
        XN2 = region(4096, 2048).rearrange("p (b h) -> p b h", b=NB)
        H32 = region(3072, 1024).rearrange("p (s t) -> p s t", s=2)
        MB = region(18432, 1024, F16).rearrange("p (b k) -> p b k", b=NB)
        GT = region(0, 6144).rearrange("p (o t) -> p o t", o=3)
        UT = region(6144, 6144).rearrange("p (o t) -> p o t", o=3)
        TT = region(12288, 6144).rearrange("p (o t) -> p o t", o=3)
        RQ = region(128, 128)
        RQH = region(256, 64, F16)
        RQT = region(320, 64, F16)
        RSG = region(384, 128)
        XQH = region(1024, 1024, F16).rearrange("p (b h) -> p b h", b=NB)
        XQT = region(2048, 1024, F16).rearrange("p (b h) -> p b h", b=NB)
        WRAW = PR[:].rearrange("p s t -> p (s t)")[:, 0:12 * P].rearrange("p (m o) -> p m o", m=12)
        CRAW = VAF[:, 0:NB * P]
        L2RAW = STK[:].rearrange("p a s t -> p (a s t)").bitcast(F32)[:, 0:9 * P]
        L2Q = PR[:].rearrange("p s t -> p (s t)")[:, 0:9 * P]

        kscr = nc.dram_tensor("kscr", (NL * NC, P, NG * CT), F16, kind="Internal").ap()
        qscr = nc.dram_tensor("qscr", (NC, P, NG * CT), F16, kind="Internal").ap()
        mscr = nc.dram_tensor("mscr", (2, NC, CT), F16, kind="Internal").ap()

        ld_w, ld_ctx, ld_x, ld_small, ld_wo, ld_moe, ld_l2 = (
            sem(n) for n in ("ld_w", "ld_ctx", "ld_x", "ld_small", "ld_wo", "ld_moe", "ld_l2"))
        ld_mask, ld_fc, ld_rhs = sem("ld_mask"), sem("ld_fc"), sem("ld_rhs")
        scr_init, mask_put, mask_rows = sem("scr_init"), sem("mask_put"), sem("mask_rows")
        ident = sem("ident")
        am_local, am_all, scales = sem("am_local"), sem("am_all"), sem("scales")
        tanh_done = sem("tanh_done")
        ctx_hi, ctx_lo, w_hi, w_lo = sem("ctx_hi"), sem("ctx_lo"), sem("w_hi"), sem("w_lo")
        moe_hi, moe_lo = sem("moe_hi"), sem("moe_lo")
        mask_ready = sem("mask_ready")
        l2_deq, l2_tr, l2_cp = sem("l2_deq"), sem("l2_tr"), sem("l2_cp")
        kp_mm, kp_sum, kp_lo = sem("kp_mm"), sem("kp_sum"), sem("kp_lo")
        kp_put = sems("kp_put", 2)
        v_mm, v_out, v_ones = sem("v_mm"), sem("v_out"), sem("v_ones")
        xn_ready, xt_mm, xt_hi, xt_lo = (sems(n, 9) for n in ("xn_ready", "xt_mm", "xt_hi", "xt_lo"))
        q_mm, q_sum, q_lo, q_put = sem("q_mm"), sem("q_sum"), sem("q_lo"), sem("q_put")
        stack_in, max_in = sems("stack_in", 4), sems("max_in", 2)
        s_done, max_done, nt_done, nm_hi, nm_lo = (
            sem(n) for n in ("s_done", "max_done", "nt_done", "nm_hi", "nm_lo"))
        st_done, exp_done, pv_done = sem("st_done"), sem("exp_done"), sem("pv_done")
        oc_cp, t_mm, rec_done, on_done, ot_done, ot_cp = (
            sem(n) for n in ("oc_cp", "t_mm", "rec_done", "on_done", "ot_done", "ot_cp"))
        y_done, x_done, xb_done, st6_done, mv_done = (
            sem(n) for n in ("y_done", "x_done", "xb_done", "st6_done", "mv_done"))
        gl_mm, sig_done, w9_ready, w9t_mm, w9t_cp, bias_mm, acc_init = (
            sem(n) for n in ("gl_mm", "sig_done", "w9_ready", "w9t_mm", "w9t_cp", "bias_mm", "acc_init"))
        lg_ready, gh_done, l2_norm = sem("lg_ready"), sem("gh_done"), sem("l2_norm")
        up_mm, gelu_done, split_done, dn_mm, comb_done = (
            sem(n) for n in ("up_mm", "gelu_done", "split_done", "dn_mm", "comb_done"))
        moe_done = sem("moe_done")
        fc_ready, h_sum, f1_mm, silu_done, f2_mm, f2_out = (
            sem(n) for n in ("fc_ready", "h_sum", "f1_mm", "silu_done", "f2_mm", "f2_out"))
        gm_part, gm_all = sem("gm_part"), sem("gm_all")
        gu_mm, gu_cp, gq_done, gate_r, sig2, o_q, d_mm, d_out = (
            sem(n) for n in ("gu_mm", "gu_cp", "gq_done", "gate_r", "sig2", "o_q", "d_mm", "d_out"))
        r_q, r_mm, r_cp, z_mm, z_out, stored = (
            sem(n) for n in ("r_q", "r_mm", "r_cp", "z_mm", "z_out", "stored"))
        expert_cp = sem("expert_cp")
        dve_self, pool_self = sem("dve_self"), sem("pool_self")

        block = ctx.enter_context(nc.Block())

        @block.sync
        def _(sp):
            sp.dma_start(WRAW, a["watt"]).then_inc(ld_w, 16)
            sp.dma_start(CRAW, a["ctx_t"]).then_inc(ld_ctx, 16)
            sp.dma_start(COLS[:], a["cols"]).then_inc(ld_small, 16)
            sp.dma_start(ROWS[:], a["rows"].partition_broadcast(P)).then_inc(ld_small, 16)
            sp.dma_start(DB[:], a["down_b"]).then_inc(ld_small, 16)
            sp.dma_start(X[:], a["x"]).then_inc(ld_x, 16)
            sp.dma_start(UPRAW, a["up_w"]).then_inc(ld_moe, 16)
            sp.dma_start(DNRAW, a["down_w"]).then_inc(ld_moe, 16)
            sp.dma_start(L2RAW, a["w_l2"]).then_inc(ld_l2, 16)
            sp.dma_start(RT[:], a["rhs_t"]).then_inc(ld_rhs, 16)
            sp.dma_start(WO[:], a["wo"]).then_inc(ld_wo, 16)

            def put_parts(scr, chunk, slot, parts, done):
                dst = scr[chunk].rearrange("(m r) (g t) -> r m g t", r=4, g=NG)
                for row, part in enumerate(parts):
                    sp.dma_start(dst[row], part[:, slot, :]).then_inc(done, 16)

            sp.wait_ge(scr_init, 32)
            def put_keys(c):
                for L in range(NL):
                    sp.wait_ge(kp_lo, 4 * c + (L + 1))
                    put_parts(kscr, c + L * NC, L % 2, (PJH, PJL, PJH), kp_put[L % 2])

            with sp.Fori(0, NC) as c:
                put_keys(c)

            def put_queries(L, c):
                units0, batches0, chunks0 = earlier(L)
                sp.wait_ge(q_lo, chunks0 + c + 1)
                put_parts(qscr, c, c % 2, (PJH, PJH, PJL), q_put)

            def load(L, b):
                c, i = divmod(b, BC)
                cols = slice(P * i, P * (i + 1))
                for side, src in enumerate((kscr[L * NC + c], qscr[c])):
                    sp.dma_start(STK[:, side, i, :].rearrange("p (g t) -> p g t", g=NG),
                                 src.rearrange("p (g t) -> p g t", g=NG)[:, :, cols]).then_inc(stack_in[i], 16)

            def put_max(L, b):
                sp.wait_ge(nm_lo, NB * L + b + 1)
                for part in range(2):
                    dst = STK[MAX_ROW + 4 * part:P:32, 1, b % 4, :].rearrange("p (g t) -> p g t", g=NG)
                    sp.dma_start(dst, NHL[:, b % 2, part, :]).then_inc(max_in[b % 2], 16)

            for L in range(NL):
                units0, batches0, chunks0 = earlier(L)
                if L == 0:
                    sp.wait_ge(kp_put[0], 48 * NC * 2)
                    sp.wait_ge(kp_put[1], 48 * NC * 2)
                if L == 1:
                    sp.wait_ge(mask_rows, 16 * 2 * NC)
                for c in range(2):
                    put_queries(L, c)
                    sp.wait_ge(q_put, 48 * (chunks0 + c + 1))
                    if c == 0:
                        for b in range(BC):
                            load(L, b)
                for b in range(NB):
                    c = (b + 3) // BC
                    if b % BC == 1 and 2 <= c < NC:
                        put_queries(L, c)
                    put_max(L, b)
                    if 1 <= b <= NB - BC:
                        if (b + 3) % BC == 0:
                            sp.wait_ge(q_put, 48 * (chunks0 + c + 1))
                        sp.wait_ge(st_done, units0 + 4 * b)
                        load(L, b + 3)

            for c in range(NC):
                sp.wait_ge(z_out, BC * (c + 1))
                sp.dma_start(out[BC * c:BC * (c + 1)].rearrange("b t d -> t b d"),
                             X[:, BC * c:BC * (c + 1), :]).then_inc(stored, 16)
            sp.wait_ge(stored, 16 * NC)

        @block.gpsimd
        def _(pool):
            order = SelfOrder(pool, pool_self)
            for scr, name, n in ((qscr, "q_const", 4 * NC), (kscr, "k_const", 4 * NL * NC)):
                dst = scr.rearrange("c (j i r) t -> r (c j) i t", j=4, r=4)[3]
                pool.dma_start(dst, a[name].rearrange("(o r) t -> o r t", o=1).to_broadcast((n, DK, NG * CT))
                               ).then_inc(scr_init, 16)
            pool.dma_start(MKI[:], a["mask1"]).then_inc(ld_mask, 16)
            pool.dma_start(MK8W[:], a["mask3"]).then_inc(ld_mask, 16)
            order(pool.memset(ID[:], 0.0))
            order(pool.affine_select(out=ID[:], in_=ID[:], compare_op=ALU.not_equal, fill=1.0, base=0,
                                     pattern=[[-1, P]], channel_multiplier=1))
            pool.tensor_copy(IDH[:], ID[:]).then_inc(ident, 1)
            pool.tensor_scalar(IDB[:], ID[:], BIG, 1.0, ALU.mult, ALU.mult).then_inc(ident, 1)
            pool.wait_ge(am_local, 1)
            pool.partition_all_reduce(AMR[:, 0:A_UP], AM[:, 0:A_UP], P, ABSMAX).then_inc(am_all, 1)
            pool.wait_ge(ctx_lo, NC)
            order(pool.memset(VAF[:, VA_N:], 0.0))
            pool.memset(VA[:, :, :, DK:DK + 1], 1.0).then_inc(v_ones, 1)
            pool.wait_ge(am_local, 2)
            pool.partition_all_reduce(AMR[:, A_UP:], AM[:, A_UP:], P, ABSMAX).then_inc(am_all, 1)
            pool.wait_ge(mask_ready, 2)
            pool.wait_ge(scr_init, 32)
            pool.dma_start(mscr.rearrange("i c (b t) -> (c b) i t", b=BC), MKH[:]).then_inc(mask_put, 16)
            pool.wait_ge(mask_put, 16)
            for i, L in enumerate((1, 3)):
                for c in range(NC):
                    dst = kscr[L * NC + c].rearrange("(j r) (g t) -> r j g t", r=32, g=NG)[MASK_ROW]
                    src = mscr[i:i + 1, c:c + 1, :].to_broadcast((4, NG, CT))
                    pool.dma_start(dst, src).then_inc(mask_rows, 16)

            def residual_bias(L):
                gbo = SMALL[:, 192:320]
                order(pool.tensor_scalar(gbo, ROWS[:, R_BO + P * L:R_BO + P * (L + 1)], TG[:, L:L + 1], 1.0,
                                         ALU.mult, ALU.mult))
                for c in range(NC):
                    pool.wait_ge(xn_ready[2 * L], BC * (c + 1))
                    xc = X[:, BC * c:BC * (c + 1), :]
                    pool.tensor_tensor(xc, xc, gbo.rearrange("p (o d) -> p o d", o=1).to_broadcast((P, BC, P)), ALU.add
                                       ).then_inc(xb_done, 1)

            pool.wait_ge(tanh_done, 1)
            residual_bias(0)
            pool.wait_ge(moe_done, 1)
            pool.dma_start(FC1I, a["fc1_q"]).then_inc(ld_fc, 16)
            pool.dma_start(FC2I, a["fc2_q"]).then_inc(ld_fc, 16)
            pool.dma_start(MRAW, a["mask2"]).then_inc(ld_fc, 16)
            residual_bias(1)
            pool.wait_ge(ld_fc, 48)
            pool.tensor_scalar(FC1[:], FC1I, -128.0, None, ALU.add).then_inc(fc_ready, 1)
            order(pool.tensor_scalar(FC2[:].rearrange("p i o -> p (i o)"), FC2I, -128.0, None, ALU.add))
            order(pool.tensor_tensor(FC2[:].rearrange("p i o -> p (i o)"), FC2[:].rearrange("p i o -> p (i o)"),
                                     ROWS[:, R_S2:R_S2 + CT], ALU.mult))
            order(pool.tensor_scalar(MB, MRAW, 0.0, -BIG, ALU.is_equal, ALU.mult))
            pool.memset(SCAL[:, 31:32], 0.0).then_inc(fc_ready, 1)
            for i in range(5):
                pool.wait_ge(gm_part, i + 1)
                pool.partition_all_reduce(SCAL[:, 8 + i:9 + i], SCAL[:, i:i + 1], P, ABSMAX).then_inc(gm_all, 1)

        @block.tensor
        def _(pe):
            def product3(dst, wh, wl, xh, xl, start=True, stop=True):
                pe.matmul(dst, wh, xh, start=start, stop=False)
                pe.matmul(dst, wh, xl, start=False, stop=False)
                return pe.matmul(dst, wl, xh, start=False, stop=stop)

            def norm_transposes(i, src, stage=6):
                for c in range(NC):
                    pe.wait_ge(xn_ready[i], BC * (c + 1))
                    if c >= 2:
                        pe.wait_ge(xt_lo[i], c - 1)
                    for b in range(BC):
                        mm = pe.transpose(bank[stage + c % 2][:, P * b:P * (b + 1)], src[:, BC * c + b, :], ID[:])
                    mm.then_inc(xt_mm[i], 1)

            pe.wait_ge(ident, 2)
            pe.wait_ge(l2_deq, 1)
            for m in range(9):
                if m >= 8:
                    pe.wait_ge(l2_cp, 1)
                mm = pe.transpose(bank[6 + m // 4 % 2][:, P * (m % 4):P * (m % 4 + 1)],
                                  L2Q[:, P * m:P * (m + 1)], ID[:])
                if m % 4 == 3 or m == 8:
                    mm.then_inc(l2_tr, 1)

            pe.wait_ge(w_lo, 9)
            pe.wait_ge(ctx_lo, NC)
            def keys(c):
                for L in range(NL):
                    if live(0, 4 * c + (L - 2), 99):
                        pe.wait_ge(kp_sum, 4 * c + (L - 1))
                    product3(bank[L % 2][:], WAH[:, 4 + L, :], WAL[:, 4 + L, :],
                             CTH[:, bass.ds(c * BC, BC), :], CTL[:, bass.ds(c * BC, BC), :]).then_inc(kp_mm, 1)

            keys(0)
            with pe.Fori(1, NC) as c:
                keys(c)

            def some_values(it):
                for u in range(2):
                    if live(1, it, 99):
                        pe.wait_ge(v_out, 2 * it + (u - 1))
                    b = 2 * it + u
                    product3(bank[2 + u][:], CTH[:, b, :], CTL[:, b, :], WAH[:, 8:12, :], WAL[:, 8:12, :]
                             ).then_inc(v_mm, 1)

            some_values(0)
            with pe.Fori(1, NB // 2) as it:
                some_values(it)

            def attention(L):
                units0, batches0, chunks0 = earlier(L)
                def transposes(c, to):
                    pe.wait_ge(xn_ready[2 * L], BC * (c + 1))
                    for i in range(BC):
                        mm = pe.transpose(to[:, P * i:P * (i + 1)], XN[:, BC * c + i, :], ID[:])
                    mm.then_inc(xt_mm[2 * L], 1)

                def queries(c, to):
                    pe.wait_ge(xt_lo[2 * L], c + 1)
                    product3(to[:], WAH[:, L, :], WAL[:, L, :],
                             XTH[:, BC * c:BC * (c + 1), :], XTL[:, BC * c:BC * (c + 1), :]).then_inc(q_mm, 1)

                for c in range(2):
                    transposes(c, bank[6 + c])
                for c in range(2):
                    queries(c, bank[4 + c])
                pe.wait_ge(q_sum, chunks0 + 2)

                def scores(n):
                    b, j = divmod(n, 4)
                    slot = b % 4
                    dst = bank[n % 2]
                    if j == 0:
                        pe.wait_ge(stack_in[slot], 8 * batches0 + 32 * (b // 4 + 1))
                    if n >= 2:
                        pe.wait_ge(max_done, units0 + n - 1)
                    rows = slice(32 * j, 32 * (j + 1))
                    for g in range(NG):
                        cols = slice(P * g, P * (g + 1))
                        if L == 2:
                            pe.matmul(dst[:, cols], IDB[:], MB[:, b, :], start=True, stop=False)
                        mm = pe.matmul(dst[:, cols], STK[rows, 1, slot, cols], STK[rows, 0, slot, cols],
                                       start=L != 2, stop=True)
                    mm.then_inc(s_done, 1)

                def shifted(n):
                    b, j = divmod(n, 4)
                    slot = b % 4
                    dst = bank[2 + n % 2]
                    if j == 0:
                        pe.wait_ge(max_in[b % 2], 16 * batches0 + 32 * (b // 2 + 1))
                    if n >= 2:
                        pe.wait_ge(exp_done, units0 + n - 1)
                    rows = slice(32 * j, 32 * (j + 1))
                    for g in range(NG):
                        cols = slice(P * g, P * (g + 1))
                        if L == 2:
                            pe.matmul(dst[:, cols], MB[:, b, :], IDB[:], start=True, stop=False)
                        mm = pe.matmul(dst[:, cols], STK[rows, 0, slot, cols], STK[rows, 1, slot, cols],
                                       start=L != 2, stop=True)
                    mm.then_inc(st_done, 1)

                def values(n):
                    b, j = divmod(n, 4)
                    pe.wait_ge(exp_done, units0 + n + 1)
                    if j == 0 and b >= 2:
                        pe.wait_ge(oc_cp, batches0 + b - 1)
                    for g in range(NG):
                        at = ((b * NL + L) * NH + NG * g + j) * (DK + 1)
                        mm = pe.matmul(bank[4 + b % 2][32 * g:32 * (g + 1), P * j:P * (j + 1)],
                                       VAF[:, at:at + 32], PR[:, j, P * g:P * (g + 1)], start=True, stop=True)
                    mm.then_inc(pv_done, 1)

                for n in range(STEPS):
                    if n < UNITS:
                        scores(n)
                    if 0 <= n - ST_LAG < UNITS:
                        shifted(n - ST_LAG)
                    if 0 <= n - PV_LAG < UNITS:
                        values(n - PV_LAG)
                    b = due(n, T_LAG)
                    if b is not None:
                        pe.wait_ge(oc_cp, batches0 + b + 1)
                        if b >= 1:
                            pe.wait_ge(on_done, batches0 + b)
                        c = chunk_at(T_STEP, n - 2)
                        if c is not None:
                            pe.wait_ge(xt_lo[2 * L], c + 1)
                        c = chunk_at(Q_STEP, n - 2)
                        if c is not None:
                            pe.wait_ge(q_sum, chunks0 + c + 1)
                        for j in range(4):
                            mm = pe.transpose(bank[6][:, P * j:P * (j + 1)], OC[:, b % 2, P * j:P * (j + 1)], ID[:])
                        mm.then_inc(t_mm, 1)
                    b = due(n, NT_LAG)
                    if b is not None:
                        pe.wait_ge(max_done, units0 + b * 4 + 4)
                        if b >= 4:
                            pe.wait_ge(x_done, batches0 + b - 3)
                        pe.transpose(bank[7][0:NH, 0:P], NM[:, b % 2, :], ID[:]).then_inc(nt_done, 1)
                    b = due(n, OT_LAG)
                    if b is not None:
                        pe.wait_ge(on_done, batches0 + b + 1)
                        pe.wait_ge(nm_lo, batches0 + min(b + 4, NB))
                        if b >= 1:
                            pe.wait_ge(x_done, batches0 + b)
                        pe.transpose(bank[7][:, P:2 * P], ON[:, b % 2, :], ID[:]).then_inc(ot_done, 1)
                    c = chunk_at(T_STEP, n)
                    if c is not None:
                        pe.wait_ge(on_done, batches0 + (n - T_LAG) // 4 + 1)
                        transposes(c, bank[6])
                    c = chunk_at(Q_STEP, n)
                    if c is not None:
                        pe.wait_ge(on_done, batches0 + (n - T_LAG) // 4 + 1)
                        queries(c, bank[6])
                    b = due(n, Y_LAG)
                    if b is not None:
                        pe.wait_ge(ot_cp, batches0 + b + 1)
                        pe.matmul(bank[7][:, 2 * P:3 * P], OT[:, b % 2, :], WO[:, L, :], start=True, stop=True
                                  ).then_inc(y_done, 1)

            def experts():
                norm_transposes(1, XN)
                pe.wait_ge(moe_lo, 2 * NE + 1)
                pe.wait_ge(xt_lo[1], NC)
                for b in range(NB):
                    mm = product3(bank[0][:, 8 * b:8 * b + 8], XTH[:, b, :], XTL[:, b, :], GWH[:], GWL[:])
                mm.then_inc(gl_mm, 1)
                pe.wait_ge(w9_ready, 1)
                for c in range(NC):
                    if c >= 2:
                        pe.wait_ge(w9t_cp, c - 1)
                    for b in range(BC):
                        mm = pe.transpose(bank[6 + c % 2][0:NE, P * b:P * (b + 1)], W9[:, BC * c + b, :], ID[:])
                    mm.then_inc(w9t_mm, 1)
                    pe.wait_ge(w9t_cp, c + 1)
                    if c >= 2:
                        pe.wait_ge(acc_init, c - 1)
                    for b in range(BC):
                        mm = pe.matmul(bank[4 + c % 2][:, P * b:P * (b + 1)],
                                       W9T[0:NE, CT * (c % 2) + P * b:CT * (c % 2) + P * (b + 1)], DB[:],
                                       start=True, stop=True)
                    mm.then_inc(bias_mm, 1)

                def up(e, n, c):
                    for i in range(NI):
                        if live(1, n, 99):
                            pe.wait_ge(gelu_done, n * 4 + (i - 3))
                        w = slice(P * i, P * (i + 1))
                        product3(bank[i][:], UPH[:, e, w], UPL[:, e, w],
                                 XTH[:, BC * c:BC * (c + 1), :], XTL[:, BC * c:BC * (c + 1), :]).then_inc(up_mm, 1)

                def down(e, n, c):
                    pe.wait_ge(split_done, n * 4 + 4)
                    pe.wait_ge(acc_init, NC)
                    if live(2, n, 99):
                        pe.wait_ge(comb_done, n - 1)
                    s = c % 2
                    for t in range(BC):
                        tok = slice(P * t, P * (t + 1))
                        for i in range(NI):
                            w = slice(P * i, P * (i + 1))
                            mm = product3(bank[4 + s][:, tok], GH[:, s, i, tok], GL[:, s, i, tok],
                                          DNH[:, e, w], DNL[:, e, w], start=i == 0, stop=i == NI - 1)
                    mm.then_inc(dn_mm, 1)

                def turn(e, n0, last):
                    for c in range(NC):
                        if c < NC - 1:
                            up(e, n0 + (c + 1), c + 1)
                        elif not last:
                            up(e + 1, n0 + NC, 0)
                        down(e, n0 + c, c)

                up(0, 0, 0)
                turn(0, 0, False)
                with pe.Fori(1, NE - 1) as e:
                    turn(e, e * 4, False)
                turn(NE - 1, 4 * (NE - 1), True)

            def quantised_mlp():
                norm_transposes(8, XN2)
                pe.wait_ge(fc_ready, 2)
                for c in range(NC):
                    pe.wait_ge(xt_lo[8], c + 1)
                    for i in range(NI):
                        if c >= 1:
                            pe.wait_ge(silu_done, 4 * (c - 1) + i + 1)
                        w = FC1[:, P * i:P * (i + 1)]
                        pe.matmul(bank[i][:], w, XTH[:, BC * c:BC * (c + 1), :], start=True, stop=False)
                        pe.matmul(bank[i][:], w, XTL[:, BC * c:BC * (c + 1), :], start=False, stop=True
                                  ).then_inc(f1_mm, 1)
                    if c >= 1:
                        second(c - 1)
                second(NC - 1)

            def second(c):
                pe.wait_ge(silu_done, 4 * (c + 1))
                if c >= 2:
                    pe.wait_ge(f2_out, 4 * (c - 1))
                for t in range(BC):
                    for i in range(NI):
                        mm = pe.matmul(bank[4 + c % 2][:, P * t:P * (t + 1)], G[:, c % 2, i, P * t:P * (t + 1)],
                                       FC2[:, i, :], start=i == 0, stop=i == NI - 1)
                mm.then_inc(f2_mm, 1)

            def fixed_point_mlp():
                norm_transposes(5, XN)
                n = 0
                for m in range(6):
                    for c in range(NC):
                        pe.wait_ge(xt_lo[5], c + 1)
                        if n >= 4:
                            pe.wait_ge(gu_cp, n - 3)
                        pe.matmul(bank[n % 4][:], WL2T[:, m, :], XT32[:, CT * c:CT * (c + 1)], start=True, stop=True
                                  ).then_inc(gu_mm, 1)
                        n += 1
                pe.wait_ge(o_q, 1)
                for b in range(NB):
                    if b >= 2:
                        pe.wait_ge(d_out, b - 1)
                    for i in range(3):
                        mm = pe.matmul(bank[4 + b % 2][:, 0:P], GT[:, i, P * b:P * (b + 1)], WL2T[:, 6 + i, :],
                                       start=i == 0, stop=i == 2)
                    mm.then_inc(d_mm, 1)

            def int8_product():
                pe.wait_ge(r_q, 1)
                pe.transpose(bank[0][:].bitcast(F16)[:, 0:P], RQH, IDH[:]).then_inc(r_mm, 1)
                pe.matmul(bank[1][:, 0:P], SCAL[:, 20:21].to_broadcast((P, P)), ID[:], start=True, stop=True
                          ).then_inc(r_mm, 1)
                for c in range(NC):
                    pe.wait_ge(xn_ready[7], NB + c + 1)
                    if c >= 2:
                        pe.wait_ge(xt_hi[7], c - 1)
                    for b in range(BC):
                        mm = pe.transpose(bank[6 + c % 2][:].bitcast(F16)[:, P * b:P * (b + 1)], XQH[:, BC * c + b, :], IDH[:])
                    mm.then_inc(xt_mm[7], 1)
                pe.wait_ge(r_cp, 2)
                for b in range(NB):
                    pe.wait_ge(xt_hi[7], b // BC + 1)
                    if b >= 2:
                        pe.wait_ge(z_out, b - 1)
                    pe.matmul(bank[4 + b % 2][:, 0:P], XQT[:, b, :], RQT, start=True, stop=True).then_inc(z_mm, 1)

            attention(0)
            experts()
            attention(1)
            quantised_mlp()
            attention(2)
            fixed_point_mlp()
            attention(3)
            int8_product()

        @block.scalar
        def _(act):
            act.wait_ge(scales, 1)
            for c in range(NC):
                act.activation(CTH[:, BC * c:BC * (c + 1), :].rearrange("p b t -> p (b t)"), CRAW[:, CT * c:CT * (c + 1)],
                               ACT.Identity, scale=SC[:, A_CTX:A_CTX + 1]).then_inc(ctx_hi, 1)
            for m in range(9):
                mats = slice(m, m + 1) if m < 8 else slice(8, 12)
                act.activation(WAH[:, mats, :], WRAW[:, mats, :], ACT.Identity, scale=SC[:, m:m + 1]).then_inc(w_hi, 1)
            act.wait_ge(ld_small, 48)
            act.activation(TG[:], ROWS[:, R_GATES:R_GATES + 8], ACT.Tanh).then_inc(tanh_done, 1)
            for i in range(3):
                act.wait_ge(l2_tr, i + 1)
                m = 4 * i
                n = 4 if i < 2 else 1
                act.copy(WL2T[:, m:m + n, :].rearrange("p m o -> p (m o)"), bank[6 + i % 2][:, 0:P * n]).then_inc(l2_cp, 1)
            def key_sums(c):
                for L in range(NL):
                    act.wait_ge(kp_mm, 4 * c + (L + 1))
                    if live(0, 4 * c + (L - 2), 99):
                        act.wait_ge(kp_lo, 4 * c + (L - 1))
                    act.activation(PJ[:, L % 2, :], bank[L % 2][:], ACT.Identity, bias=COLS[:, C_BK + L:C_BK + L + 1],
                                   scale=DK_[:, L:L + 1]).then_inc(kp_sum, 1)

            key_sums(0)
            with act.Fori(1, NC) as c:
                key_sums(c)

            act.wait_ge(scales, 2)
            act.activation(GWH[:], COLS[:, C_GW:C_GW + 8], ACT.Identity, scale=SC[:, A_GW:A_GW + 1]).then_inc(moe_hi, 1)
            for e in range(NE):
                act.activation(UPH[:, e, :], UPRAW[:, e, :], ACT.Identity, scale=SC[:, A_UP + e:A_UP + e + 1]
                               ).then_inc(moe_hi, 1)
                act.activation(DNH[:, e, :], DNRAW[:, e, :], ACT.Identity, scale=SC[:, A_DN + e:A_DN + e + 1]
                               ).then_inc(moe_hi, 1)

            def norm_hi(i):
                for c in range(NC):
                    act.wait_ge(xt_mm[i], c + 1)
                    act.copy(XTH[:, BC * c:BC * (c + 1), :].rearrange("p b t -> p (b t)"), bank[6 + c % 2][:]
                             ).then_inc(xt_hi[i], 1)

            def attention(L):
                units0, batches0, chunks0 = earlier(L)
                def hi_part(c, of):
                    act.wait_ge(xt_mm[2 * L], c + 1)
                    act.copy(XTH[:, BC * c:BC * (c + 1), :].rearrange("p b t -> p (b t)"), of[:]).then_inc(xt_hi[2 * L], 1)

                def query_sums(c, of):
                    act.wait_ge(q_mm, chunks0 + c + 1)
                    if chunks0 + c >= 2:
                        act.wait_ge(q_lo, chunks0 + c - 1)
                        act.wait_ge(q_put, 48 * (chunks0 + c - 1))
                    for dst in (PJH, PJ):
                        ins = act.activation(dst[:, c % 2, :], of[:], ACT.Identity, bias=COLS[:, C_BQ + L:C_BQ + L + 1],
                                             scale=DS[:, A_Q + L:A_Q + L + 1])
                    ins.then_inc(q_sum, 1)

                for c in range(2):
                    hi_part(c, bank[6 + c])
                for c in range(2):
                    query_sums(c, bank[4 + c])

                for n in range(STEPS):
                    b = due(n, L_LAG)
                    if b is not None:
                        act.wait_ge(nt_done, batches0 + b + 1)
                        if b >= 2:
                            act.wait_ge(max_in[b % 2], 16 * batches0 + 32 * (b // 2))
                        act.activation(NHL[:, b % 2, 0, :], bank[7][0:NH, 0:P], ACT.Copy, scale=1.0 / BIG
                                       ).then_inc(nm_hi, 1)
                    b = due(n, OT_LAG + 1)
                    if b is not None:
                        act.wait_ge(ot_done, batches0 + b + 1)
                        if b >= 2:
                            act.wait_ge(y_done, batches0 + b - 1)
                        act.copy(OT[:, b % 2, :], bank[7][:, P:2 * P]).then_inc(ot_cp, 1)
                    c = chunk_at(T_STEP, n - 1)
                    if c is not None:
                        hi_part(c, bank[6])
                    c = chunk_at(Q_STEP, n - 1)
                    if c is not None:
                        query_sums(c, bank[6])
                    m = n - ST_LAG
                    if 0 <= m < UNITS:
                        act.wait_ge(st_done, units0 + m + 1)
                        if m >= 4:
                            act.wait_ge(pv_done, units0 + m - 3)
                        act.activation(PR[:, m % 4, :], bank[2 + m % 2][:], ACT.Exp, scale=float(DK) ** -0.5
                                       ).then_inc(exp_done, 1)
                    b = due(n, OC_LAG)
                    if b is not None:
                        act.wait_ge(pv_done, units0 + b * 4 + 4)
                        if b >= 2:
                            act.wait_ge(t_mm, batches0 + b - 1)
                        act.copy(OC[:, b % 2, :], bank[4 + b % 2][:]).then_inc(oc_cp, 1)

            def experts():
                norm_hi(1)
                act.wait_ge(lg_ready, 1)
                act.activation(SIG[:], LG[:], ACT.Sigmoid).then_inc(sig_done, 1)
                for c in range(NC):
                    act.wait_ge(w9t_mm, c + 1)
                    if c >= 2:
                        act.wait_ge(bias_mm, c - 1)
                    act.copy(W9T[0:NE, CT * (c % 2):CT * (c % 2 + 1)], bank[6 + c % 2][0:NE, :]).then_inc(w9t_cp, 1)

                def turn(e, n0, slot):
                    act.copy(EXPERT[:, slot, :], EXPERTS[:, e, :]).then_inc(expert_cp, 1)
                    act.wait_ge(expert_cp, e + 1)
                    for c in range(NC):
                        n = n0 + c
                        for i in range(NI):
                            act.wait_ge(up_mm, n * 4 + (i + 1))
                            if live(2, n, 99):
                                act.wait_ge(split_done, n * 4 + (i - 7))
                            act.activation(G[:, c % 2, i, :], bank[i][:], ACT.Gelu, bias=EXPERT[:, slot, i:i + 1],
                                           scale=EXPERT[:, slot, NI:NI + 1]).then_inc(gelu_done, 1)

                turn(0, 0, 0)
                with act.Fori(0, NE // 2) as pair:
                    for slot in (1, 0):
                        e = 2 * pair + (2 - slot)
                        turn(e, e * 4, slot)

            def quantised_mlp():
                for c in range(NC):
                    act.wait_ge(xt_mm[8], c + 1)
                    if c >= 2:
                        act.wait_ge(xt_lo[8], c - 1)
                    act.activation(H32[:, c % 2, :], bank[6 + c % 2][:], ACT.Identity, bias=COLS[:, C_BETA:C_BETA + 1],
                                   scale=COLS[:, C_GAMMA:C_GAMMA + 1]).then_inc(h_sum, 1)
                for c in range(NC):
                    for i in range(NI):
                        act.wait_ge(f1_mm, 4 * c + i + 1)
                        if c >= 2:
                            act.wait_ge(f2_mm, c - 1)
                        act.activation(G[:, c % 2, i, :], bank[i][:], ACT.Silu, bias=COLS[:, C_B1 + i:C_B1 + i + 1],
                                       scale=COLS[:, C_S1 + i:C_S1 + i + 1]).then_inc(silu_done, 1)

            def fixed_point_mlp():
                for c in range(NC):
                    act.wait_ge(xt_mm[5], c + 1)
                    act.copy(XT32[:, CT * c:CT * (c + 1)], bank[6 + c % 2][:]).then_inc(xt_lo[5], 1)
                for m in range(6):
                    dst = GT if m < 3 else UT
                    for c in range(NC):
                        n = 4 * m + c
                        act.wait_ge(gu_mm, n + 1)
                        act.copy(dst[:, m % 3, CT * c:CT * (c + 1)], bank[n % 4][:]).then_inc(gu_cp, 1)
                for o in range(3):
                    act.wait_ge(gate_r, o + 1)
                    act.activation(TT[:, o, :], GT[:, o, :], ACT.Sigmoid).then_inc(sig2, 1)

            def int8_product():
                act.wait_ge(r_mm, 1)
                act.copy(RQT, bank[0][:].bitcast(F16)[:, 0:P]).then_inc(r_cp, 1)
                for c in range(NC):
                    act.wait_ge(xt_mm[7], c + 1)
                    act.copy(XQT[:, BC * c:BC * (c + 1), :].rearrange("p b t -> p (b t)"), bank[6 + c % 2][:].bitcast(F16)[:, 0:CT]
                             ).then_inc(xt_hi[7], 1)

            attention(0)
            experts()
            attention(1)
            quantised_mlp()
            attention(2)
            fixed_point_mlp()
            attention(3)
            int8_product()

        @block.vector
        def _(dve):
            order = SelfOrder(dve, dve_self)

            def power_scales(lo, hi):
                p2 = SMALL[:, 0:hi - lo]
                order(dve.tensor_scalar(p2.bitcast(I32), AMR[:, lo:hi].bitcast(I32), 0x7F800000, None, ALU.bitwise_and))
                order(dve.tensor_scalar(p2, p2, 2.0 ** -100, None, ALU.max))
                order(dve.tensor_scalar(DS[:, lo:hi], p2, 2.0 ** -14, None, ALU.mult))
                order(dve.reciprocal(p2, p2))
                order(dve.tensor_scalar(SC[:, lo:hi], p2, 2.0 ** 14, None, ALU.mult))

            def low(dst, src, scale, hi):
                return dve.scalar_tensor_tensor(out=dst, in0=src, scalar=scale, in1=hi, op0=ALU.mult, op1=ALU.subtract)

            def flat(ap):
                return ap.rearrange("p b t -> p (b t)")

            dve.wait_ge(ld_w, 16)
            dve.tensor_reduce(AM[:, 0:8], WRAW[:, 0:8, :], AX.X, ALU.max, apply_absolute_value=True)
            dve.tensor_reduce(AM[:, A_V:A_V + 1], WRAW[:, 8:12, :], AX.XY, ALU.max, apply_absolute_value=True)
            dve.wait_ge(ld_ctx, 16)
            dve.tensor_reduce(AM[:, A_CTX:A_CTX + 1], CRAW, AX.X, ALU.max, apply_absolute_value=True).then_inc(am_local, 1)
            dve.wait_ge(am_all, 1)
            power_scales(0, A_UP)
            order(dve.tensor_scalar(DK_[:, 0:4], DS[:, A_K:A_K + 4], DS[:, A_CTX:A_CTX + 1], None, ALU.mult))
            dve.tensor_scalar(DK_[:, 4:5], DS[:, A_V:A_V + 1], DS[:, A_CTX:A_CTX + 1], None, ALU.mult).then_inc(scales, 1)
            for c in range(NC):
                dve.wait_ge(ctx_hi, c + 1)
                low(flat(CTL[:, BC * c:BC * (c + 1), :]), CRAW[:, CT * c:CT * (c + 1)], SC[:, A_CTX:A_CTX + 1],
                    flat(CTH[:, BC * c:BC * (c + 1), :])).then_inc(ctx_lo, 1)
            for m in range(9):
                mats = slice(m, m + 1) if m < 8 else slice(8, 12)
                dve.wait_ge(w_hi, m + 1)
                low(flat(WAL[:, mats, :]), flat(WRAW[:, mats, :]), SC[:, m:m + 1], flat(WAH[:, mats, :])).then_inc(w_lo, 1)
            dve.wait_ge(ld_mask, 32)
            dve.tensor_scalar(MKH[:, 0, :], MKI[:], 0.0, -BIG, ALU.is_equal, ALU.mult).then_inc(mask_ready, 1)
            dve.tensor_scalar(MKH[:, 1, :], MK8, 0.0, -BIG, ALU.is_equal, ALU.mult).then_inc(mask_ready, 1)

            dve.wait_ge(ld_l2, 16)
            w = L2RAW.rearrange("p (k n) -> p k n", n=32)
            q = L2Q.rearrange("p (k n) -> p k n", n=32)
            blk = SMALL[:, 0:36]
            each = blk.rearrange("p (k o) -> p k o", o=1).to_broadcast((P, 36, 32))
            inv = SMALL[:, 64:100]
            order(dve.tensor_reduce(blk, w, AX.X, ALU.max, apply_absolute_value=True))
            order(dve.tensor_scalar(blk, blk, 1.0 / 7.0, 1e-12, ALU.mult, ALU.max))
            order(dve.reciprocal(inv, blk))
            order(dve.tensor_tensor(q, w, inv.rearrange("p (k o) -> p k o", o=1).to_broadcast((P, 36, 32)), ALU.mult))
            order(dve.tensor_scalar(L2Q, L2Q, ROUND, None, ALU.add))
            order(dve.tensor_scalar(L2Q, L2Q, ROUND, -8.0, ALU.subtract, ALU.max))
            order(dve.tensor_scalar(L2Q, L2Q, 7.0, None, ALU.min))
            dve.tensor_tensor(q, q, each, ALU.mult).then_inc(l2_deq, 1)

            def split_keys(c):
                for L in range(NL):
                    s = L % 2
                    dve.wait_ge(kp_sum, 4 * c + (L + 1))
                    if live(1, 2 * c + L // 2, 99):
                        dve.wait_ge(kp_put[s], c * 96 + 48 * (L // 2))
                    order(dve.tensor_copy(PJH[:, s, :], PJ[:, s, :]))
                    dve.tensor_tensor(PJL[:, s, :], PJ[:, s, :], PJH[:, s, :], ALU.subtract).then_inc(kp_lo, 1)

            split_keys(0)
            with dve.Fori(1, NC) as c:
                order.loop(c - 1, 4)
                split_keys(c)
                order.end(NC - 1)
            dve.wait_ge(v_ones, 1)
            dve.wait_ge(ld_small, 48)
            with dve.Fori(0, NB // 2) as it:
                for u in range(2):
                    dve.wait_ge(v_mm, 2 * it + (u + 1))
                    dve.scalar_tensor_tensor(out=VA[:, 2 * it + u, :, 0:DK],
                                             in0=bank[2 + u][:].rearrange("p (h d) -> p h d", d=DK), scalar=DK_[:, 4:5],
                                             in1=ROWS[:, R_BV:R_BV + CT].rearrange("p (h d) -> p h d", d=DK),
                                             op0=ALU.mult, op1=ALU.add).then_inc(v_out, 1)

            dve.wait_ge(ld_moe, 32)
            dve.tensor_reduce(AM[:, A_UP:A_UP + NE], UPRAW, AX.X, ALU.max, apply_absolute_value=True)
            dve.tensor_reduce(AM[:, A_DN:A_DN + NE], DNRAW, AX.X, ALU.max, apply_absolute_value=True)
            dve.tensor_reduce(AM[:, A_GW:A_GW + 1], COLS[:, C_GW:C_GW + 8], AX.X, ALU.max, apply_absolute_value=True)
            dve.tensor_reduce(AM[:, A_UB:A_UB + NE], COLS[:, C_UB:C_UB + 36].rearrange("p (e i) -> p e i", e=NE), AX.X,
                              ALU.max, apply_absolute_value=True).then_inc(am_local, 1)
            dve.wait_ge(am_all, 2)
            power_scales(A_UP, A_N)
            order(dve.tensor_copy(EXPERTS[:, :, 0:NI], COLS[:, C_UB:C_UB + 36].rearrange("p (e i) -> p e i", e=NE)))
            order(dve.tensor_copy(EXPERTS[:, :, NI], DS[:, A_UP:A_UP + NE]))
            order(dve.scalar_tensor_tensor(out=SMALL[:, 0:NE], in0=AMR[:, A_UP:A_UP + NE], scalar=float(P),
                                           in1=AMR[:, A_UB:A_UB + NE], op0=ALU.mult, op1=ALU.add))
            order(dve.tensor_scalar(SMALL[:, 0:NE].bitcast(I32), SMALL[:, 0:NE].bitcast(I32), 0x7F800000, None,
                                    ALU.bitwise_and))
            order(dve.tensor_scalar(SMALL[:, 0:NE], SMALL[:, 0:NE], 2.0 ** -100, None, ALU.max))
            order(dve.tensor_scalar(HS[:, 1, :], SMALL[:, 0:NE], 2.0 ** -14, None, ALU.mult))
            order(dve.reciprocal(SMALL[:, 0:NE], SMALL[:, 0:NE]))
            dve.tensor_scalar(HS[:, 0, :], SMALL[:, 0:NE], 2.0 ** 14, None, ALU.mult).then_inc(scales, 1)
            dve.wait_ge(moe_hi, 1)
            low(GWL[:], COLS[:, C_GW:C_GW + 8], SC[:, A_GW:A_GW + 1], GWH[:]).then_inc(moe_lo, 1)
            for e in range(NE):
                dve.wait_ge(moe_hi, 2 * e + 3)
                low(UPL[:, e, :], UPRAW[:, e, :], SC[:, A_UP + e:A_UP + e + 1], UPH[:, e, :]).then_inc(moe_lo, 1)
                low(DNL[:, e, :], DNRAW[:, e, :], SC[:, A_DN + e:A_DN + e + 1], DNH[:, e, :]).then_inc(moe_lo, 1)

            def stats(src, mv, batches):
                for b in batches:
                    ins = dve.bn_stats(ST6[:, b, :], src[:, b, :])
                order(ins)
                for b in batches:
                    ins = dve.bn_aggr(mv[:, b, :], ST6[:, b, :])
                return ins

            def inverse_root(mv):
                v, y, t = SMALL[:, 0:NB], RSTD[:], SMALL[:, 32:32 + NB]
                order(dve.tensor_scalar(v, mv[:, :, 1], EPS, None, ALU.add))
                order(dve.tensor_scalar(y.bitcast(I32), v.bitcast(I32), 1, None, ALU.logical_shift_right))
                order(dve.tensor_scalar(y.bitcast(I32), y.bitcast(I32), -1.0, float(0x5F3759DF), ALU.mult, ALU.add))
                for _ in range(3):
                    order(dve.tensor_tensor(t, y, y, ALU.mult))
                    order(dve.scalar_tensor_tensor(out=t, in0=t, scalar=-0.5, in1=v, op0=ALU.mult, op1=ALU.mult))
                    order(dve.scalar_tensor_tensor(out=y, in0=t, scalar=1.5, in1=y, op0=ALU.add, op1=ALU.mult))

            def normalise(dst, src, mv, ready):
                for b in range(NB):
                    dve.tensor_scalar(dst[:, b, :], src[:, b, :], mv[:, b, 0:1], RSTD[:, b:b + 1],
                                      ALU.subtract, ALU.mult).then_inc(ready, 1)

            def norm_lo(i):
                for c in range(NC):
                    dve.wait_ge(xt_hi[i], c + 1)
                    dve.tensor_tensor(flat(XTL[:, BC * c:BC * (c + 1), :]), bank[6 + c % 2][:],
                                      flat(XTH[:, BC * c:BC * (c + 1), :]), ALU.subtract).then_inc(xt_lo[i], 1)

            def attention(L):
                units0, batches0, chunks0 = earlier(L)
                inverse_root(MV)
                if L == 2:
                    dve.wait_ge(fc_ready, 2)
                    keep = SMALL[:, 64:64 + NB]
                    order(dve.tensor_reduce(keep, MB, AX.X, ALU.max))
                    order(dve.tensor_scalar(keep, keep, 0.0, None, ALU.is_equal))
                    order(dve.tensor_tensor(RSTD[:], RSTD[:], keep, ALU.mult))

                def normed(b):
                    dve.tensor_scalar(XN[:, b, :], X[:, b, :], MV[:, b, 0:1], RSTD[:, b:b + 1], ALU.subtract, ALU.mult
                                      ).then_inc(xn_ready[2 * L], 1)

                def lo_part(c, of):
                    dve.wait_ge(xt_hi[2 * L], c + 1)
                    dve.tensor_tensor(flat(XTL[:, BC * c:BC * (c + 1), :]), of[:], flat(XTH[:, BC * c:BC * (c + 1), :]),
                                      ALU.subtract).then_inc(xt_lo[2 * L], 1)

                def query_lo(c):
                    dve.wait_ge(q_sum, chunks0 + c + 1)
                    dve.tensor_tensor(PJL[:, c % 2, :], PJ[:, c % 2, :], PJH[:, c % 2, :], ALU.subtract).then_inc(q_lo, 1)

                for b in range(2 * BC):
                    normed(b)
                for c in range(2):
                    lo_part(c, bank[6 + c])
                for c in range(2):
                    query_lo(c)

                heads = bank[6][:].rearrange("p (h d) -> p h d", d=32)
                for n in range(STEPS):
                    b = due(n, L_LAG)
                    if b is not None:
                        dve.wait_ge(nm_hi, batches0 + b + 1)
                        low(NHL[:, b % 2, 1, :], bank[7][0:NH, 0:P], 1.0 / BIG, NHL[:, b % 2, 0, :]).then_inc(nm_lo, 1)
                    b = due(n, STAT_LAG)
                    if b is not None:
                        dve.wait_ge(x_done, batches0 + b + 1)
                        dve.bn_stats(ST6[:, b, :], X[:, b, :]).then_inc(st6_done, 1)
                    b = due(n, X_LAG)
                    if b is not None:
                        dve.wait_ge(y_done, batches0 + b + 1)
                        if L < 2:
                            dve.wait_ge(xb_done, NC * L + b // BC + 1)
                        dve.scalar_tensor_tensor(out=X[:, b, :], in0=bank[7][:, 2 * P:3 * P], scalar=TG[:, L:L + 1],
                                                 in1=X[:, b, :], op0=ALU.mult, op1=ALU.add).then_inc(x_done, 1)
                    if n < UNITS:
                        b, j = divmod(n, 4)
                        dve.wait_ge(s_done, units0 + n + 1)
                        if j == 0 and b >= 2:
                            dve.wait_ge(nt_done, batches0 + b - 1)
                        dve.tensor_reduce(NM[:, b % 2, 4 * j:4 * j + 4], bank[n % 2][:].rearrange("p (g t) -> p g t", g=NG),
                                          AX.X, ALU.max, negate=True).then_inc(max_done, 1)
                    b = due(n, STAT_LAG)
                    if b is not None:
                        dve.wait_ge(st6_done, batches0 + b + 1)
                        dve.bn_aggr(MV[:, b, :], ST6[:, b, :]).then_inc(mv_done, 1)
                    for c, at in T_STEP.items():
                        if 0 <= at - 1 - n < BC:
                            normed(BC * c + at - 1 - n)
                    c = chunk_at(T_STEP, n - 1)
                    if c is not None:
                        lo_part(c, bank[6])
                    c = chunk_at(Q_STEP, n - 1)
                    if c is not None:
                        query_lo(c)
                    b = due(n, REC_LAG)
                    if b is not None:
                        dve.wait_ge(t_mm, batches0 + b + 1)
                        dve.reciprocal(REC[:, b % 2, :], heads[:, :, DK]).then_inc(rec_done, 1)
                    b = due(n, ON_LAG)
                    if b is not None:
                        dve.wait_ge(rec_done, batches0 + b + 1)
                        if b >= 2:
                            dve.wait_ge(ot_done, batches0 + b - 1)
                        dve.tensor_tensor(ON[:, b % 2, :].rearrange("p (h d) -> p h d", d=DK), heads[:, :, 0:DK],
                                          REC[:, b % 2, :].rearrange("p (h o) -> p h o", o=1).to_broadcast((P, NH, DK)),
                                          ALU.mult).then_inc(on_done, 1)
                dve.wait_ge(mv_done, batches0 + NB)

            def experts():
                inverse_root(MV)
                normalise(XN, X, MV, xn_ready[1])
                norm_lo(1)
                def each(ap, n=8):
                    return ap.rearrange("p (b o) -> p b o", o=1).to_broadcast((P, NB, n))

                lg, key, sel, m = (SMALL[:, 0:0 + 128], SMALL[:, 128:256], W9[:], SMALL[:, 256:256 + NB])
                lg, key = (v.rearrange("p (b e) -> p b e", e=8) for v in (lg, key))
                sel = W9[:, :, 0:8]
                prio = ROWS[:, R_PRIO:R_PRIO + 8].rearrange("p (o e) -> p o e", o=1).to_broadcast((P, NB, 8))
                bias = ROWS[:, R_GBIAS:R_GBIAS + 8].rearrange("p (o e) -> p o e", o=1).to_broadcast((P, NB, 8))
                dve.wait_ge(gl_mm, 1)
                order(dve.tensor_scalar(LG[:], bank[0][:, 0:128].rearrange("p (b e) -> p b e", e=8),
                                        DS[:, A_GW:A_GW + 1], None, ALU.mult))
                dve.tensor_tensor(LG[:], LG[:], bias, ALU.add).then_inc(lg_ready, 1)
                dve.wait_ge(lg_ready, 1)
                order(dve.tensor_scalar(lg, LG[:], 16.6, -88.0, ALU.min, ALU.max))
                order(dve.memset(W9[:], 0.0))
                for _ in range(2):
                    order(dve.tensor_reduce(m, lg, AX.X, ALU.max))
                    order(dve.tensor_tensor(key, lg, each(m), ALU.is_equal))
                    order(dve.tensor_tensor(key, key, prio, ALU.mult))
                    order(dve.tensor_reduce(m, key, AX.X, ALU.max))
                    order(dve.tensor_tensor(key, key, each(m), ALU.is_equal))
                    order(dve.tensor_tensor(sel, sel, key, ALU.add))
                    order(dve.scalar_tensor_tensor(out=SMALL[:, 0:128], in0=SMALL[:, 128:256], scalar=-1e4,
                                                   in1=SMALL[:, 0:128], op0=ALU.mult, op1=ALU.add))
                dve.wait_ge(sig_done, 1)
                order(dve.tensor_tensor(sel, sel, SIG[:], ALU.mult))
                order(dve.tensor_reduce(m, sel, AX.X, ALU.add))
                order(dve.tensor_scalar(m, m, 1e-6, None, ALU.add))
                order(dve.reciprocal(m, m))
                order(dve.tensor_tensor(sel, sel, each(m), ALU.mult))
                order(dve.memset(W9[:, :, 8:9], 1.0))
                f = SMALL[:, 288:288 + NE]
                order(dve.tensor_tensor(f, DS[:, A_DN:A_DN + NE], HS[:, 1, :], ALU.mult))
                order(dve.tensor_scalar(f, f, 0.1, None, ALU.mult))
                dve.tensor_tensor(WF[:], W9[:], f.rearrange("p (o e) -> p o e", o=1).to_broadcast((P, NB, NE)),
                                  ALU.mult).then_inc(w9_ready, 1)
                for c in range(NC):
                    dve.wait_ge(bias_mm, c + 1)
                    dve.tensor_scalar(flat(ACC[:, BC * c:BC * (c + 1), :]), bank[4 + c % 2][:], 0.1, None, ALU.mult
                                      ).then_inc(acc_init, 1)

                def split(e, n, c):
                    for i in range(NI):
                        dve.wait_ge(gelu_done, n * 4 + (i + 1))
                        if live(2, n, 99):
                            dve.wait_ge(dn_mm, n - 1)
                        dve.tensor_scalar(GH[:, c % 2, i, :], G[:, c % 2, i, :], HS[:, 0, bass.ds(e, 1)], None, ALU.mult
                                          ).then_inc(gh_done, 1)
                        dve.wait_ge(gh_done, n * 4 + (i + 1))
                        low(GL[:, c % 2, i, :], G[:, c % 2, i, :], HS[:, 0, bass.ds(e, 1)], GH[:, c % 2, i, :]
                            ).then_inc(split_done, 1)

                def combine(e, n, c):
                    dve.wait_ge(dn_mm, n + 1)
                    dve.wait_ge(acc_init, NC)
                    if live(4, n, 99):
                        dve.wait_ge(comb_done, n - 3)
                    for t in range(BC):
                        b = BC * c + t
                        ins = dve.scalar_tensor_tensor(out=ACC[:, b, :], in0=bank[4 + c % 2][:, P * t:P * (t + 1)],
                                                       scalar=WF[:, b, bass.ds(e, 1)], in1=ACC[:, b, :],
                                                       op0=ALU.mult, op1=ALU.add)
                    ins.then_inc(comb_done, 1)

                def turn(e, n0, last):
                    for c in range(NC):
                        if c < NC - 1:
                            split(e, n0 + (c + 1), c + 1)
                        elif not last:
                            split(e + 1, n0 + NC, 0)
                        combine(e, n0 + c, c)

                split(0, 0, 0)
                turn(0, 0, False)
                with dve.Fori(1, NE - 1) as e:
                    turn(e, e * 4, False)
                turn(NE - 1, 4 * (NE - 1), True)
                dve.wait_ge(comb_done, NC * NE)
                order(dve.tensor_reduce(m, ACC[:], AX.X, ALU.max, apply_absolute_value=True))
                order(dve.tensor_scalar(m, m, 1e-6, None, ALU.add))
                order(dve.reciprocal(m, m))
                order(dve.tensor_scalar(m, m, TG[:, 4:5], None, ALU.mult))
                for c in range(NC):
                    for b in range(BC * c, BC * (c + 1)):
                        ins = dve.scalar_tensor_tensor(out=X[:, b, :], in0=ACC[:, b, :], scalar=SMALL[:, 256 + b:257 + b],
                                                       in1=X[:, b, :], op0=ALU.mult, op1=ALU.add)
                    order(ins)
                    order(stats(X, MV, range(BC * c, BC * (c + 1))))
                dve.memset(SCAL[:, 30:31], 0.0).then_inc(moe_done, 1)

            def quantised_mlp():
                inverse_root(MV)
                normalise(XN, X, MV, xn_ready[3])
                dve.wait_ge(xn_ready[3], NB)
                for c in range(NC):
                    order(stats(XN, MV2, range(BC * c, BC * (c + 1))))
                inverse_root(MV2)
                normalise(XN2, XN, MV2, xn_ready[8])
                order(dve.tensor_scalar(SCAL[:, 24:25], TG[:, 5:6], 0.5, None, ALU.mult))
                order(dve.scalar_tensor_tensor(out=flat(X[:]), in0=flat(XN[:]), scalar=TG[:, 5:6], in1=flat(X[:]),
                                               op0=ALU.mult, op1=ALU.add))
                order(dve.tensor_scalar(SMALL[:, 128:256], ROWS[:, R_B2:R_B2 + P], SCAL[:, 24:25], None, ALU.mult))
                order(dve.tensor_tensor(X[:], X[:],
                                        SMALL[:, 128:256].rearrange("p (o d) -> p o d", o=1).to_broadcast((P, NB, P)),
                                        ALU.add))
                for c in range(NC):
                    dve.wait_ge(h_sum, c + 1)
                    hi = flat(XTH[:, BC * c:BC * (c + 1), :])
                    order(dve.tensor_copy(hi, H32[:, c % 2, :]))
                    dve.tensor_tensor(flat(XTL[:, BC * c:BC * (c + 1), :]), H32[:, c % 2, :], hi, ALU.subtract
                                      ).then_inc(xt_lo[8], 1)
                for c in range(NC):
                    dve.wait_ge(f2_mm, c + 1)
                    for t in range(BC):
                        b = BC * c + t
                        ins = dve.scalar_tensor_tensor(out=X[:, b, :], in0=bank[4 + c % 2][:, P * t:P * (t + 1)],
                                                       scalar=SCAL[:, 24:25], in1=X[:, b, :], op0=ALU.mult, op1=ALU.add)
                        ins.then_inc(f2_out, 1)
                    dve.wait_ge(f2_out, BC * (c + 1))
                    order(stats(X, MV, range(BC * c, BC * (c + 1))))

            def fixed_point_mlp():
                part = [0]

                def global_max(pieces):
                    i = part[0]
                    for n, piece in enumerate(pieces):
                        order(dve.tensor_reduce(SCAL[:, 16 + n:17 + n], piece, AX.X, ALU.max, apply_absolute_value=True))
                    dve.tensor_reduce(SCAL[:, i:i + 1], SCAL[:, 16:16 + len(pieces)], AX.X, ALU.max).then_inc(gm_part, 1)
                    part[0] += 1

                def scale_of(i):
                    dve.wait_ge(gm_all, i + 1)
                    order(dve.tensor_scalar(SCAL[:, 22:23], SCAL[:, 8 + i:9 + i], 1.0 / 32767.0, 1e-12, ALU.mult, ALU.max))
                    order(dve.reciprocal(SCAL[:, 23:24], SCAL[:, 22:23]))

                def quantise(ap):
                    order(dve.tensor_scalar(ap, ap, SCAL[:, 23:24], ROUND, ALU.mult, ALU.add))
                    return dve.tensor_scalar(ap, ap, ROUND, SCAL[:, 22:23], ALU.subtract, ALU.mult)

                inverse_root(MV)
                normalise(XN, X, MV, l2_norm)
                dve.wait_ge(l2_norm, NB)
                global_max([flat(XN[:])])
                scale_of(0)
                for c in range(NC):
                    quantise(flat(XN[:, BC * c:BC * (c + 1), :])).then_inc(xn_ready[5], BC)
                for o in range(3):
                    dve.wait_ge(gu_cp, 4 * (o + 1))
                    order(dve.tensor_reduce(SCAL[:, 16 + o:17 + o], GT[:, o, :], AX.X, ALU.max, apply_absolute_value=True))
                dve.tensor_reduce(SCAL[:, 1:2], SCAL[:, 16:19], AX.X, ALU.max).then_inc(gm_part, 1)
                scale_of(1)
                for o in range(3):
                    quantise(GT[:, o, :]).then_inc(gate_r, 1)
                dve.wait_ge(gm_part, 2)
                for o in range(3):
                    dve.wait_ge(gu_cp, 12 + 4 * (o + 1))
                    order(dve.tensor_reduce(SCAL[:, 16 + o:17 + o], UT[:, o, :], AX.X, ALU.max, apply_absolute_value=True))
                dve.tensor_reduce(SCAL[:, 2:3], SCAL[:, 16:19], AX.X, ALU.max).then_inc(gm_part, 1)
                scale_of(2)
                for o in range(3):
                    order(quantise(UT[:, o, :]))
                for o in range(3):
                    dve.wait_ge(sig2, o + 1)
                    order(dve.tensor_scalar(TT[:, o, :], TT[:, o, :], 65536.0, ROUND, ALU.mult, ALU.add))
                    order(dve.tensor_scalar(TT[:, o, :], TT[:, o, :], ROUND, 65535.0, ALU.subtract, ALU.min))
                    order(dve.scalar_tensor_tensor(out=GT[:, o, :], in0=TT[:, o, :], scalar=2.0 ** -16, in1=GT[:, o, :],
                                                   op0=ALU.mult, op1=ALU.mult))
                part[0] = 3
                global_max([GT[:, o, :] for o in range(3)])
                scale_of(3)
                for o in range(3):
                    order(quantise(GT[:, o, :]))
                    order(dve.tensor_tensor(GT[:, o, :], GT[:, o, :], UT[:, o, :], ALU.mult))
                global_max([GT[:, o, :] for o in range(3)])
                scale_of(4)
                for o in range(3):
                    ins = quantise(GT[:, o, :])
                    if o < 2:
                        order(ins)
                ins.then_inc(o_q, 1)
                for c in range(NC):
                    for b in range(BC * c, BC * (c + 1)):
                        dve.wait_ge(d_mm, b + 1)
                        dve.scalar_tensor_tensor(out=X[:, b, :], in0=bank[4 + b % 2][:, 0:P], scalar=TG[:, 6:7],
                                                 in1=X[:, b, :], op0=ALU.mult, op1=ALU.add).then_inc(d_out, 1)
                    dve.wait_ge(d_out, BC * (c + 1))
                    order(stats(X, MV, range(BC * c, BC * (c + 1))))

            def int8_product():
                dve.wait_ge(ld_rhs, 16)
                order(dve.tensor_reduce(SCAL[:, 20:21], RT[:], AX.X, ALU.max, apply_absolute_value=True))
                order(dve.tensor_scalar(SCAL[:, 20:21], SCAL[:, 20:21], 1e-12, 1.0 / 127.0, ALU.max, ALU.mult))
                order(dve.reciprocal(SCAL[:, 21:22], SCAL[:, 20:21]))
                order(dve.tensor_scalar(RQ, RT[:], SCAL[:, 21:22], ROUND, ALU.mult, ALU.add))
                dve.tensor_scalar(RQH, RQ, ROUND, None, ALU.subtract).then_inc(r_q, 1)
                inverse_root(MV)
                normalise(XN, X, MV, xn_ready[7])
                dve.wait_ge(xn_ready[7], NB)
                ls, inv = SMALL[:, 64:64 + NB], SMALL[:, 96:96 + NB]
                order(dve.tensor_reduce(ls, XN[:], AX.X, ALU.max, apply_absolute_value=True))
                order(dve.tensor_scalar(ls, ls, 1e-12, 1.0 / 127.0, ALU.max, ALU.mult))
                order(dve.reciprocal(inv, ls))
                for c in range(NC):
                    for b in range(BC * c, BC * (c + 1)):
                        ins = dve.tensor_scalar(XN[:, b, :], XN[:, b, :], SMALL[:, 96 + b:97 + b], ROUND, ALU.mult, ALU.add)
                    order(ins)
                    dve.tensor_scalar(flat(XQH[:, BC * c:BC * (c + 1), :]), flat(XN[:, BC * c:BC * (c + 1), :]), ROUND,
                                      None, ALU.subtract).then_inc(xn_ready[7], 1)
                dve.wait_ge(r_mm, 2)
                dve.tensor_scalar(RSG, bank[1][:, 0:P], TG[:, 7:8], None, ALU.mult).then_inc(r_cp, 1)
                dve.wait_ge(r_cp, 2)
                for b in range(NB):
                    dve.wait_ge(z_mm, b + 1)
                    order(dve.scalar_tensor_tensor(out=ON[:, b % 2, :], in0=bank[4 + b % 2][:, 0:P],
                                                   scalar=SMALL[:, 64 + b:65 + b], in1=RSG, op0=ALU.mult, op1=ALU.mult))
                    dve.tensor_tensor(X[:, b, :], X[:, b, :], ON[:, b % 2, :], ALU.add).then_inc(z_out, 1)

            for put in kp_put:
                dve.wait_ge(put, 48 * NC * 2)
            dve.wait_ge(ld_x, 16)
            for c in range(NC):
                order(stats(X, MV, range(BC * c, BC * (c + 1))))
            attention(0)
            experts()
            attention(1)
            quantised_mlp()
            attention(2)
            fixed_point_mlp()
            attention(3)
            int8_product()


def _laid_out(x):
    f = np.float32
    m = np.arange(P)
    perm = DK * (NG * (m % 4) + m // 32) + m // 4 % 8
    t = [True, False, True, True]

    def w(L, name):
        v = np.asarray(x[f"L{L}_xattn_W{name}"])
        return v.T if t[L] else v

    def b(L, name):
        return np.asarray(x[f"L{L}_xattn_b{name}"]) if L < 2 else np.zeros(P, f)

    def row(*parts):
        return np.concatenate([np.asarray(p).reshape(-1) for p in parts]).reshape(1, -1)

    qk = [w(L, n)[:, perm] for n in "qk" for L in range(NL)]
    v = [w(L, "v") for L in range(NL)]
    up = np.concatenate([x["L0_ffn_up_w"], x["L0_ffn_sw_up"][None]])
    dn = np.concatenate([x["L0_ffn_down_w"], x["L0_ffn_sw_down"][None]])
    ub = np.concatenate([x["L0_ffn_up_b"], x["L0_ffn_sb_up"][None]])
    cols = ([b(L, "q")[perm] for L in range(NL)] + [b(L, "k")[perm] for L in range(NL)]
            + list(ub.reshape(NE * NI, P)) + list(x["L1_ffn_fc1_scales"].reshape(NI, P))
            + list(x["L1_ffn_fc1_bias"].reshape(NI, P)) + [x["L1_ffn_ln_gamma"], x["L1_ffn_ln_beta"]]
            + list(np.asarray(x["L0_ffn_gate_w"]).T))
    const = {side: np.zeros((DK, NG * CT), np.float16) for side in "qk"}
    const["q"][0] = BIG
    const["k"][1:3] = BIG
    return {
        "watt": np.stack(qk + v, 1),
        "ctx_t": x["ctx_1024"].transpose(2, 0, 1).reshape(P, NB * P),
        "x": x["x"].transpose(1, 0, 2),
        "cols": np.stack(cols, 1),
        "rows": row(x["g_xattn"], x["g_ffn"], x["L0_ffn_bias"], np.arange(8, 0, -1, dtype=f),
                    *[b(L, "v") for L in range(NL)], *[b(L, "o") for L in range(NL)],
                    x["L1_ffn_fc2_bias"], x["L1_ffn_fc2_scales"]),
        "down_b": np.concatenate([x["L0_ffn_down_b"], x["L0_ffn_sb_down"][None]]),
        "up_w": up.transpose(1, 0, 2),
        "down_w": dn.reshape(NE, NI, P, P).transpose(2, 0, 1, 3).reshape(P, NE, CT),
        "w_l2": np.concatenate([np.asarray(x[f"L2_ffn_w_{n}"]).reshape(3, P, P).transpose(1, 0, 2).reshape(P, 3 * P)
                                for n in ("gate", "up")] + [x["L2_ffn_w_down"]], 1),
        "wo": np.stack([w(L, "o").reshape(NG, 4, DK, P).transpose(1, 0, 2, 3).reshape(P, P) for L in range(NL)], 1),
        "rhs_t": x["L3_ffn_rhs"].T,
        "fc1_q": x["L1_ffn_fc1_q"],
        "fc2_q": x["L1_ffn_fc2_q"].reshape(NI, P, P).transpose(1, 0, 2).reshape(P, CT),
        "mask1": x["mask_BxS2_if1"],
        "mask2": x["mask_BxSxS2_if1"].transpose(1, 0, 2),
        "mask3": np.asarray(x["mask_BxS2_bk1"]).view(np.int32),
        "q_const": const["q"],
        "k_const": const["k"],
    }


def kernel(**inputs):
    import concourse.bacc as bacc
    from concourse.bass_utils import run_bass_kernel_spmd

    nc = bacc.Bacc("TRN2", target_bir_lowering=False, num_devices=1)
    arrays = {k: np.ascontiguousarray(v) for k, v in _laid_out({k: np.asarray(v) for k, v in inputs.items()}).items()}
    aps = {k: nc.dram_tensor(f"{k}_in", v.shape, mybir.dt.from_np(v.dtype), kind="ExternalInput").ap()
           for k, v in arrays.items()}
    out = nc.dram_tensor("out", (NB, P, P), F32, kind="ExternalOutput").ap()
    flamingo(nc, aps, out)
    r = run_bass_kernel_spmd(nc, [{f"{k}_in": v for k, v in arrays.items()}], core_ids=[0])
    return r.results[0]["out"]
```

```python
from contextlib import ExitStack

import numpy as np

import concourse.bass as bass
from concourse import mybir

F32 = mybir.dt.float32
F16 = mybir.dt.float16
I32 = mybir.dt.int32
U8 = mybir.dt.uint8
ACT = mybir.ActivationFunctionType
ALU = mybir.AluOpType
AX = mybir.AxisListType
ABSMAX = bass.bass_isa.ReduceOp.absmax

P = 128
NB = 16
NL = 4
NH = 16
DK = 8
NC = 4
CT = 512
BC = NB // NC
NG = 4
NE = 9
NI = 4
BIG = 32768.0
MASK_ROW = 3
LO_AT = 32
ROUND = 12582912.0
EPS = 1e-5

R_GATES, R_GBIAS, R_PRIO, R_BV, R_BO = 0, 8, 16, 24, 536
R_B2, R_S2, R_N = 1048, 1176, 1688
C_BQ, C_BK, C_UB, C_S1, C_B1, C_GAMMA, C_BETA, C_GW, C_N = 0, 4, 8, 44, 48, 52, 53, 54, 62
A_Q, A_K, A_V, A_CTX, A_UP, A_DN, A_GW, A_UB, A_N = 0, 4, 8, 9, 10, 19, 28, 29, 38

UNITS = NB * 4
VA_N = NB * NL * NH * (DK + 1)
ST_LAG, PV_LAG = 8, 9
NT_LAG, L_LAG = 5, 6
OC_LAG, T_LAG, REC_LAG, ON_LAG, OT_LAG, Y_LAG, X_LAG, STAT_LAG = 13, 15, 15, 16, 18, 20, 21, 22
STEPS = 4 * (NB - 1) + STAT_LAG + 1
T_STEP = {c: 4 * BC * c - 15 for c in range(2, NC)}
Q_STEP = {c: 4 * BC * c - 11 for c in range(2, NC)}


V_STEP = {c: 5 + c for c in range(NC)}
K_STEP = {0: 25, 1: 29, 2: 41, 3: 45}


def query_job(L, c):
    return NC + 2 * NC * L + (c if c < 3 or L == NL - 1 else 5)


def key_job(L, c):
    return c if L == 0 else NC + 2 * NC * (L - 1) + (3, 4, 6, 7)[c]


def chunk_at(steps, n):
    return next((c for c, at in steps.items() if at == n), None)


def low(engine, dst, src, scale, hi):
    return engine.scalar_tensor_tensor(out=dst, in0=src, scalar=scale, in1=hi, op0=ALU.mult, op1=ALU.subtract)


def due(n, lag):
    b, off = divmod(n - lag, 4)
    return b if off == 0 and 0 <= b < NB else None


def live(lo, v, hi):
    return lo <= v < hi if isinstance(v, int) else True


def earlier(L):
    return UNITS * L, NB * L, NC * L


class SelfOrder:

    def __init__(self, engine, sem):
        self.engine, self.sem, self.n, self.base = engine, sem, 0, 0

    def __call__(self, ins):
        self.n += 1
        ins.then_inc(self.sem, 1)
        self.engine.wait_ge(self.sem, self.base + self.n)

    def loop(self, i, per):
        self.base, self.start = i * per, self.n
        self.per = per

    def end(self, trips):
        assert self.n - self.start == self.per, (self.n - self.start, self.per)
        self.base, self.n = 0, self.start + trips * self.per


def flamingo(nc, a, out):
    with ExitStack() as ctx:
        def sb(name, shape, dt=F32):
            return ctx.enter_context(nc.sbuf_tensor(name, shape, dt))

        def sem(name):
            return ctx.enter_context(nc.semaphore(name))

        def sems(name, n=NL):
            return [sem(f"{name}{i}") for i in range(n)]

        bank = [ctx.enter_context(nc.psum_tensor(f"bank{i}", [P, CT], F32)) for i in range(8)]

        X = sb("X", [P, NB, P])
        XT = sb("XT", [P, 2, NB, P], F16)
        XTH, XTL = XT[:, 0], XT[:, 1]
        XT32 = XT[:].rearrange("p s b t -> p (s b t)").bitcast(F32)
        CTH = sb("CTH", [P, NB, P], F16)
        CTL = sb("CTL", [P, NB, P], F16)
        WAH = sb("WAH", [P, 12, P], F16)
        WAL = sb("WAL", [P, 12, P], F16)
        WO = sb("WO", [P, NL, P])
        VAF = sb("VAF", [P, VA_N + 32])
        VA = VAF[:, 0:VA_N].rearrange("p (b h d) -> p b h d", b=NB, h=NL * NH)
        SK = sb("SK", [P, 4, CT], F16)
        SQ = sb("SQ", [P, 4, 4, CT], F16)
        XN = SQ[:].rearrange("p s j t -> p (s j t)").bitcast(F32)[:, 0:NB * P].rearrange("p (b d) -> p b d", b=NB)
        SEL = sb("SEL", [LO_AT + NH, NH], F16)
        PR = sb("PR", [P, 4, CT])
        ROWS = sb("ROWS", [P, R_N])
        COLS = sb("COLS", [P, C_N])
        DB = sb("DB", [NE, P])
        PJ = sb("PJ", [P, 2, CT])
        PJH = sb("PJH", [P, 2, CT], F16)
        PJL = sb("PJL", [P, 2, CT], F16)
        FC1 = sb("FC1", [P, CT], F16)
        FC2 = sb("FC2", [P, NI, P])
        ID = sb("ID", [P, P])
        IDH = sb("IDH", [P, P], F16)
        IDB = sb("IDB", [P, P], F16)
        MV = sb("MV", [P, NB, 2])
        ST6 = sb("ST6", [P, NB, 6])
        RSTD = sb("RSTD", [P, NB])
        NM = sb("NM", [P, 2, NH])
        NHL = sb("NHL", [LO_AT + NH, 2, P], F16)
        REC = sb("REC", [P, 2, NH])
        OC = sb("OC", [P, 2, CT])
        ON = sb("ON", [P, 2, P])
        OT = sb("OT", [P, 2, P])
        AM = sb("AM", [P, A_N])
        AMR = sb("AMR", [P, A_N])
        SC = sb("SC", [P, A_N])
        DS = sb("DS", [P, A_N])
        SMALL = sb("SMALL", [P, 320])
        GWH = sb("GWH", [P, 8], F16)
        GWL = sb("GWL", [P, 8], F16)
        LG = sb("LG", [P, NB, 8])
        SIG = sb("SIG", [P, NB, 8])
        W9 = sb("W9", [P, NB, NE])
        WF = sb("WF", [P, NB, NE])
        DK_ = sb("DK_", [P, 8])
        HS = sb("HS", [P, 2, NE])
        EXPERTS = sb("EXPERTS", [P, NE, NI + 2])
        EXPERT = sb("EXPERT", [P, 2, NI + 2])
        TG = sb("TG", [P, 8])
        SCAL = sb("SCAL", [P, 32])
        SCALE = sb("SCALE", [P, 18])
        BLK = sb("BLK", [P, 2, 36])
        RT = sb("RT", [P, P])
        MV2 = sb("MV2", [P, NB, 2])
        MKH = sb("MKH", [NB, 2, P], F16)
        MK8W = sb("MK8", [NB, P // 4], I32)
        MK8 = MK8W[:].bitcast(U8)
        MKI = sb("MKI", [NB, P], I32)
        REGION = sb("REGION", [P, 19456])

        def region(at, n, dt=F32):
            v = REGION[:, at:at + n]
            return v if dt == F32 else v.bitcast(dt)

        UPH = region(0, 2304, F16).rearrange("p (e i) -> p e i", e=NE)
        UPL = region(2304, 2304, F16).rearrange("p (e i) -> p e i", e=NE)
        DNH = region(4608, 2304, F16).rearrange("p (e i) -> p e i", e=NE)
        DNL = region(6912, 2304, F16).rearrange("p (e i) -> p e i", e=NE)
        G = region(9216, 4096).rearrange("p (s i t) -> p s i t", s=2, i=NI)
        GH = region(13312, 2048, F16).rearrange("p (s i t) -> p s i t", s=2, i=NI)
        GL = region(15360, 2048, F16).rearrange("p (s i t) -> p s i t", s=2, i=NI)
        ACC = region(17408, 2048).rearrange("p (b h) -> p b h", b=NB)
        W9T = region(9216, 1024)
        UPRAW = region(9216, 4608).rearrange("p (e i) -> p e i", e=NE)
        DNRAW = region(13824, 4608).rearrange("p (e i) -> p e i", e=NE)
        FC1I = region(0, 512, I32)
        FC2I = region(512, 512, I32)
        MRAW = region(1024, 2048, I32).rearrange("p (b k) -> p b k", b=NB)
        XN2 = region(4096, 2048).rearrange("p (b h) -> p b h", b=NB)
        H32 = region(3072, 1024).rearrange("p (s t) -> p s t", s=2)
        L2RAW = region(6144, 9 * P)
        MB = region(18432, 1024, F16).rearrange("p (b k) -> p b k", b=NB)
        GT = region(0, 6144).rearrange("p (o t) -> p o t", o=3)
        UT = region(6144, 6144).rearrange("p (o t) -> p o t", o=3)
        TT = (XT32, XN.rearrange("p b d -> p (b d)"), region(12288, 2048))
        WL2T = region(14336, 9 * P).rearrange("p (m o) -> p m o", m=9)
        XNC = [region(18432 if L == 0 else 17408, 2 * CT).rearrange("p (s i d) -> p s i d", s=2, i=BC) for L in range(NL)]
        RQ = region(128, 128)
        RQH = region(256, 64, F16)
        RQT = region(320, 64, F16)
        RSG = region(384, 128)
        XQH = region(1024, 1024, F16).rearrange("p (b h) -> p b h", b=NB)
        XQT = region(2048, 1024, F16).rearrange("p (b h) -> p b h", b=NB)
        WRAW = PR[:].rearrange("p s t -> p (s t)")[:, 0:12 * P].rearrange("p (m o) -> p m o", m=12)
        CRAW = VAF[:, 0:NB * P]

        kscr = nc.dram_tensor("kscr", (NL * NC, P, NG * CT), F16, kind="Internal").ap()
        qscr = nc.dram_tensor("qscr", (NC, P, NG * CT), F16, kind="Internal").ap()
        mscr = nc.dram_tensor("mscr", (2, NC, CT), F16, kind="Internal").ap()

        ld_w, ld_ctx, ld_x, ld_small, ld_wo, ld_moe, ld_l2 = (
            sem(n) for n in ("ld_w", "ld_ctx", "ld_x", "ld_small", "ld_wo", "ld_moe", "ld_l2"))
        ld_mask, ld_fc, ld_rhs, ld_sel = sem("ld_mask"), sem("ld_fc"), sem("ld_rhs"), sem("ld_sel")
        scr_init, mask_put, mask_rows = sem("scr_init"), sem("mask_put"), sem("mask_rows")
        ident = sem("ident")
        am_local, am_all, scales = sem("am_local"), sem("am_all"), sem("scales")
        tanh_done = sem("tanh_done")
        ctx_hi, ctx_lo, w_hi, w_lo = sem("ctx_hi"), sem("ctx_lo"), sem("w_hi"), sem("w_lo")
        moe_hi, moe_lo = sem("moe_hi"), sem("moe_lo")
        mask_ready = sem("mask_ready")
        l2_deq, l2_tr, l2_cp = sem("l2_deq"), sem("l2_tr"), sem("l2_cp")
        p_mm, p_sum, p_lo = sem("p_mm"), sem("p_sum"), sem("p_lo")
        p_put = sems("p_put", 2)
        v_mm, v_out, v_ones = sem("v_mm"), sem("v_out"), sem("v_ones")
        xn_ready, xt_mm, xt_hi, xt_lo = (sems(n, 9) for n in ("xn_ready", "xt_mm", "xt_hi", "xt_lo"))
        stack_in, zeroed = sems("stack_in", 4), sem("zeroed")
        s_done, max_done, nt_done, nm_hi, nm_lo = (
            sem(n) for n in ("s_done", "max_done", "nt_done", "nm_hi", "nm_lo"))
        st_done, exp_done, pv_done = sem("st_done"), sem("exp_done"), sem("pv_done")
        oc_cp, t_mm, rec_done, on_done, ot_done, ot_cp = (
            sem(n) for n in ("oc_cp", "t_mm", "rec_done", "on_done", "ot_done", "ot_cp"))
        y_done, x_done, xb_done, st6_done, mv_done = (
            sem(n) for n in ("y_done", "x_done", "xb_done", "st6_done", "mv_done"))
        gl_mm, sig_done, w9_ready, w9t_mm, w9t_cp, bias_mm, acc_init = (
            sem(n) for n in ("gl_mm", "sig_done", "w9_ready", "w9t_mm", "w9t_cp", "bias_mm", "acc_init"))
        lg_ready, gh_done, l2_norm = sem("lg_ready"), sem("gh_done"), sem("l2_norm")
        up_mm, gelu_done, split_done, dn_mm, comb_done = (
            sem(n) for n in ("up_mm", "gelu_done", "split_done", "dn_mm", "comb_done"))
        moe_done = sem("moe_done")
        fc_ready, h_sum, f1_mm, silu_done, f2_mm, f2_out = (
            sem(n) for n in ("fc_ready", "h_sum", "f1_mm", "silu_done", "f2_mm", "f2_out"))
        gm_part, gm_all = sem("gm_part"), sem("gm_all")
        gu_mm, gu_cp, gq_done, gate_r, sig2, o_q, d_mm, d_out = (
            sem(n) for n in ("gu_mm", "gu_cp", "gq_done", "gate_r", "sig2", "o_q", "d_mm", "d_out"))
        r_q, r_mm, r_cp, z_mm, z_out, stored = (
            sem(n) for n in ("r_q", "r_mm", "r_cp", "z_mm", "z_out", "stored"))
        expert_cp = sem("expert_cp")
        l2_inv, up_scale, up_q = sem("l2_inv"), sem("up_scale"), sem("up_q")
        dve_self, pool_self = sem("dve_self"), sem("pool_self")

        block = ctx.enter_context(nc.Block())

        @block.sync
        def _(sp):
            sp.dma_start(WRAW, a["watt"]).then_inc(ld_w, 16)
            sp.dma_start(CRAW, a["ctx_t"]).then_inc(ld_ctx, 16)
            sp.dma_start(COLS[:], a["cols"]).then_inc(ld_small, 16)
            sp.dma_start(ROWS[:], a["rows"].partition_broadcast(P)).then_inc(ld_small, 16)
            sp.dma_start(DB[:], a["down_b"]).then_inc(ld_small, 16)
            sp.dma_start(X[:], a["x"]).then_inc(ld_x, 16)
            sp.dma_start(UPRAW, a["up_w"]).then_inc(ld_moe, 16)
            sp.dma_start(DNRAW, a["down_w"]).then_inc(ld_moe, 16)
            sp.dma_start(RT[:], a["rhs_t"]).then_inc(ld_rhs, 16)
            sp.dma_start(WO[:], a["wo"]).then_inc(ld_wo, 16)

            def put(job, scr, side):
                sp.wait_ge(p_lo, job + 1)
                dst = scr.rearrange("(m r) (g t) -> r m g t", r=4, g=NG)
                for row, part in enumerate((PJH, PJL, PJH) if side == "k" else (PJH, PJH, PJL)):
                    sp.dma_start(dst[row], part[:, job % 2, :]).then_inc(p_put[job % 2], 16)

            def put_keys(L, c):
                put(key_job(L, c), kscr[L * NC + c], "k")

            def put_queries(L, c):
                put(query_job(L, c), qscr[c], "q")

            def wait_written(job):
                for j in (job, job - 1):
                    sp.wait_ge(p_put[j % 2], 48 * (j // 2 + 1))

            sp.wait_ge(scr_init, 32)
            for c in range(NC):
                put_keys(0, c)

            def load(L, b):
                c, i = divmod(b, BC)
                cols = slice(P * i, P * (i + 1))
                k, q = (src.rearrange("p (g t) -> p g t", g=NG)[:, :, cols] for src in (kscr[L * NC + c], qscr[c]))
                sp.dma_start(SK[:, i, :].rearrange("p (g t) -> p g t", g=NG), k).then_inc(stack_in[i], 16)
                for j in range(4):
                    rows = slice(32 * j, 32 * (j + 1))
                    sp.dma_start(SQ[rows, i, j, :].rearrange("p (g t) -> p g t", g=NG), q[rows]).then_inc(stack_in[i], 16)

            for L in range(NL):
                units0, batches0, chunks0 = earlier(L)
                if L == 1:
                    sp.wait_ge(mask_rows, 16 * 2 * NC)
                put_queries(L, 0)
                wait_written(query_job(L, 0))
                sp.wait_ge(zeroed, L + 1)
                load(L, 0)
                put_queries(L, 1)
                for b in range(1, BC):
                    load(L, b)
                for b in range(BC, NB):
                    c, i = divmod(b, BC)
                    sp.wait_ge(st_done, units0 + 4 * (b - BC + 1))
                    if i == 0:
                        if c > 1:
                            put_queries(L, c)
                        wait_written(query_job(L, c))
                    load(L, b)
                    c = chunk_at({k: (at + 2) // 4 + 2 for k, at in K_STEP.items()}, b)
                    if c is not None and L < NL - 1:
                        put_keys(L + 1, c)

            for c in range(NC):
                sp.wait_ge(z_out, BC * (c + 1))
                sp.dma_start(out[BC * c:BC * (c + 1)].rearrange("b t d -> t b d"),
                             X[:, BC * c:BC * (c + 1), :]).then_inc(stored, 16)
            sp.wait_ge(stored, 16 * NC)

        @block.gpsimd
        def _(pool):
            order = SelfOrder(pool, pool_self)
            for scr, name, n in ((qscr, "q_const", 4 * NC), (kscr, "k_const", 4 * NL * NC)):
                dst = scr.rearrange("c (j i r) t -> r (c j) i t", j=4, r=4)[3]
                pool.dma_start(dst, a[name].rearrange("(o r) t -> o r t", o=1).to_broadcast((n, DK, NG * CT))
                               ).then_inc(scr_init, 16)
            pool.dma_start(MKI[:], a["mask1"]).then_inc(ld_mask, 16)
            pool.dma_start(MK8W[:], a["mask3"]).then_inc(ld_mask, 16)
            order(pool.memset(ID[:], 0.0))
            order(pool.affine_select(out=ID[:], in_=ID[:], compare_op=ALU.not_equal, fill=1.0, base=0,
                                     pattern=[[-1, P]], channel_multiplier=1))
            pool.tensor_copy(IDH[:], ID[:]).then_inc(ident, 1)
            pool.tensor_scalar(IDB[:], ID[:], BIG, 1.0, ALU.mult, ALU.mult).then_inc(ident, 1)
            pool.dma_start(SEL[:], a["select"]).then_inc(ld_sel, 16)
            order(pool.memset(NHL[:], 0.0))

            def zero_stacks():
                pool.memset(SQ[:].rearrange("p s j t -> p (s j t)").bitcast(F32), 0.0).then_inc(zeroed, 1)

            zero_stacks()
            pool.wait_ge(am_local, 1)
            pool.partition_all_reduce(AMR[:, 0:A_UP], AM[:, 0:A_UP], P, ABSMAX).then_inc(am_all, 1)
            pool.wait_ge(ctx_lo, NC)
            order(pool.memset(VAF[:, VA_N:], 0.0))
            pool.memset(VA[:, :, :, DK:DK + 1], 1.0).then_inc(v_ones, 1)
            pool.wait_ge(am_local, 2)
            pool.partition_all_reduce(AMR[:, A_UP:], AM[:, A_UP:], P, ABSMAX).then_inc(am_all, 1)
            pool.wait_ge(mask_ready, 2)
            pool.wait_ge(scr_init, 32)
            pool.dma_start(mscr.rearrange("i c (b t) -> (c b) i t", b=BC), MKH[:]).then_inc(mask_put, 16)
            pool.wait_ge(mask_put, 16)
            for i, L in enumerate((1, 3)):
                for c in range(NC):
                    dst = kscr[L * NC + c].rearrange("(j r) (g t) -> r j g t", r=32, g=NG)[MASK_ROW]
                    src = mscr[i:i + 1, c:c + 1, :].to_broadcast((4, NG, CT))
                    pool.dma_start(dst, src).then_inc(mask_rows, 16)

            def residual_bias(L):
                gbo = SMALL[:, 192:320]
                order(pool.tensor_scalar(gbo, ROWS[:, R_BO + P * L:R_BO + P * (L + 1)], TG[:, L:L + 1], 1.0,
                                         ALU.mult, ALU.mult))
                for c in range(NC):
                    pool.wait_ge(xn_ready[2 * L], BC * (c + 1))
                    xc = X[:, BC * c:BC * (c + 1), :]
                    pool.tensor_tensor(xc, xc, gbo.rearrange("p (o d) -> p o d", o=1).to_broadcast((P, BC, P)), ALU.add
                                       ).then_inc(xb_done, 1)

            pool.wait_ge(tanh_done, 1)
            residual_bias(0)
            for e in range(NE):
                for i, (lo, raw, hi, at) in enumerate(((UPL, UPRAW, UPH, A_UP), (DNL, DNRAW, DNH, A_DN))):
                    pool.wait_ge(moe_hi, 2 * e + i + 2)
                    order(pool.tensor_scalar(raw[:, e, :], raw[:, e, :], SC[:, at + e:at + e + 1], 1.0, ALU.mult, ALU.mult))
                    pool.tensor_tensor(lo[:, e, :], raw[:, e, :], hi[:, e, :], ALU.subtract).then_inc(moe_lo, 1)
            pool.wait_ge(moe_done, 1)
            pool.dma_start(FC1I, a["fc1_q"]).then_inc(ld_fc, 16)
            pool.dma_start(FC2I, a["fc2_q"]).then_inc(ld_fc, 16)
            pool.dma_start(MRAW, a["mask2"]).then_inc(ld_fc, 16)
            pool.dma_start(L2RAW, a["w_l2"]).then_inc(ld_l2, 16)
            zero_stacks()
            residual_bias(1)
            pool.wait_ge(ld_fc, 48)
            pool.tensor_scalar(FC1[:], FC1I, -128.0, None, ALU.add).then_inc(fc_ready, 1)
            order(pool.tensor_scalar(FC2[:].rearrange("p i o -> p (i o)"), FC2I, -128.0, None, ALU.add))
            order(pool.tensor_tensor(FC2[:].rearrange("p i o -> p (i o)"), FC2[:].rearrange("p i o -> p (i o)"),
                                     ROWS[:, R_S2:R_S2 + CT], ALU.mult))
            order(pool.tensor_scalar(MB, MRAW, 0.0, -BIG, ALU.is_equal, ALU.mult))
            pool.memset(SCAL[:, 31:32], 0.0).then_inc(fc_ready, 1)
            w = L2RAW.rearrange("p (k n) -> p k n", n=32)
            scale, inv = (v.rearrange("p (k o) -> p k o", o=1).to_broadcast((P, 36, 32)) for v in (BLK[:, 0], BLK[:, 1]))
            pool.wait_ge(l2_inv, 1)
            order(pool.tensor_tensor(w, w, inv, ALU.mult))
            order(pool.tensor_scalar(L2RAW, L2RAW, ROUND, None, ALU.add))
            order(pool.tensor_scalar(L2RAW, L2RAW, ROUND, -8.0, ALU.subtract, ALU.max))
            order(pool.tensor_scalar(L2RAW, L2RAW, 7.0, None, ALU.min))
            pool.tensor_tensor(w, w, scale, ALU.mult).then_inc(l2_deq, 1)
            pool.wait_ge(f2_out, NB)
            zero_stacks()
            for i in range(5):
                pool.wait_ge(gm_part, i + 1)
                pool.partition_all_reduce(SCAL[:, 8 + i:9 + i], SCAL[:, i:i + 1], P, ABSMAX).then_inc(gm_all, 1)
                if i == 2:
                    pool.wait_ge(up_scale, 1)
                    for o in range(3):
                        order(pool.tensor_scalar(UT[:, o, :], UT[:, o, :], SCALE[:, 10:11], ROUND, ALU.mult, ALU.add))
                        pool.tensor_scalar(UT[:, o, :], UT[:, o, :], -ROUND, 1.0, ALU.add, ALU.mult).then_inc(up_q, 1)
            pool.wait_ge(d_out, NB)
            zero_stacks()

        @block.tensor
        def _(pe):
            def product3(dst, wh, wl, xh, xl, start=True, stop=True):
                pe.matmul(dst, wh, xh, start=start, stop=False)
                pe.matmul(dst, wh, xl, start=False, stop=False)
                return pe.matmul(dst, wl, xh, start=False, stop=stop)

            def norm_transposes(i, src, stage=6):
                for c in range(NC):
                    pe.wait_ge(xn_ready[i], BC * (c + 1))
                    if c >= 2:
                        pe.wait_ge(xt_lo[i], c - 1)
                    for b in range(BC):
                        mm = pe.transpose(bank[stage + c % 2][:, P * b:P * (b + 1)], src[:, BC * c + b, :], ID[:])
                    mm.then_inc(xt_mm[i], 1)

            def keys(L, c, to):
                product3(to[:], WAH[:, 4 + L, :], WAL[:, 4 + L, :],
                         CTH[:, BC * c:BC * (c + 1), :], CTL[:, BC * c:BC * (c + 1), :]).then_inc(p_mm, 1)

            def values_of(L, c, to):
                for i in range(BC):
                    mm = product3(to[:, P * i:P * (i + 1)], CTH[:, BC * c + i, :], CTL[:, BC * c + i, :],
                                  WAH[:, 8 + L, :], WAL[:, 8 + L, :])
                mm.then_inc(v_mm, 1)

            pe.wait_ge(ident, 2)
            pe.wait_ge(w_lo, 9)
            pe.wait_ge(ctx_lo, NC)
            for c in range(NC):
                keys(0, c, bank[c])

            def attention(L):
                units0, batches0, chunks0 = earlier(L)
                def transposes(c, to):
                    pe.wait_ge(xn_ready[2 * L], BC * (c + 1))
                    for i in range(BC):
                        mm = pe.transpose(to[:, P * i:P * (i + 1)], XNC[L][:, c % 2, i, :], ID[:])
                    mm.then_inc(xt_mm[2 * L], 1)

                def queries(c, to):
                    pe.wait_ge(xt_lo[2 * L], c + 1)
                    product3(to[:], WAH[:, L, :], WAL[:, L, :],
                             XTH[:, BC * c:BC * (c + 1), :], XTL[:, BC * c:BC * (c + 1), :]).then_inc(p_mm, 1)

                if L == 2:
                    pe.wait_ge(l2_cp, 3)
                if L == 0:
                    pe.wait_ge(ld_sel, 16)
                for c in range(2):
                    transposes(c, bank[6 + c])
                if L == 0:
                    pe.wait_ge(p_sum, NC)
                for c in range(2):
                    queries(c, bank[4 + c])
                if L == 0:
                    for c in range(NC):
                        values_of(0, c, bank[c])
                pe.wait_ge(p_sum, query_job(L, 1) + 1)
                if L == 0:
                    pe.wait_ge(v_out, NB)

                def scores(n):
                    b, j = divmod(n, 4)
                    slot = b % 4
                    dst = bank[n % 2]
                    if j == 0:
                        pe.wait_ge(stack_in[slot], 20 * batches0 + 80 * (b // 4 + 1))
                    if n >= 2:
                        pe.wait_ge(max_done, units0 + n - 1)
                    for g in range(NG):
                        cols = slice(P * g, P * (g + 1))
                        if L == 2:
                            pe.matmul(dst[:, cols], IDB[:], MB[:, b, :], start=True, stop=False)
                        mm = pe.matmul(dst[:, cols], SQ[:, slot, j, cols], SK[:, slot, cols], start=L != 2, stop=True)
                    mm.then_inc(s_done, 1)

                def shifted(n):
                    b, j = divmod(n, 4)
                    slot = b % 4
                    dst = bank[2 + n % 2]
                    if j == 0:
                        pe.wait_ge(nm_lo, batches0 + b + 1)
                    if n >= 2:
                        pe.wait_ge(exp_done, units0 + n - 1)
                    for g in range(NG):
                        cols = slice(P * g, P * (g + 1))
                        if L == 2:
                            pe.matmul(dst[:, cols], MB[:, b, :], IDB[:], start=True, stop=False)
                        pe.matmul(dst[:, cols], SK[:, slot, cols], SQ[:, slot, j, cols], start=L != 2, stop=False)
                        mm = pe.matmul(dst[:, cols], SEL[:, NG * j + g:NG * j + g + 1].to_broadcast((LO_AT + NH, P)),
                                       NHL[:, b % 2, :], start=False, stop=True)
                    mm.then_inc(st_done, 1)

                def values(n):
                    b, j = divmod(n, 4)
                    pe.wait_ge(exp_done, units0 + n + 1)
                    if j == 0 and b >= 2:
                        pe.wait_ge(oc_cp, batches0 + b - 1)
                    for g in range(NG):
                        at = ((b * NL + L) * NH + NG * g + j) * (DK + 1)
                        mm = pe.matmul(bank[4 + b % 2][32 * g:32 * (g + 1), P * j:P * (j + 1)],
                                       VAF[:, at:at + 32], PR[:, j, P * g:P * (g + 1)], start=True, stop=True)
                    mm.then_inc(pv_done, 1)

                for n in range(STEPS):
                    if n < UNITS:
                        scores(n)
                    if 0 <= n - ST_LAG < UNITS:
                        shifted(n - ST_LAG)
                    if n == PV_LAG:
                        pe.wait_ge(v_out, NB * min(L + 2, NL))
                    b = due(n, Y_LAG)
                    if b is not None:
                        pe.wait_ge(ot_cp, batches0 + b + 1)
                        pe.matmul(bank[7][:, 2 * P:3 * P], OT[:, b % 2, :], WO[:, L, :], start=True, stop=True
                                  ).then_inc(y_done, 1)
                    if 0 <= n - PV_LAG < UNITS:
                        values(n - PV_LAG)
                    b = due(n, T_LAG)
                    if b is not None:
                        pe.wait_ge(oc_cp, batches0 + b + 1)
                        if b >= 1:
                            pe.wait_ge(on_done, batches0 + b)
                        c = chunk_at(T_STEP, n - 2)
                        if c is not None:
                            pe.wait_ge(xt_lo[2 * L], c + 1)
                        c = chunk_at(Q_STEP, n - 2)
                        if c is not None:
                            pe.wait_ge(p_sum, query_job(L, c) + 1)
                        c = chunk_at(K_STEP, n - 2)
                        if c is not None and L < NL - 1:
                            pe.wait_ge(p_sum, key_job(L + 1, c) + 1)
                        for j in range(4):
                            mm = pe.transpose(bank[6][:, P * j:P * (j + 1)], OC[:, b % 2, P * j:P * (j + 1)], ID[:])
                        mm.then_inc(t_mm, 1)
                    b = due(n, NT_LAG)
                    if b is not None:
                        pe.wait_ge(max_done, units0 + b * 4 + 4)
                        if b >= 4:
                            pe.wait_ge(x_done, batches0 + b - 3)
                        pe.transpose(bank[7][0:NH, 0:P], NM[:, b % 2, :], ID[:]).then_inc(nt_done, 1)
                    b = due(n, OT_LAG)
                    if b is not None:
                        pe.wait_ge(on_done, batches0 + b + 1)
                        pe.wait_ge(nm_lo, batches0 + min(b + 4, NB))
                        if b >= 1:
                            pe.wait_ge(x_done, batches0 + b)
                        pe.transpose(bank[7][:, P:2 * P], ON[:, b % 2, :], ID[:]).then_inc(ot_done, 1)
                    c = chunk_at(V_STEP, n)
                    if c is not None and L < NL - 1:
                        if c >= 2:
                            pe.wait_ge(v_out, NB * (L + 1) + BC * (c - 1))
                        values_of(L + 1, c, bank[5 + c % 2])
                    c = chunk_at(T_STEP, n)
                    if c is not None:
                        pe.wait_ge(on_done, batches0 + (n - T_LAG) // 4 + 1)
                        transposes(c, bank[6])
                    c = chunk_at(Q_STEP, n)
                    if c is not None:
                        pe.wait_ge(on_done, batches0 + (n - T_LAG) // 4 + 1)
                        queries(c, bank[6])
                    c = chunk_at(K_STEP, n)
                    if c is not None and L < NL - 1:
                        pe.wait_ge(on_done, batches0 + (n - T_LAG) // 4 + 1)
                        keys(L + 1, c, bank[6])

            def experts():
                norm_transposes(1, XN)
                pe.wait_ge(moe_lo, 2 * NE + 1)
                pe.wait_ge(xt_lo[1], NC)
                for b in range(NB):
                    mm = product3(bank[0][:, 8 * b:8 * b + 8], XTH[:, b, :], XTL[:, b, :], GWH[:], GWL[:])
                mm.then_inc(gl_mm, 1)
                pe.wait_ge(w9_ready, 1)
                for c in range(NC):
                    if c >= 2:
                        pe.wait_ge(w9t_cp, c - 1)
                    for b in range(BC):
                        mm = pe.transpose(bank[6 + c % 2][0:NE, P * b:P * (b + 1)], W9[:, BC * c + b, :], ID[:])
                    mm.then_inc(w9t_mm, 1)
                    pe.wait_ge(w9t_cp, c + 1)
                    if c >= 2:
                        pe.wait_ge(acc_init, c - 1)
                    for b in range(BC):
                        mm = pe.matmul(bank[4 + c % 2][:, P * b:P * (b + 1)],
                                       W9T[0:NE, CT * (c % 2) + P * b:CT * (c % 2) + P * (b + 1)], DB[:],
                                       start=True, stop=True)
                    mm.then_inc(bias_mm, 1)

                def up(e, n, c):
                    for i in range(NI):
                        if live(1, n, 99):
                            pe.wait_ge(gelu_done, n * 4 + (i - 3))
                        w = slice(P * i, P * (i + 1))
                        product3(bank[i][:], UPH[:, e, w], UPL[:, e, w],
                                 XTH[:, BC * c:BC * (c + 1), :], XTL[:, BC * c:BC * (c + 1), :]).then_inc(up_mm, 1)

                def down(e, n, c):
                    pe.wait_ge(split_done, n * 4 + 4)
                    pe.wait_ge(acc_init, NC)
                    if live(2, n, 99):
                        pe.wait_ge(comb_done, n - 1)
                    s = c % 2
                    for t in range(BC):
                        tok = slice(P * t, P * (t + 1))
                        for i in range(NI):
                            w = slice(P * i, P * (i + 1))
                            mm = product3(bank[4 + s][:, tok], GH[:, s, i, tok], GL[:, s, i, tok],
                                          DNH[:, e, w], DNL[:, e, w], start=i == 0, stop=i == NI - 1)
                    mm.then_inc(dn_mm, 1)

                def turn(e, n0, last):
                    for c in range(NC):
                        if c < NC - 1:
                            up(e, n0 + (c + 1), c + 1)
                        elif not last:
                            up(e + 1, n0 + NC, 0)
                        down(e, n0 + c, c)

                up(0, 0, 0)
                turn(0, 0, False)
                with pe.Fori(1, NE - 1) as e:
                    turn(e, e * 4, False)
                turn(NE - 1, 4 * (NE - 1), True)

            def quantised_mlp():
                norm_transposes(8, XN2)
                pe.wait_ge(fc_ready, 2)
                for c in range(NC):
                    pe.wait_ge(xt_lo[8], c + 1)
                    for i in range(NI):
                        if c >= 1:
                            pe.wait_ge(silu_done, 4 * (c - 1) + i + 1)
                        w = FC1[:, P * i:P * (i + 1)]
                        pe.matmul(bank[i][:], w, XTH[:, BC * c:BC * (c + 1), :], start=True, stop=False)
                        pe.matmul(bank[i][:], w, XTL[:, BC * c:BC * (c + 1), :], start=False, stop=True
                                  ).then_inc(f1_mm, 1)
                    if c >= 1:
                        second(c - 1)
                second(NC - 1)
                pe.wait_ge(l2_deq, 1)
                for m in range(9):
                    if m >= 8:
                        pe.wait_ge(l2_cp, 1)
                    mm = pe.transpose(bank[6 + m // 4 % 2][:, P * (m % 4):P * (m % 4 + 1)],
                                      L2RAW[:, P * m:P * (m + 1)], ID[:])
                    if m % 4 == 3 or m == 8:
                        mm.then_inc(l2_tr, 1)

            def second(c):
                pe.wait_ge(silu_done, 4 * (c + 1))
                if c >= 2:
                    pe.wait_ge(f2_out, 4 * (c - 1))
                for t in range(BC):
                    for i in range(NI):
                        mm = pe.matmul(bank[4 + c % 2][:, P * t:P * (t + 1)], G[:, c % 2, i, P * t:P * (t + 1)],
                                       FC2[:, i, :], start=i == 0, stop=i == NI - 1)
                mm.then_inc(f2_mm, 1)

            def fixed_point_mlp():
                norm_transposes(5, XN)
                n = 0
                for m in range(6):
                    for c in range(NC):
                        pe.wait_ge(xt_lo[5], c + 1)
                        if n >= 4:
                            pe.wait_ge(gu_cp, n - 3)
                        pe.matmul(bank[n % 4][:], WL2T[:, m, :], XT32[:, CT * c:CT * (c + 1)], start=True, stop=True
                                  ).then_inc(gu_mm, 1)
                        n += 1
                for b in range(NB):
                    pe.wait_ge(o_q, b // BC + 1)
                    if b >= 2:
                        pe.wait_ge(d_out, b - 1)
                    for i in range(3):
                        mm = pe.matmul(bank[4 + b % 2][:, 0:P], GT[:, i, P * b:P * (b + 1)], WL2T[:, 6 + i, :],
                                       start=i == 0, stop=i == 2)
                    mm.then_inc(d_mm, 1)

            def int8_product():
                pe.wait_ge(r_q, 1)
                pe.transpose(bank[0][:].bitcast(F16)[:, 0:P], RQH, IDH[:]).then_inc(r_mm, 1)
                pe.matmul(bank[1][:, 0:P], SCAL[:, 20:21].to_broadcast((P, P)), ID[:], start=True, stop=True
                          ).then_inc(r_mm, 1)
                for c in range(NC):
                    pe.wait_ge(xn_ready[7], NB + c + 1)
                    if c >= 2:
                        pe.wait_ge(xt_hi[7], c - 1)
                    for b in range(BC):
                        mm = pe.transpose(bank[6 + c % 2][:].bitcast(F16)[:, P * b:P * (b + 1)], XQH[:, BC * c + b, :], IDH[:])
                    mm.then_inc(xt_mm[7], 1)
                pe.wait_ge(r_cp, 2)
                for b in range(NB):
                    pe.wait_ge(xt_hi[7], b // BC + 1)
                    if b >= 2:
                        pe.wait_ge(z_out, b - 1)
                    pe.matmul(bank[4 + b % 2][:, 0:P], XQT[:, b, :], RQT, start=True, stop=True).then_inc(z_mm, 1)

            attention(0)
            experts()
            attention(1)
            quantised_mlp()
            attention(2)
            fixed_point_mlp()
            attention(3)
            int8_product()

        @block.scalar
        def _(act):
            act.wait_ge(scales, 1)
            for c in range(NC):
                act.activation(CTH[:, BC * c:BC * (c + 1), :].rearrange("p b t -> p (b t)"), CRAW[:, CT * c:CT * (c + 1)],
                               ACT.Identity, scale=SC[:, A_CTX:A_CTX + 1]).then_inc(ctx_hi, 1)
            for m in range(9):
                mats = slice(m, m + 1) if m < 8 else slice(8, 12)
                act.activation(WAH[:, mats, :], WRAW[:, mats, :], ACT.Identity, scale=SC[:, m:m + 1]).then_inc(w_hi, 1)
            act.wait_ge(ld_small, 48)
            act.activation(TG[:], ROWS[:, R_GATES:R_GATES + 8], ACT.Tanh).then_inc(tanh_done, 1)
            def projected(job, of, bias, scale):
                act.wait_ge(p_mm, job + 1)
                if job >= 2:
                    act.wait_ge(p_lo, job - 1)
                    act.wait_ge(p_put[job % 2], 48 * (job // 2))
                for dst in (PJH, PJ):
                    ins = act.activation(dst[:, job % 2, :], of[:], ACT.Identity, bias=bias, scale=scale)
                ins.then_inc(p_sum, 1)

            def keys(L, c, of):
                projected(key_job(L, c), of, COLS[:, C_BK + L:C_BK + L + 1], DK_[:, L:L + 1])

            def expert_weights(m):
                if m == 0:
                    act.wait_ge(scales, 2)
                    act.activation(GWH[:], COLS[:, C_GW:C_GW + 8], ACT.Identity, scale=SC[:, A_GW:A_GW + 1]
                                   ).then_inc(moe_hi, 1)
                    return
                e, down = divmod(m - 1, 2)
                dst, src, at = ((UPH, UPRAW, A_UP), (DNH, DNRAW, A_DN))[down]
                act.activation(dst[:, e, :], src[:, e, :], ACT.Identity, scale=SC[:, at + e:at + e + 1]).then_inc(moe_hi, 1)

            for c in range(NC):
                keys(0, c, bank[c])

            def norm_hi(i):
                for c in range(NC):
                    act.wait_ge(xt_mm[i], c + 1)
                    act.copy(XTH[:, BC * c:BC * (c + 1), :].rearrange("p b t -> p (b t)"), bank[6 + c % 2][:]
                             ).then_inc(xt_hi[i], 1)

            def attention(L):
                units0, batches0, chunks0 = earlier(L)
                def hi_part(c, of):
                    act.wait_ge(xt_mm[2 * L], c + 1)
                    act.copy(XTH[:, BC * c:BC * (c + 1), :].rearrange("p b t -> p (b t)"), of[:]).then_inc(xt_hi[2 * L], 1)

                def query_sums(c, of):
                    projected(query_job(L, c), of, COLS[:, C_BQ + L:C_BQ + L + 1], DS[:, A_Q + L:A_Q + L + 1])

                for c in range(2):
                    hi_part(c, bank[6 + c])
                for c in range(2):
                    query_sums(c, bank[4 + c])

                for n in range(STEPS):
                    b = due(n, L_LAG)
                    if b is not None:
                        act.wait_ge(nt_done, batches0 + b + 1)
                        if b >= 2:
                            act.wait_ge(st_done, units0 + 4 * (b - 1))
                        act.activation(NHL[0:NH, b % 2, :], bank[7][0:NH, 0:P], ACT.Copy, scale=1.0 / BIG
                                       ).then_inc(nm_hi, 1)
                    b = due(n, OT_LAG + 1)
                    if b is not None:
                        act.wait_ge(ot_done, batches0 + b + 1)
                        if b >= 2:
                            act.wait_ge(y_done, batches0 + b - 1)
                        act.copy(OT[:, b % 2, :], bank[7][:, P:2 * P]).then_inc(ot_cp, 1)
                    c = chunk_at(T_STEP, n - 1)
                    if c is not None:
                        hi_part(c, bank[6])
                    c = chunk_at(Q_STEP, n - 1)
                    if c is not None:
                        query_sums(c, bank[6])
                    c = chunk_at(K_STEP, n - 1)
                    if c is not None and L < NL - 1:
                        keys(L + 1, c, bank[6])
                    if L == 0 and 20 <= n < 20 + 2 * (2 * NE + 1) and n % 2 == 0:
                        expert_weights((n - 20) // 2)
                    m = n - ST_LAG
                    if 0 <= m < UNITS:
                        act.wait_ge(st_done, units0 + m + 1)
                        if m >= 4:
                            act.wait_ge(pv_done, units0 + m - 3)
                        act.activation(PR[:, m % 4, :], bank[2 + m % 2][:], ACT.Exp, scale=float(DK) ** -0.5
                                       ).then_inc(exp_done, 1)
                    b = due(n, OC_LAG)
                    if b is not None:
                        act.wait_ge(pv_done, units0 + b * 4 + 4)
                        if b >= 2:
                            act.wait_ge(t_mm, batches0 + b - 1)
                        act.copy(OC[:, b % 2, :], bank[4 + b % 2][:]).then_inc(oc_cp, 1)

            def experts():
                norm_hi(1)
                act.wait_ge(lg_ready, 1)
                act.activation(SIG[:], LG[:], ACT.Sigmoid).then_inc(sig_done, 1)
                for c in range(NC):
                    act.wait_ge(w9t_mm, c + 1)
                    if c >= 2:
                        act.wait_ge(bias_mm, c - 1)
                    act.copy(W9T[0:NE, CT * (c % 2):CT * (c % 2 + 1)], bank[6 + c % 2][0:NE, :]).then_inc(w9t_cp, 1)

                def turn(e, n0, slot):
                    act.copy(EXPERT[:, slot, :], EXPERTS[:, e, :]).then_inc(expert_cp, 1)
                    act.wait_ge(expert_cp, e + 1)
                    for c in range(NC):
                        n = n0 + c
                        for i in range(NI + 1):
                            if i < NI:
                                act.wait_ge(up_mm, n * 4 + (i + 1))
                                if live(2, n, 99):
                                    act.wait_ge(split_done, n * 4 + (i - 7))
                                act.activation(G[:, c % 2, i, :], bank[i][:], ACT.Gelu, bias=EXPERT[:, slot, i:i + 1],
                                               scale=EXPERT[:, slot, NI:NI + 1]).then_inc(gelu_done, 1)
                            if i > 0:
                                act.wait_ge(gelu_done, n * 4 + i)
                                if live(2, n, 99):
                                    act.wait_ge(dn_mm, n - 1)
                                act.activation(GH[:, c % 2, i - 1, :], G[:, c % 2, i - 1, :], ACT.Identity,
                                               scale=EXPERT[:, slot, NI + 1:NI + 2]).then_inc(gh_done, 1)

                turn(0, 0, 0)
                with act.Fori(0, NE // 2) as pair:
                    for slot in (1, 0):
                        e = 2 * pair + (2 - slot)
                        turn(e, e * 4, slot)

            def quantised_mlp():
                for c in range(NC):
                    act.wait_ge(xt_mm[8], c + 1)
                    if c >= 2:
                        act.wait_ge(xt_lo[8], c - 1)
                    act.activation(H32[:, c % 2, :], bank[6 + c % 2][:], ACT.Identity, bias=COLS[:, C_BETA:C_BETA + 1],
                                   scale=COLS[:, C_GAMMA:C_GAMMA + 1]).then_inc(h_sum, 1)
                for c in range(NC):
                    for i in range(NI):
                        act.wait_ge(f1_mm, 4 * c + i + 1)
                        if c >= 2:
                            act.wait_ge(f2_mm, c - 1)
                        act.activation(G[:, c % 2, i, :], bank[i][:], ACT.Silu, bias=COLS[:, C_B1 + i:C_B1 + i + 1],
                                       scale=COLS[:, C_S1 + i:C_S1 + i + 1]).then_inc(silu_done, 1)
                for i in range(3):
                    act.wait_ge(l2_tr, i + 1)
                    m = 4 * i
                    n = 4 if i < 2 else 1
                    act.copy(WL2T[:, m:m + n, :].rearrange("p m o -> p (m o)"), bank[6 + i % 2][:, 0:P * n]
                             ).then_inc(l2_cp, 1)

            def fixed_point_mlp():
                for c in range(NC):
                    act.wait_ge(xt_mm[5], c + 1)
                    act.copy(XT32[:, CT * c:CT * (c + 1)], bank[6 + c % 2][:]).then_inc(xt_lo[5], 1)
                for m in range(6):
                    dst = GT if m < 3 else UT
                    for c in range(NC):
                        n = 4 * m + c
                        act.wait_ge(gu_mm, n + 1)
                        act.copy(dst[:, m % 3, CT * c:CT * (c + 1)], bank[n % 4][:]).then_inc(gu_cp, 1)
                for o in range(3):
                    act.wait_ge(gate_r, o + 1)
                    act.activation(TT[o], GT[:, o, :], ACT.Sigmoid, scale=SCALE[:, 1:2]).then_inc(sig2, 1)

            def int8_product():
                act.wait_ge(r_mm, 1)
                act.copy(RQT, bank[0][:].bitcast(F16)[:, 0:P]).then_inc(r_cp, 1)
                for c in range(NC):
                    act.wait_ge(xt_mm[7], c + 1)
                    act.copy(XQT[:, BC * c:BC * (c + 1), :].rearrange("p b t -> p (b t)"), bank[6 + c % 2][:].bitcast(F16)[:, 0:CT]
                             ).then_inc(xt_hi[7], 1)

            attention(0)
            experts()
            attention(1)
            quantised_mlp()
            attention(2)
            fixed_point_mlp()
            attention(3)
            int8_product()

        @block.vector
        def _(dve):
            order = SelfOrder(dve, dve_self)

            def power_scales(lo, hi):
                p2 = SMALL[:, 0:hi - lo]
                order(dve.tensor_scalar(p2.bitcast(I32), AMR[:, lo:hi].bitcast(I32), 0x7F800000, None, ALU.bitwise_and))
                order(dve.tensor_scalar(p2, p2, 2.0 ** -100, None, ALU.max))
                order(dve.tensor_scalar(DS[:, lo:hi], p2, 2.0 ** -14, None, ALU.mult))
                order(dve.reciprocal(p2, p2))
                order(dve.tensor_scalar(SC[:, lo:hi], p2, 2.0 ** 14, None, ALU.mult))

            def flat(ap):
                return ap.rearrange("p b t -> p (b t)")

            dve.wait_ge(ld_w, 16)
            dve.tensor_reduce(AM[:, 0:8], WRAW[:, 0:8, :], AX.X, ALU.max, apply_absolute_value=True)
            dve.tensor_reduce(AM[:, A_V:A_V + 1], WRAW[:, 8:12, :], AX.XY, ALU.max, apply_absolute_value=True)
            dve.wait_ge(ld_ctx, 16)
            dve.tensor_reduce(AM[:, A_CTX:A_CTX + 1], CRAW, AX.X, ALU.max, apply_absolute_value=True).then_inc(am_local, 1)
            dve.wait_ge(am_all, 1)
            power_scales(0, A_UP)
            order(dve.tensor_scalar(DK_[:, 0:4], DS[:, A_K:A_K + 4], DS[:, A_CTX:A_CTX + 1], None, ALU.mult))
            dve.tensor_scalar(DK_[:, 4:5], DS[:, A_V:A_V + 1], DS[:, A_CTX:A_CTX + 1], None, ALU.mult).then_inc(scales, 1)
            for c in range(NC):
                dve.wait_ge(ctx_hi, c + 1)
                low(dve, flat(CTL[:, BC * c:BC * (c + 1), :]), CRAW[:, CT * c:CT * (c + 1)], SC[:, A_CTX:A_CTX + 1],
                    flat(CTH[:, BC * c:BC * (c + 1), :])).then_inc(ctx_lo, 1)
            for m in range(9):
                mats = slice(m, m + 1) if m < 8 else slice(8, 12)
                dve.wait_ge(w_hi, m + 1)
                low(dve, flat(WAL[:, mats, :]), flat(WRAW[:, mats, :]), SC[:, m:m + 1], flat(WAH[:, mats, :])).then_inc(w_lo, 1)
            def projection_lo(job):
                dve.wait_ge(p_sum, job + 1)
                dve.tensor_tensor(PJL[:, job % 2, :], PJ[:, job % 2, :], PJH[:, job % 2, :], ALU.subtract).then_inc(p_lo, 1)

            def values_out(L, c, of):
                dve.wait_ge(v_mm, NC * L + c + 1)
                for i in range(BC):
                    dve.scalar_tensor_tensor(out=VA[:, BC * c + i, NH * L:NH * (L + 1), 0:DK],
                                             in0=of[:, P * i:P * (i + 1)].rearrange("p (h d) -> p h d", d=DK),
                                             scalar=DK_[:, 4:5],
                                             in1=ROWS[:, R_BV + P * L:R_BV + P * (L + 1)].rearrange("p (h d) -> p h d", d=DK),
                                             op0=ALU.mult, op1=ALU.add).then_inc(v_out, 1)

            def masks():
                dve.wait_ge(ld_mask, 32)
                dve.tensor_scalar(MKH[:, 0, :], MKI[:], 0.0, -BIG, ALU.is_equal, ALU.mult).then_inc(mask_ready, 1)
                dve.tensor_scalar(MKH[:, 1, :], MK8, 0.0, -BIG, ALU.is_equal, ALU.mult).then_inc(mask_ready, 1)

            def expert_magnitudes(part):
                at, src = ((A_UP, UPRAW), (A_DN, DNRAW))[part % 2]
                e = part // 2 * 3
                dve.wait_ge(ld_moe, 32)
                dve.tensor_reduce(AM[:, at + e:at + e + 3], src[:, e:e + 3, :], AX.X, ALU.max, apply_absolute_value=True)
                if part == 5:
                    dve.tensor_reduce(AM[:, A_GW:A_GW + 1], COLS[:, C_GW:C_GW + 8], AX.X, ALU.max, apply_absolute_value=True)
                    dve.tensor_reduce(AM[:, A_UB:A_UB + NE], COLS[:, C_UB:C_UB + 36].rearrange("p (e i) -> p e i", e=NE),
                                            AX.X, ALU.max, apply_absolute_value=True).then_inc(am_local, 1)

            def expert_scales():
                dve.wait_ge(am_all, 2)
                power_scales(A_UP, A_N)
                order(dve.tensor_copy(EXPERTS[:, :, 0:NI], COLS[:, C_UB:C_UB + 36].rearrange("p (e i) -> p e i", e=NE)))
                order(dve.tensor_copy(EXPERTS[:, :, NI], DS[:, A_UP:A_UP + NE]))
                b = SMALL[:, 0:NE]
                order(dve.scalar_tensor_tensor(out=b, in0=AMR[:, A_UP:A_UP + NE], scalar=float(P),
                                               in1=AMR[:, A_UB:A_UB + NE], op0=ALU.mult, op1=ALU.add))
                order(dve.tensor_scalar(b.bitcast(I32), b.bitcast(I32), 0x7F800000, None, ALU.bitwise_and))
                order(dve.tensor_scalar(b, b, 2.0 ** -100, None, ALU.max))
                order(dve.tensor_scalar(HS[:, 1, :], b, 2.0 ** -14, None, ALU.mult))
                order(dve.reciprocal(b, b))
                order(dve.tensor_scalar(EXPERTS[:, :, NI + 1], b, 2.0 ** 14, None, ALU.mult))
                dve.tensor_scalar(HS[:, 0, :], b, 2.0 ** 14, None, ALU.mult).then_inc(scales, 1)

            def stats(src, mv, batches):
                for b in batches:
                    ins = dve.bn_stats(ST6[:, b, :], src[:, b, :])
                order(ins)
                for b in batches:
                    ins = dve.bn_aggr(mv[:, b, :], ST6[:, b, :])
                return ins

            def inverse_root(mv):
                v, y, t = SMALL[:, 0:NB], RSTD[:], SMALL[:, 32:32 + NB]
                order(dve.tensor_scalar(v, mv[:, :, 1], EPS, None, ALU.add))
                order(dve.tensor_scalar(y.bitcast(I32), v.bitcast(I32), 1, None, ALU.logical_shift_right))
                order(dve.tensor_scalar(y.bitcast(I32), y.bitcast(I32), -1.0, float(0x5F3759DF), ALU.mult, ALU.add))
                for _ in range(3):
                    order(dve.tensor_tensor(t, y, y, ALU.mult))
                    order(dve.scalar_tensor_tensor(out=t, in0=t, scalar=-0.5, in1=v, op0=ALU.mult, op1=ALU.mult))
                    order(dve.scalar_tensor_tensor(out=y, in0=t, scalar=1.5, in1=y, op0=ALU.add, op1=ALU.mult))

            def normalise(dst, src, mv, ready):
                for b in range(NB):
                    dve.tensor_scalar(dst[:, b, :], src[:, b, :], mv[:, b, 0:1], RSTD[:, b:b + 1],
                                      ALU.subtract, ALU.mult).then_inc(ready, 1)

            def norm_lo(i):
                for c in range(NC):
                    dve.wait_ge(xt_hi[i], c + 1)
                    dve.tensor_tensor(flat(XTL[:, BC * c:BC * (c + 1), :]), bank[6 + c % 2][:],
                                      flat(XTH[:, BC * c:BC * (c + 1), :]), ALU.subtract).then_inc(xt_lo[i], 1)

            def attention(L):
                units0, batches0, chunks0 = earlier(L)
                inverse_root(MV)
                if L == 2:
                    dve.wait_ge(fc_ready, 2)
                    keep = SMALL[:, 64:64 + NB]
                    order(dve.tensor_reduce(keep, MB, AX.X, ALU.max))
                    order(dve.tensor_scalar(keep, keep, 0.0, None, ALU.is_equal))
                    order(dve.tensor_tensor(RSTD[:], RSTD[:], keep, ALU.mult))

                def normed(b):
                    c, i = divmod(b, BC)
                    if c >= 2:
                        dve.wait_ge(xt_mm[2 * L], c - 1)
                    dve.tensor_scalar(XNC[L][:, c % 2, i, :], X[:, b, :], MV[:, b, 0:1], RSTD[:, b:b + 1], ALU.subtract, ALU.mult
                                      ).then_inc(xn_ready[2 * L], 1)

                def lo_part(c, of):
                    dve.wait_ge(xt_hi[2 * L], c + 1)
                    dve.tensor_tensor(flat(XTL[:, BC * c:BC * (c + 1), :]), of[:], flat(XTH[:, BC * c:BC * (c + 1), :]),
                                      ALU.subtract).then_inc(xt_lo[2 * L], 1)

                def query_lo(c):
                    projection_lo(query_job(L, c))

                for b in range(2 * BC):
                    normed(b)
                for c in range(2):
                    lo_part(c, bank[6 + c])
                for c in range(2):
                    query_lo(c)
                if L == 0:
                    dve.wait_ge(v_ones, 1)
                    dve.wait_ge(ld_small, 48)
                    for c in range(NC):
                        values_out(0, c, bank[c])
                if L == 0:
                    masks()
                    for part in range(6):
                        expert_magnitudes(part)

                heads = bank[6][:].rearrange("p (h d) -> p h d", d=32)
                for n in range(STEPS):
                    b = due(n, L_LAG)
                    if b is not None:
                        dve.wait_ge(nm_hi, batches0 + b + 1)
                        low(dve, NHL[LO_AT:LO_AT + NH, b % 2, :], bank[7][0:NH, 0:P], 1.0 / BIG, NHL[0:NH, b % 2, :]).then_inc(nm_lo, 1)
                    b = due(n, STAT_LAG)
                    if b is not None:
                        dve.wait_ge(x_done, batches0 + b + 1)
                        dve.bn_stats(ST6[:, b, :], X[:, b, :]).then_inc(st6_done, 1)
                    b = due(n, X_LAG)
                    if b is not None:
                        dve.wait_ge(y_done, batches0 + b + 1)
                        if L < 2:
                            dve.wait_ge(xb_done, NC * L + b // BC + 1)
                        dve.scalar_tensor_tensor(out=X[:, b, :], in0=bank[7][:, 2 * P:3 * P], scalar=TG[:, L:L + 1],
                                                 in1=X[:, b, :], op0=ALU.mult, op1=ALU.add).then_inc(x_done, 1)
                    if n < UNITS:
                        b, j = divmod(n, 4)
                        dve.wait_ge(s_done, units0 + n + 1)
                        if j == 0 and b >= 2:
                            dve.wait_ge(nt_done, batches0 + b - 1)
                        dve.tensor_reduce(NM[:, b % 2, 4 * j:4 * j + 4], bank[n % 2][:].rearrange("p (g t) -> p g t", g=NG),
                                          AX.X, ALU.max, negate=True).then_inc(max_done, 1)
                    b = due(n, STAT_LAG)
                    if b is not None:
                        dve.wait_ge(st6_done, batches0 + b + 1)
                        dve.bn_aggr(MV[:, b, :], ST6[:, b, :]).then_inc(mv_done, 1)
                    c = chunk_at(V_STEP, n - 1)
                    if c is not None and L < NL - 1:
                        values_out(L + 1, c, bank[5 + c % 2])
                    if L == 0 and n == 16:
                        expert_scales()
                    if L == 0 and n == 24:
                        dve.wait_ge(moe_hi, 1)
                        low(dve, GWL[:], COLS[:, C_GW:C_GW + 8], SC[:, A_GW:A_GW + 1], GWH[:]).then_inc(moe_lo, 1)
                    for c, at in T_STEP.items():
                        if 0 <= at - 1 - n < BC:
                            normed(BC * c + at - 1 - n)
                    c = chunk_at(T_STEP, n - 1)
                    if c is not None:
                        lo_part(c, bank[6])
                    c = chunk_at(Q_STEP, n - 1)
                    if c is not None:
                        query_lo(c)
                    c = chunk_at(K_STEP, n - 1)
                    if c is not None and L < NL - 1:
                        projection_lo(key_job(L + 1, c))
                    b = due(n, REC_LAG)
                    if b is not None:
                        dve.wait_ge(t_mm, batches0 + b + 1)
                        dve.reciprocal(REC[:, b % 2, :], heads[:, :, DK]).then_inc(rec_done, 1)
                    b = due(n, ON_LAG)
                    if b is not None:
                        dve.wait_ge(rec_done, batches0 + b + 1)
                        if b >= 2:
                            dve.wait_ge(ot_done, batches0 + b - 1)
                        dve.tensor_tensor(ON[:, b % 2, :].rearrange("p (h d) -> p h d", d=DK), heads[:, :, 0:DK],
                                          REC[:, b % 2, :].rearrange("p (h o) -> p h o", o=1).to_broadcast((P, NH, DK)),
                                          ALU.mult).then_inc(on_done, 1)
                dve.wait_ge(mv_done, batches0 + NB)

            def experts():
                inverse_root(MV)
                normalise(XN, X, MV, xn_ready[1])
                norm_lo(1)
                def each(ap, n=8):
                    return ap.rearrange("p (b o) -> p b o", o=1).to_broadcast((P, NB, n))

                lg, key, sel, m = (SMALL[:, 0:0 + 128], SMALL[:, 128:256], W9[:], SMALL[:, 256:256 + NB])
                lg, key = (v.rearrange("p (b e) -> p b e", e=8) for v in (lg, key))
                sel = W9[:, :, 0:8]
                prio = ROWS[:, R_PRIO:R_PRIO + 8].rearrange("p (o e) -> p o e", o=1).to_broadcast((P, NB, 8))
                bias = ROWS[:, R_GBIAS:R_GBIAS + 8].rearrange("p (o e) -> p o e", o=1).to_broadcast((P, NB, 8))
                dve.wait_ge(gl_mm, 1)
                order(dve.tensor_scalar(LG[:], bank[0][:, 0:128].rearrange("p (b e) -> p b e", e=8),
                                        DS[:, A_GW:A_GW + 1], None, ALU.mult))
                dve.tensor_tensor(LG[:], LG[:], bias, ALU.add).then_inc(lg_ready, 1)
                dve.wait_ge(lg_ready, 1)
                order(dve.tensor_scalar(lg, LG[:], 16.6, -88.0, ALU.min, ALU.max))
                order(dve.memset(W9[:], 0.0))
                for _ in range(2):
                    order(dve.tensor_reduce(m, lg, AX.X, ALU.max))
                    order(dve.tensor_tensor(key, lg, each(m), ALU.is_equal))
                    order(dve.tensor_tensor(key, key, prio, ALU.mult))
                    order(dve.tensor_reduce(m, key, AX.X, ALU.max))
                    order(dve.tensor_tensor(key, key, each(m), ALU.is_equal))
                    order(dve.tensor_tensor(sel, sel, key, ALU.add))
                    order(dve.scalar_tensor_tensor(out=SMALL[:, 0:128], in0=SMALL[:, 128:256], scalar=-1e4,
                                                   in1=SMALL[:, 0:128], op0=ALU.mult, op1=ALU.add))
                dve.wait_ge(sig_done, 1)
                order(dve.tensor_tensor(sel, sel, SIG[:], ALU.mult))
                order(dve.tensor_reduce(m, sel, AX.X, ALU.add))
                order(dve.tensor_scalar(m, m, 1e-6, None, ALU.add))
                order(dve.reciprocal(m, m))
                order(dve.tensor_tensor(sel, sel, each(m), ALU.mult))
                order(dve.memset(W9[:, :, 8:9], 1.0))
                f = SMALL[:, 288:288 + NE]
                order(dve.tensor_tensor(f, DS[:, A_DN:A_DN + NE], HS[:, 1, :], ALU.mult))
                order(dve.tensor_scalar(f, f, 0.1, None, ALU.mult))
                dve.tensor_tensor(WF[:], W9[:], f.rearrange("p (o e) -> p o e", o=1).to_broadcast((P, NB, NE)),
                                  ALU.mult).then_inc(w9_ready, 1)
                for c in range(NC):
                    dve.wait_ge(bias_mm, c + 1)
                    dve.tensor_scalar(flat(ACC[:, BC * c:BC * (c + 1), :]), bank[4 + c % 2][:], 0.1, None, ALU.mult
                                      ).then_inc(acc_init, 1)

                def split(e, n, c):
                    for i in range(NI):
                        dve.wait_ge(gh_done, n * 4 + (i + 1))
                        low(dve, GL[:, c % 2, i, :], G[:, c % 2, i, :], HS[:, 0, bass.ds(e, 1)], GH[:, c % 2, i, :]
                            ).then_inc(split_done, 1)

                def combine(e, n, c):
                    dve.wait_ge(dn_mm, n + 1)
                    dve.wait_ge(acc_init, NC)
                    if live(4, n, 99):
                        dve.wait_ge(comb_done, n - 3)
                    for t in range(BC):
                        b = BC * c + t
                        ins = dve.scalar_tensor_tensor(out=ACC[:, b, :], in0=bank[4 + c % 2][:, P * t:P * (t + 1)],
                                                       scalar=WF[:, b, bass.ds(e, 1)], in1=ACC[:, b, :],
                                                       op0=ALU.mult, op1=ALU.add)
                    ins.then_inc(comb_done, 1)

                def turn(e, n0, last):
                    for c in range(NC):
                        if c < NC - 1:
                            split(e, n0 + (c + 1), c + 1)
                        elif not last:
                            split(e + 1, n0 + NC, 0)
                        combine(e, n0 + c, c)

                split(0, 0, 0)
                turn(0, 0, False)
                with dve.Fori(1, NE - 1) as e:
                    turn(e, e * 4, False)
                turn(NE - 1, 4 * (NE - 1), True)
                dve.wait_ge(comb_done, NC * NE)
                order(dve.tensor_reduce(m, ACC[:], AX.X, ALU.max, apply_absolute_value=True))
                order(dve.tensor_scalar(m, m, 1e-6, None, ALU.add))
                order(dve.reciprocal(m, m))
                order(dve.tensor_scalar(m, m, TG[:, 4:5], None, ALU.mult))
                for c in range(NC):
                    for b in range(BC * c, BC * (c + 1)):
                        ins = dve.scalar_tensor_tensor(out=X[:, b, :], in0=ACC[:, b, :], scalar=SMALL[:, 256 + b:257 + b],
                                                       in1=X[:, b, :], op0=ALU.mult, op1=ALU.add)
                    order(ins)
                    order(stats(X, MV, range(BC * c, BC * (c + 1))))
                dve.memset(SCAL[:, 30:31], 0.0).then_inc(moe_done, 1)

            def quantised_mlp():
                dve.wait_ge(ld_l2, 16)
                order(dve.tensor_reduce(BLK[:, 0], L2RAW.rearrange("p (k n) -> p k n", n=32), AX.X, ALU.max,
                                        apply_absolute_value=True))
                order(dve.tensor_scalar(BLK[:, 0], BLK[:, 0], 1.0 / 7.0, 1e-12, ALU.mult, ALU.max))
                dve.reciprocal(BLK[:, 1], BLK[:, 0]).then_inc(l2_inv, 1)
                inverse_root(MV)
                normalise(XN, X, MV, xn_ready[3])
                dve.wait_ge(xn_ready[3], NB)
                for c in range(NC):
                    order(stats(XN, MV2, range(BC * c, BC * (c + 1))))
                inverse_root(MV2)
                normalise(XN2, XN, MV2, xn_ready[8])
                order(dve.tensor_scalar(SCAL[:, 24:25], TG[:, 5:6], 0.5, None, ALU.mult))
                order(dve.scalar_tensor_tensor(out=flat(X[:]), in0=flat(XN[:]), scalar=TG[:, 5:6], in1=flat(X[:]),
                                               op0=ALU.mult, op1=ALU.add))
                order(dve.tensor_scalar(SMALL[:, 128:256], ROWS[:, R_B2:R_B2 + P], SCAL[:, 24:25], None, ALU.mult))
                order(dve.tensor_tensor(X[:], X[:],
                                        SMALL[:, 128:256].rearrange("p (o d) -> p o d", o=1).to_broadcast((P, NB, P)),
                                        ALU.add))
                for c in range(NC):
                    dve.wait_ge(h_sum, c + 1)
                    hi = flat(XTH[:, BC * c:BC * (c + 1), :])
                    order(dve.tensor_copy(hi, H32[:, c % 2, :]))
                    dve.tensor_tensor(flat(XTL[:, BC * c:BC * (c + 1), :]), H32[:, c % 2, :], hi, ALU.subtract
                                      ).then_inc(xt_lo[8], 1)
                for c in range(NC):
                    dve.wait_ge(f2_mm, c + 1)
                    for t in range(BC):
                        b = BC * c + t
                        ins = dve.scalar_tensor_tensor(out=X[:, b, :], in0=bank[4 + c % 2][:, P * t:P * (t + 1)],
                                                       scalar=SCAL[:, 24:25], in1=X[:, b, :], op0=ALU.mult, op1=ALU.add)
                        ins.then_inc(f2_out, 1)
                    dve.wait_ge(f2_out, BC * (c + 1))
                    order(stats(X, MV, range(BC * c, BC * (c + 1))))

            def fixed_point_mlp():

                def global_max(i, pieces, waits=None):
                    for n, piece in enumerate(pieces):
                        if waits is not None:
                            dve.wait_ge(gu_cp, waits + 4 * (n + 1))
                        order(dve.tensor_reduce(SCAL[:, 16 + n:17 + n], piece, AX.X, ALU.max, apply_absolute_value=True))
                    dve.tensor_reduce(SCAL[:, i:i + 1], SCAL[:, 16:16 + len(pieces)], AX.X, ALU.max).then_inc(gm_part, 1)

                def scale_of(i, unit=None):
                    dve.wait_ge(gm_all, i + 1)
                    top = SCAL[:, 8 + i:9 + i]
                    if unit is not None:
                        order(dve.tensor_tensor(top, top, unit, ALU.mult))
                    order(dve.tensor_scalar(SCALE[:, i:i + 1], top, 1.0 / 32767.0, 1e-12, ALU.mult, ALU.max))
                    ins = dve.reciprocal(SCALE[:, 8 + i:9 + i], SCALE[:, i:i + 1])
                    if unit is not None:
                        order(ins)
                        ins = dve.tensor_tensor(SCALE[:, 8 + i:9 + i], SCALE[:, 8 + i:9 + i], unit, ALU.mult)
                    return ins

                def shifted(ap, i):
                    return dve.tensor_scalar(ap, ap, SCALE[:, 8 + i:9 + i], ROUND, ALU.mult, ALU.add)

                inverse_root(MV)
                normalise(XN, X, MV, l2_norm)
                dve.wait_ge(l2_norm, NB)
                global_max(0, [flat(XN[:])])
                order(scale_of(0))
                for c in range(NC):
                    xc = flat(XN[:, BC * c:BC * (c + 1), :])
                    order(shifted(xc, 0))
                    dve.tensor_scalar(xc, xc, ROUND, SCALE[:, 0:1], ALU.subtract, ALU.mult).then_inc(xn_ready[5], BC)
                dve.wait_ge(gm_part, 1)
                global_max(1, [GT[:, o, :] for o in range(3)], waits=0)
                order(scale_of(1))
                for o in range(3):
                    order(shifted(GT[:, o, :], 1))
                    dve.tensor_scalar(GT[:, o, :], GT[:, o, :], ROUND, None, ALU.subtract).then_inc(gate_r, 1)
                global_max(2, [UT[:, o, :] for o in range(3)], waits=12)
                scale_of(2).then_inc(up_scale, 1)
                for o in range(3):
                    dve.wait_ge(sig2, o + 1)
                    order(dve.tensor_scalar(TT[o], TT[o], 65535.0 / 65536.0, 192.0, ALU.min, ALU.add))
                    order(dve.scalar_tensor_tensor(out=GT[:, o, :], in0=TT[o], scalar=-192.0, in1=GT[:, o, :],
                                                   op0=ALU.add, op1=ALU.mult))
                global_max(3, [GT[:, o, :] for o in range(3)])
                order(scale_of(3, SCALE[:, 1:2]))
                order(dve.tensor_tensor(SCALE[:, 16:17], SCALE[:, 3:4], SCALE[:, 2:3], ALU.mult))
                for o in range(3):
                    order(shifted(GT[:, o, :], 3))
                    dve.wait_ge(up_q, o + 1)
                    order(dve.scalar_tensor_tensor(out=GT[:, o, :], in0=GT[:, o, :], scalar=-ROUND, in1=UT[:, o, :],
                                                   op0=ALU.add, op1=ALU.mult))
                global_max(4, [GT[:, o, :] for o in range(3)])
                order(scale_of(4, SCALE[:, 16:17]))
                order(dve.tensor_tensor(SCALE[:, 17:18], SCALE[:, 4:5], TG[:, 6:7], ALU.mult))
                for c in range(NC):
                    gc = GT[:, :, CT * c:CT * (c + 1)]
                    order(shifted(gc, 4))
                    dve.tensor_scalar(gc, gc, ROUND, None, ALU.subtract).then_inc(o_q, 1)
                for c in range(NC):
                    for b in range(BC * c, BC * (c + 1)):
                        dve.wait_ge(d_mm, b + 1)
                        dve.scalar_tensor_tensor(out=X[:, b, :], in0=bank[4 + b % 2][:, 0:P], scalar=SCALE[:, 17:18],
                                                 in1=X[:, b, :], op0=ALU.mult, op1=ALU.add).then_inc(d_out, 1)
                    dve.wait_ge(d_out, BC * (c + 1))
                    order(stats(X, MV, range(BC * c, BC * (c + 1))))

            def int8_product():
                dve.wait_ge(ld_rhs, 16)
                order(dve.tensor_reduce(SCAL[:, 20:21], RT[:], AX.X, ALU.max, apply_absolute_value=True))
                order(dve.tensor_scalar(SCAL[:, 20:21], SCAL[:, 20:21], 1e-12, 1.0 / 127.0, ALU.max, ALU.mult))
                order(dve.reciprocal(SCAL[:, 21:22], SCAL[:, 20:21]))
                order(dve.tensor_scalar(RQ, RT[:], SCAL[:, 21:22], ROUND, ALU.mult, ALU.add))
                dve.tensor_scalar(RQH, RQ, ROUND, None, ALU.subtract).then_inc(r_q, 1)
                inverse_root(MV)
                normalise(XN, X, MV, xn_ready[7])
                dve.wait_ge(xn_ready[7], NB)
                ls, inv = SMALL[:, 64:64 + NB], SMALL[:, 96:96 + NB]
                order(dve.tensor_reduce(ls, XN[:], AX.X, ALU.max, apply_absolute_value=True))
                order(dve.tensor_scalar(ls, ls, 1e-12, 1.0 / 127.0, ALU.max, ALU.mult))
                order(dve.reciprocal(inv, ls))
                for c in range(NC):
                    for b in range(BC * c, BC * (c + 1)):
                        ins = dve.tensor_scalar(XN[:, b, :], XN[:, b, :], SMALL[:, 96 + b:97 + b], ROUND, ALU.mult, ALU.add)
                    order(ins)
                    dve.tensor_scalar(flat(XQH[:, BC * c:BC * (c + 1), :]), flat(XN[:, BC * c:BC * (c + 1), :]), ROUND,
                                      None, ALU.subtract).then_inc(xn_ready[7], 1)
                dve.wait_ge(r_mm, 2)
                dve.tensor_scalar(RSG, bank[1][:, 0:P], TG[:, 7:8], None, ALU.mult).then_inc(r_cp, 1)
                dve.wait_ge(r_cp, 2)
                for b in range(NB):
                    dve.wait_ge(z_mm, b + 1)
                    order(dve.scalar_tensor_tensor(out=ON[:, b % 2, :], in0=bank[4 + b % 2][:, 0:P],
                                                   scalar=SMALL[:, 64 + b:65 + b], in1=RSG, op0=ALU.mult, op1=ALU.mult))
                    dve.tensor_tensor(X[:, b, :], X[:, b, :], ON[:, b % 2, :], ALU.add).then_inc(z_out, 1)

            dve.wait_ge(ld_x, 16)
            for c in range(NC):
                order(stats(X, MV, range(BC * c, BC * (c + 1))))
            for c in range(NC):
                projection_lo(key_job(0, c))
            attention(0)
            experts()
            attention(1)
            quantised_mlp()
            attention(2)
            fixed_point_mlp()
            attention(3)
            int8_product()


def _laid_out(x):
    f = np.float32
    m = np.arange(P)
    perm = DK * (NG * (m % 4) + m // 32) + m // 4 % 8
    t = [True, False, True, True]

    def w(L, name):
        v = np.asarray(x[f"L{L}_xattn_W{name}"])
        return v.T if t[L] else v

    def b(L, name):
        return np.asarray(x[f"L{L}_xattn_b{name}"]) if L < 2 else np.zeros(P, f)

    def row(*parts):
        return np.concatenate([np.asarray(p).reshape(-1) for p in parts]).reshape(1, -1)

    qk = [w(L, n)[:, perm] for n in "qk" for L in range(NL)]
    v = [w(L, "v") for L in range(NL)]
    up = np.concatenate([x["L0_ffn_up_w"], x["L0_ffn_sw_up"][None]])
    dn = np.concatenate([x["L0_ffn_down_w"], x["L0_ffn_sw_down"][None]])
    ub = np.concatenate([x["L0_ffn_up_b"], x["L0_ffn_sb_up"][None]])
    cols = ([b(L, "q")[perm] for L in range(NL)] + [b(L, "k")[perm] for L in range(NL)]
            + list(ub.reshape(NE * NI, P)) + list(x["L1_ffn_fc1_scales"].reshape(NI, P))
            + list(x["L1_ffn_fc1_bias"].reshape(NI, P)) + [x["L1_ffn_ln_gamma"], x["L1_ffn_ln_beta"]]
            + list(np.asarray(x["L0_ffn_gate_w"]).T))
    const = {side: np.zeros((DK, NG * CT), np.float16) for side in "qk"}
    const["q"][0] = BIG
    select = np.zeros((LO_AT + NH, NH), np.float16)
    for h in range(NH):
        select[[h, LO_AT + h], h] = BIG
    return {
        "watt": np.stack(qk + v, 1),
        "ctx_t": x["ctx_1024"].transpose(2, 0, 1).reshape(P, NB * P),
        "x": x["x"].transpose(1, 0, 2),
        "cols": np.stack(cols, 1),
        "rows": row(x["g_xattn"], x["g_ffn"], x["L0_ffn_bias"], np.arange(8, 0, -1, dtype=f),
                    *[b(L, "v") for L in range(NL)], *[b(L, "o") for L in range(NL)],
                    x["L1_ffn_fc2_bias"], x["L1_ffn_fc2_scales"]),
        "down_b": np.concatenate([x["L0_ffn_down_b"], x["L0_ffn_sb_down"][None]]),
        "up_w": up.transpose(1, 0, 2),
        "down_w": dn.reshape(NE, NI, P, P).transpose(2, 0, 1, 3).reshape(P, NE, CT),
        "w_l2": np.concatenate([np.asarray(x[f"L2_ffn_w_{n}"]).reshape(3, P, P).transpose(1, 0, 2).reshape(P, 3 * P)
                                for n in ("gate", "up")] + [x["L2_ffn_w_down"]], 1),
        "wo": np.stack([w(L, "o").reshape(NG, 4, DK, P).transpose(1, 0, 2, 3).reshape(P, P) for L in range(NL)], 1),
        "rhs_t": x["L3_ffn_rhs"].T,
        "fc1_q": x["L1_ffn_fc1_q"],
        "fc2_q": x["L1_ffn_fc2_q"].reshape(NI, P, P).transpose(1, 0, 2).reshape(P, CT),
        "mask1": x["mask_BxS2_if1"],
        "mask2": x["mask_BxSxS2_if1"].transpose(1, 0, 2),
        "mask3": np.asarray(x["mask_BxS2_bk1"]).view(np.int32),
        "select": select,
        "q_const": const["q"],
        "k_const": const["k"],
    }


def kernel(**inputs):
    import concourse.bacc as bacc
    from concourse.bass_utils import run_bass_kernel_spmd

    nc = bacc.Bacc("TRN2", target_bir_lowering=False, num_devices=1)
    arrays = {k: np.ascontiguousarray(v) for k, v in _laid_out({k: np.asarray(v) for k, v in inputs.items()}).items()}
    aps = {k: nc.dram_tensor(f"{k}_in", v.shape, mybir.dt.from_np(v.dtype), kind="ExternalInput").ap()
           for k, v in arrays.items()}
    out = nc.dram_tensor("out", (NB, P, P), F32, kind="ExternalOutput").ap()
    flamingo(nc, aps, out)
    r = run_bass_kernel_spmd(nc, [{f"{k}_in": v for k, v in arrays.items()}], core_ids=[0])
    return r.results[0]["out"]
```

```python
from contextlib import ExitStack

import numpy as np

import concourse.bass as bass
from concourse import mybir

F32 = mybir.dt.float32
F16 = mybir.dt.float16
I32 = mybir.dt.int32
U8 = mybir.dt.uint8
ACT = mybir.ActivationFunctionType
ALU = mybir.AluOpType
AX = mybir.AxisListType
ABSMAX = bass.bass_isa.ReduceOp.absmax

P = 128
NB = 16
NL = 4
NH = 16
DK = 8
NC = 4
CT = 512
BC = NB // NC
NG = 4
NE = 9
NI = 4
BIG = 32768.0
MASK_ROW = 3
LO_AT = 32
ROUND = 12582912.0
EPS = 1e-5

R_GATES, R_GBIAS, R_PRIO, R_BV, R_BO = 0, 8, 16, 24, 536
R_B2, R_S2, R_N = 1048, 1176, 1688
C_BQ, C_BK, C_UB, C_S1, C_B1, C_GAMMA, C_BETA, C_GW, C_N = 0, 4, 8, 44, 48, 52, 53, 54, 62
A_Q, A_K, A_V, A_CTX, A_UP, A_DN, A_GW, A_UB, A_N = 0, 4, 8, 9, 10, 19, 28, 29, 38

UNITS = NB * 4
VA_N = NB * NL * NH * (DK + 1)
ST_LAG, PV_LAG = 8, 9
NT_LAG, L_LAG = 5, 6
OC_LAG, T_LAG, REC_LAG, ON_LAG, OT_LAG, Y_LAG, X_LAG, STAT_LAG = 13, 15, 15, 16, 18, 20, 21, 22
STEPS = 4 * (NB - 1) + STAT_LAG + 1
T_STEP = {2: 9, 3: 21}
Q_STEP = {2: 13, 3: 25}
V_STEP = {c: 5 + c for c in range(NC)}
K_STEP = {0: 17, 1: 29, 2: 37, 3: 41}
Q_PUT = {2: 6, 3: 9}
K_PUT = {0: 7, 1: 10, 2: 12, 3: 13}
EXPERT_STEPS = [4, 6, 8, 10, 22, 24]
NORM_STEPS = (51, 53, 55, 57, 59)
BLOCK_STEP = 40
ZEROED = (1, 2, 2, 3)


def query_job(L, c):
    return NC + 2 * NC * L + (c if c < 3 or L == NL - 1 else 4)


def key_job(L, c):
    return c if L == 0 else NC + 2 * NC * (L - 1) + (3, 5, 6, 7)[c]


def chunk_at(steps, n):
    return next((c for c, at in steps.items() if at == n), None)


def low(engine, dst, src, scale, hi):
    return engine.scalar_tensor_tensor(out=dst, in0=src, scalar=scale, in1=hi, op0=ALU.mult, op1=ALU.subtract)


def due(n, lag):
    b, off = divmod(n - lag, 4)
    return b if off == 0 and 0 <= b < NB else None


def at_least(n, lo):
    return n >= lo if isinstance(n, int) else True


def earlier(L):
    return UNITS * L, NB * L


class SelfOrder:

    def __init__(self, engine, sem):
        self.engine, self.sem, self.n = engine, sem, 0

    def __call__(self, ins):
        self.n += 1
        ins.then_inc(self.sem, 1)
        self.engine.wait_ge(self.sem, self.n)


def flamingo(nc, a, out):
    with ExitStack() as ctx:
        def sb(name, shape, dt=F32):
            return ctx.enter_context(nc.sbuf_tensor(name, shape, dt))

        def sem(name):
            return ctx.enter_context(nc.semaphore(name))

        def sems(name, n=NL):
            return [sem(f"{name}{i}") for i in range(n)]

        bank = [ctx.enter_context(nc.psum_tensor(f"bank{i}", [P, CT], F32)) for i in range(8)]

        X = sb("X", [P, NB, P])
        XT = sb("XT", [P, 2, NB, P], F16)
        XTH, XTL = XT[:, 0], XT[:, 1]
        XT32 = XT[:].rearrange("p s b t -> p (s b t)").bitcast(F32)
        CTH = sb("CTH", [P, NB, P], F16)
        CTL = sb("CTL", [P, NB, P], F16)
        WAH = sb("WAH", [P, 12, P], F16)
        WAL = sb("WAL", [P, 12, P], F16)
        WO = sb("WO", [P, NL, P])
        VAF = sb("VAF", [P, VA_N + 32])
        VA = VAF[:, 0:VA_N].rearrange("p (b h d) -> p b h d", b=NB, h=NL * NH)
        SK = sb("SK", [P, 4, CT], F16)
        SQ = sb("SQ", [P, 4, 4, CT], F16)
        XN = SQ[:].rearrange("p s j t -> p (s j t)").bitcast(F32)[:, 0:NB * P].rearrange("p (b d) -> p b d", b=NB)
        SEL = sb("SEL", [LO_AT + NH, NH], F16)
        PR = sb("PR", [P, 4, CT])
        ROWS = sb("ROWS", [P, R_N])
        COLS = sb("COLS", [P, C_N])
        DB = sb("DB", [NE, P])
        PJ = sb("PJ", [P, 2, CT])
        PJH = sb("PJH", [P, 2, CT], F16)
        PJL = sb("PJL", [P, 2, CT], F16)
        FC1 = sb("FC1", [P, CT], F16)
        FC2 = sb("FC2", [P, NI, P])
        ID = sb("ID", [P, P])
        IDH = sb("IDH", [P, P], F16)
        IDB = sb("IDB", [P, P], F16)
        MV = sb("MV", [P, NB, 2])
        ST6 = sb("ST6", [P, NB, 6])
        RSTD = sb("RSTD", [P, NB])
        NM = sb("NM", [P, 2, NH])
        NHL = sb("NHL", [LO_AT + NH, 2, P], F16)
        REC = sb("REC", [P, 2, NH])
        OC = sb("OC", [P, 2, CT])
        ON = sb("ON", [P, 2, P])
        OT = sb("OT", [P, 2, P])
        AM = sb("AM", [P, A_N])
        AMR = sb("AMR", [P, A_N])
        SC = sb("SC", [P, A_N])
        DS = sb("DS", [P, A_N])
        SMALL = sb("SMALL", [P, 320])
        GWH = sb("GWH", [P, 8], F16)
        GWL = sb("GWL", [P, 8], F16)
        LG = sb("LG", [P, NB, 8])
        SIG = sb("SIG", [P, NB, 8])
        W9 = sb("W9", [P, NB, NE])
        WF = sb("WF", [P, NB, NE])
        DK_ = sb("DK_", [P, 8])
        HS = sb("HS", [P, 2, NE])
        EXPERTS = sb("EXPERTS", [P, NE, NI + 2])
        EXPERT = sb("EXPERT", [P, 2, NI + 2])
        TG = sb("TG", [P, 8])
        SCAL = sb("SCAL", [P, 32])
        SCALE = sb("SCALE", [P, 20])
        ROUNDS = sb("ROUNDS", [P, 1])
        BLK = sb("BLK", [P, 2, 36])
        RT = sb("RT", [P, P])
        MV2 = sb("MV2", [P, NB, 2])
        MKH = sb("MKH", [NB, 2, P], F16)
        MK8W = sb("MK8", [NB, P // 4], I32)
        MK8 = MK8W[:].bitcast(U8)
        MKI = sb("MKI", [NB, P], I32)
        REGION = sb("REGION", [P, 19456])

        def region(at, n, dt=F32):
            v = REGION[:, at:at + n]
            return v if dt == F32 else v.bitcast(dt)

        UPH = region(0, 2304, F16).rearrange("p (e i) -> p e i", e=NE)
        UPL = region(2304, 2304, F16).rearrange("p (e i) -> p e i", e=NE)
        DNH = region(4608, 2304, F16).rearrange("p (e i) -> p e i", e=NE)
        DNL = region(6912, 2304, F16).rearrange("p (e i) -> p e i", e=NE)
        G = region(9216, 4096).rearrange("p (s i t) -> p s i t", s=2, i=NI)
        GH = region(13312, 2048, F16).rearrange("p (s i t) -> p s i t", s=2, i=NI)
        GL = region(15360, 2048, F16).rearrange("p (s i t) -> p s i t", s=2, i=NI)
        ACC = region(17408, 2048).rearrange("p (b h) -> p b h", b=NB)
        W9T = region(16384, 1024)
        UPRAW = region(9216, 4608).rearrange("p (e i) -> p e i", e=NE)
        DNRAW = region(13824, 4608).rearrange("p (e i) -> p e i", e=NE)
        FC1I = region(0, 512, I32)
        FC2I = region(512, 512, I32)
        MRAW = region(1024, 2048, I32).rearrange("p (b k) -> p b k", b=NB)
        XN1 = region(15488, 2048).rearrange("p (b h) -> p b h", b=NB)
        XN2 = region(4096, 2048).rearrange("p (b h) -> p b h", b=NB)
        H32 = region(3072, 1024).rearrange("p (s t) -> p s t", s=2)
        L2RAW = region(6144, 9 * P)
        MB = region(18432, 1024, F16).rearrange("p (b k) -> p b k", b=NB)
        GT = region(0, 6144).rearrange("p (o t) -> p o t", o=3)
        UT = region(6144, 6144).rearrange("p (o t) -> p o t", o=3)
        TT = (XT32, XN.rearrange("p b d -> p (b d)"), region(12288, 2048))
        WL2T = region(14336, 9 * P).rearrange("p (m o) -> p m o", m=9)
        XNC = [region(18432 if L == 0 else 17408, 2 * CT).rearrange("p (s i d) -> p s i d", s=2, i=BC) for L in range(NL)]
        RQ = region(128, 128)
        RQH = region(256, 64, F16)
        RQT = region(320, 64, F16)
        RSG = region(384, 128)
        XQH = region(1024, 1024, F16).rearrange("p (b h) -> p b h", b=NB)
        XQT = region(2048, 1024, F16).rearrange("p (b h) -> p b h", b=NB)
        WRAW = PR[:].rearrange("p s t -> p (s t)")[:, 0:12 * P].rearrange("p (m o) -> p m o", m=12)
        CRAW = VAF[:, 0:NB * P]

        kscr = nc.dram_tensor("kscr", (NL * NC, P, NG * CT), F16, kind="Internal").ap()
        qscr = nc.dram_tensor("qscr", (NC, P, NG * CT), F16, kind="Internal").ap()
        mscr = nc.dram_tensor("mscr", (2, NC, CT), F16, kind="Internal").ap()

        ld_w, ld_ctx, ld_x, ld_small, ld_wo, ld_l2 = (
            sem(n) for n in ("ld_w", "ld_ctx", "ld_x", "ld_small", "ld_wo", "ld_l2"))
        ld_moe = sems("ld_moe", 6)
        ld_mask, ld_fc, ld_rhs, ld_sel = sem("ld_mask"), sem("ld_fc"), sem("ld_rhs"), sem("ld_sel")
        scr_init, mask_put, mask_rows = sem("scr_init"), sem("mask_put"), sem("mask_rows")
        ident = sem("ident")
        am_local, am_all, scales = sem("am_local"), sem("am_all"), sem("scales")
        tanh_done = sem("tanh_done")
        ctx_hi, ctx_lo, w_hi, w_lo = sem("ctx_hi"), sem("ctx_lo"), sem("w_hi"), sem("w_lo")
        moe_hi, moe_lo = sem("moe_hi"), sem("moe_lo")
        mask_ready = sem("mask_ready")
        l2_deq, l2_tr, l2_cp = sem("l2_deq"), sem("l2_tr"), sem("l2_cp")
        p_mm, p_sum, p_lo = sem("p_mm"), sem("p_sum"), sem("p_lo")
        p_put = sems("p_put", 2)
        v_mm, v_out, v_ones = sem("v_mm"), sem("v_out"), sem("v_ones")
        xn_ready, xt_mm, xt_hi, xt_lo = (sems(n, 9) for n in ("xn_ready", "xt_mm", "xt_hi", "xt_lo"))
        stack_in, zeroed = sems("stack_in", 4), sem("zeroed")
        s_done, max_done, nt_done, nm_hi, nm_lo = (
            sem(n) for n in ("s_done", "max_done", "nt_done", "nm_hi", "nm_lo"))
        st_done, exp_done, pv_done = sem("st_done"), sem("exp_done"), sem("pv_done")
        oc_cp, t_mm, rec_done, on_done, ot_done, ot_cp = (
            sem(n) for n in ("oc_cp", "t_mm", "rec_done", "on_done", "ot_done", "ot_cp"))
        y_done, x_done, xb_done, st6_done, mv_done = (
            sem(n) for n in ("y_done", "x_done", "xb_done", "st6_done", "mv_done"))
        gl_mm, sig_done, w9_ready, w9t_mm, w9t_cp, bias_mm, acc_init = (
            sem(n) for n in ("gl_mm", "sig_done", "w9_ready", "w9t_mm", "w9t_cp", "bias_mm", "acc_init"))
        lg_ready, gh_done, l2_norm = sem("lg_ready"), sem("gh_done"), sem("l2_norm")
        up_mm, gelu_done, split_done, dn_mm, comb_done = (
            sem(n) for n in ("up_mm", "gelu_done", "split_done", "dn_mm", "comb_done"))
        moe_done = sem("moe_done")
        fc_ready, h_sum, f1_mm, silu_done, f2_mm, f2_out = (
            sem(n) for n in ("fc_ready", "h_sum", "f1_mm", "silu_done", "f2_mm", "f2_out"))
        gm_part, gm_all = sem("gm_part"), sem("gm_all")
        gu_mm, gu_cp, gate_r, sig2, o_q, d_mm, d_out = (
            sem(n) for n in ("gu_mm", "gu_cp", "gate_r", "sig2", "o_q", "d_mm", "d_out"))
        r_q, r_mm, r_cp, z_mm, z_cols, z_out, stored = (
            sem(n) for n in ("r_q", "r_mm", "r_cp", "z_mm", "z_cols", "z_out", "stored"))
        expert_cp = sem("expert_cp")
        l2_inv, up_scale, up_q, act_go, act_shift = (
            sem(n) for n in ("l2_inv", "up_scale", "up_q", "act_go", "act_shift"))
        dve_self, pool_self = sem("dve_self"), sem("pool_self")

        block = ctx.enter_context(nc.Block())

        @block.sync
        def _(sp):
            sp.dma_start(WRAW, a["watt"]).then_inc(ld_w, 16)
            sp.dma_start(CRAW, a["ctx_t"]).then_inc(ld_ctx, 16)
            sp.dma_start(COLS[:], a["cols"]).then_inc(ld_small, 16)
            sp.dma_start(ROWS[:], a["rows"].partition_broadcast(P)).then_inc(ld_small, 16)
            sp.dma_start(DB[:], a["down_b"]).then_inc(ld_small, 16)
            sp.dma_start(X[:], a["x"]).then_inc(ld_x, 16)
            sp.dma_start(RT[:], a["rhs_t"]).then_inc(ld_rhs, 16)
            sp.dma_start(WO[:], a["wo"]).then_inc(ld_wo, 16)

            def load_experts(part):
                dst, src = ((UPRAW, a["up_w"]), (DNRAW, a["down_w"]))[part % 2]
                e = slice(part // 2 * 3, part // 2 * 3 + 3)
                sp.dma_start(dst[:, e, :], src[:, e, :]).then_inc(ld_moe[part], 16)

            def put(job, scr, side):
                sp.wait_ge(p_lo, job + 1)
                dst = scr.rearrange("(m r) (g t) -> r m g t", r=4, g=NG)
                for row, part in enumerate((PJH, PJL, PJH) if side == "k" else (PJH, PJH, PJL)):
                    sp.dma_start(dst[row], part[:, job % 2, :]).then_inc(p_put[job % 2], 16)

            def put_keys(L, c):
                put(key_job(L, c), kscr[L * NC + c], "k")

            def put_queries(L, c):
                put(query_job(L, c), qscr[c], "q")

            def wait_written(job):
                for j in (job, job - 1):
                    sp.wait_ge(p_put[j % 2], 48 * (j // 2 + 1))

            for c in range(NC):
                put_keys(0, c)
            load_experts(0)
            load_experts(1)

            def load(L, b, sides="kq"):
                c, i = divmod(b, BC)
                cols = slice(P * i, P * (i + 1))
                k, q = (src.rearrange("p (g t) -> p g t", g=NG)[:, :, cols] for src in (kscr[L * NC + c], qscr[c]))
                if "k" in sides:
                    sp.dma_start(SK[:, i, :].rearrange("p (g t) -> p g t", g=NG), k).then_inc(stack_in[i], 16)
                if "q" in sides:
                    for j in range(4):
                        rows = slice(32 * j, 32 * (j + 1))
                        sp.dma_start(SQ[rows, i, j, :].rearrange("p (g t) -> p g t", g=NG), q[rows]).then_inc(stack_in[i], 16)

            for L in range(NL):
                units0, _ = earlier(L)
                if L == 1:
                    sp.wait_ge(mask_rows, 16 * 2 * NC)
                if L > 0:
                    sp.wait_ge(pv_done, units0)
                if L == 0:
                    sp.wait_ge(scr_init, 32)
                wait_written(key_job(L, NC - 1))
                for b in range(BC):
                    load(L, b, "k")
                put_queries(L, 0)
                wait_written(query_job(L, 0))
                sp.wait_ge(zeroed, ZEROED[L])
                load(L, 0, "q")
                put_queries(L, 1)
                for b in range(1, BC):
                    load(L, b, "q")
                if L == 0:
                    load_experts(2)
                    load_experts(3)
                for b in range(BC, NB):
                    c, i = divmod(b, BC)
                    if chunk_at(Q_PUT, b) is not None:
                        put_queries(L, chunk_at(Q_PUT, b))
                    if chunk_at(K_PUT, b) is not None and L < NL - 1:
                        put_keys(L + 1, chunk_at(K_PUT, b))
                    sp.wait_ge(st_done, units0 + 4 * (b - BC + 1))
                    if i == 0:
                        wait_written(query_job(L, c))
                    load(L, b)
                    if L == 0 and b in (BC, BC + 1):
                        load_experts(b)

            for c in range(NC):
                sp.wait_ge(z_out, BC * (c + 1))
                sp.dma_start(out[BC * c:BC * (c + 1)].rearrange("b t d -> t b d"),
                             X[:, BC * c:BC * (c + 1), :]).then_inc(stored, 16)
            sp.wait_ge(stored, 16 * NC)

        @block.gpsimd
        def _(pool):
            order = SelfOrder(pool, pool_self)
            for scr, name, n in ((qscr, "q_const", 4 * NC), (kscr, "k_const", 4 * NL * NC)):
                dst = scr.rearrange("c (j i r) t -> r (c j) i t", j=4, r=4)[3]
                pool.dma_start(dst, a[name].rearrange("(o r) t -> o r t", o=1).to_broadcast((n, DK, NG * CT))
                               ).then_inc(scr_init, 16)
            pool.dma_start(MKI[:], a["mask1"]).then_inc(ld_mask, 16)
            pool.dma_start(MK8W[:], a["mask3"]).then_inc(ld_mask, 16)
            order(pool.memset(ID[:], 0.0))
            order(pool.affine_select(out=ID[:], in_=ID[:], compare_op=ALU.not_equal, fill=1.0, base=0,
                                     pattern=[[-1, P]], channel_multiplier=1))
            pool.tensor_copy(IDH[:], ID[:]).then_inc(ident, 1)
            pool.tensor_scalar(IDB[:], ID[:], BIG, 1.0, ALU.mult, ALU.mult).then_inc(ident, 1)
            pool.dma_start(SEL[:], a["select"]).then_inc(ld_sel, 16)
            order(pool.memset(NHL[:], 0.0))
            order(pool.memset(ROUNDS[:], ROUND))

            def zero_stacks():
                pool.memset(SQ[:].rearrange("p s j t -> p (s j t)").bitcast(F32), 0.0).then_inc(zeroed, 1)

            zero_stacks()
            pool.wait_ge(am_local, 1)
            pool.partition_all_reduce(AMR[:, 0:A_UP], AM[:, 0:A_UP], P, ABSMAX).then_inc(am_all, 1)
            pool.wait_ge(ctx_lo, NC)
            order(pool.memset(VAF[:, VA_N:], 0.0))
            pool.memset(VA[:, :, :, DK:DK + 1], 1.0).then_inc(v_ones, 1)
            pool.wait_ge(mask_ready, 2)
            pool.wait_ge(scr_init, 32)
            pool.dma_start(mscr.rearrange("i c (b t) -> (c b) i t", b=BC), MKH[:]).then_inc(mask_put, 16)
            pool.wait_ge(mask_put, 16)
            for i, L in enumerate((1, 3)):
                for c in range(NC):
                    dst = kscr[L * NC + c].rearrange("(j r) (g t) -> r j g t", r=32, g=NG)[MASK_ROW]
                    src = mscr[i:i + 1, c:c + 1, :].to_broadcast((4, NG, CT))
                    pool.dma_start(dst, src).then_inc(mask_rows, 16)

            def residual_bias(L):
                gbo = SMALL[:, 192:320]
                order(pool.tensor_scalar(gbo, ROWS[:, R_BO + P * L:R_BO + P * (L + 1)], TG[:, L:L + 1], 1.0,
                                         ALU.mult, ALU.mult))
                for c in range(NC):
                    pool.wait_ge(xn_ready[2 * L], BC * (c + 1))
                    xc = X[:, BC * c:BC * (c + 1), :]
                    pool.tensor_tensor(xc, xc, gbo.rearrange("p (o d) -> p o d", o=1).to_broadcast((P, BC, P)), ALU.add
                                       ).then_inc(xb_done, 1)

            pool.wait_ge(tanh_done, 1)
            residual_bias(0)
            pool.wait_ge(am_local, 2)
            pool.partition_all_reduce(AMR[:, A_UP:], AM[:, A_UP:], P, ABSMAX).then_inc(am_all, 1)
            for e in range(NE):
                for i, (lo, raw, hi, at) in enumerate(((UPL, UPRAW, UPH, A_UP), (DNL, DNRAW, DNH, A_DN))):
                    pool.wait_ge(moe_hi, 2 * e + i + 2)
                    order(pool.tensor_scalar(raw[:, e, :], raw[:, e, :], SC[:, at + e:at + e + 1], 1.0, ALU.mult, ALU.mult))
                    pool.tensor_tensor(lo[:, e, :], raw[:, e, :], hi[:, e, :], ALU.subtract).then_inc(moe_lo, 1)
            pool.wait_ge(moe_done, 1)
            pool.dma_start(FC1I, a["fc1_q"]).then_inc(ld_fc, 16)
            pool.dma_start(FC2I, a["fc2_q"]).then_inc(ld_fc, 16)
            pool.dma_start(MRAW, a["mask2"]).then_inc(ld_fc, 16)
            pool.dma_start(L2RAW, a["w_l2"]).then_inc(ld_l2, 16)
            zero_stacks()
            residual_bias(1)
            pool.wait_ge(ld_fc, 48)
            pool.tensor_scalar(FC1[:], FC1I, -128.0, None, ALU.add).then_inc(fc_ready, 1)
            order(pool.tensor_scalar(FC2[:].rearrange("p i o -> p (i o)"), FC2I, -128.0, None, ALU.add))
            order(pool.tensor_tensor(FC2[:].rearrange("p i o -> p (i o)"), FC2[:].rearrange("p i o -> p (i o)"),
                                     ROWS[:, R_S2:R_S2 + CT], ALU.mult))
            order(pool.tensor_scalar(MB, MRAW, 0.0, -BIG, ALU.is_equal, ALU.mult))
            pool.memset(SCAL[:, 31:32], 0.0).then_inc(fc_ready, 1)
            w = L2RAW.rearrange("p (k n) -> p k n", n=32)
            scale, inv = (v.rearrange("p (k o) -> p k o", o=1).to_broadcast((P, 36, 32)) for v in (BLK[:, 0], BLK[:, 1]))
            pool.wait_ge(l2_inv, 1)
            order(pool.tensor_tensor(w, w, inv, ALU.mult))
            order(pool.tensor_scalar(L2RAW, L2RAW, ROUND, None, ALU.add))
            order(pool.tensor_scalar(L2RAW, L2RAW, ROUND, -8.0, ALU.subtract, ALU.max))
            order(pool.tensor_scalar(L2RAW, L2RAW, 7.0, None, ALU.min))
            pool.tensor_tensor(w, w, scale, ALU.mult).then_inc(l2_deq, 1)
            for i in range(5):
                pool.wait_ge(gm_part, i + 1)
                pool.partition_all_reduce(SCAL[:, 8 + i:9 + i], SCAL[:, i:i + 1], P, ABSMAX).then_inc(gm_all, 1)
                if i == 2:
                    pool.wait_ge(up_scale, 1)
                    for o in range(3):
                        order(pool.tensor_scalar(UT[:, o, :], UT[:, o, :], SCALE[:, 10:11], ROUND, ALU.mult, ALU.add))
                        pool.tensor_scalar(UT[:, o, :], UT[:, o, :], -ROUND, 1.0, ALU.add, ALU.mult).then_inc(up_q, 1)
            pool.wait_ge(d_out, NB)
            zero_stacks()

        @block.tensor
        def _(pe):
            def product3(dst, wh, wl, xh, xl, start=True, stop=True):
                pe.matmul(dst, wh, xh, start=start, stop=False)
                pe.matmul(dst, wh, xl, start=False, stop=False)
                return pe.matmul(dst, wl, xh, start=False, stop=stop)

            def norm_transposes(i, src, chunks=range(NC)):
                for c in chunks:
                    pe.wait_ge(xn_ready[i], BC * (c + 1))
                    if c >= 2:
                        pe.wait_ge(xt_lo[i], c - 1)
                    for b in range(BC):
                        mm = pe.transpose(bank[6 + c % 2][:, P * b:P * (b + 1)], src[:, BC * c + b, :], ID[:])
                    mm.then_inc(xt_mm[i], 1)

            def keys(L, c, to):
                product3(to[:], WAH[:, 4 + L, :], WAL[:, 4 + L, :],
                         CTH[:, BC * c:BC * (c + 1), :], CTL[:, BC * c:BC * (c + 1), :]).then_inc(p_mm, 1)

            def values_of(L, c, to):
                for i in range(BC):
                    mm = product3(to[:, P * i:P * (i + 1)], CTH[:, BC * c + i, :], CTL[:, BC * c + i, :],
                                  WAH[:, 8 + L, :], WAL[:, 8 + L, :])
                mm.then_inc(v_mm, 1)

            pe.wait_ge(ident, 2)
            pe.wait_ge(w_lo, 9)
            pe.wait_ge(ctx_lo, NC)
            for c in range(NC):
                keys(0, c, bank[c])

            def attention(L):
                units0, batches0 = earlier(L)

                def transposes(c, to):
                    pe.wait_ge(xn_ready[2 * L], BC * (c + 1))
                    for i in range(BC):
                        mm = pe.transpose(to[:, P * i:P * (i + 1)], XNC[L][:, c % 2, i, :], ID[:])
                    mm.then_inc(xt_mm[2 * L], 1)

                def queries(c, to):
                    pe.wait_ge(xt_lo[2 * L], c + 1)
                    product3(to[:], WAH[:, L, :], WAL[:, L, :],
                             XTH[:, BC * c:BC * (c + 1), :], XTL[:, BC * c:BC * (c + 1), :]).then_inc(p_mm, 1)

                if L == 2:
                    pe.wait_ge(l2_cp, 3)
                if L == 0:
                    pe.wait_ge(ld_sel, 16)
                for c in range(2):
                    transposes(c, bank[6 + c])
                if L == 0:
                    pe.wait_ge(p_sum, NC)
                for c in range(2):
                    queries(c, bank[4 + c])
                if L == 0:
                    for c in range(NC):
                        values_of(0, c, bank[c])
                pe.wait_ge(p_sum, query_job(L, 1) + 1)
                if L == 0:
                    pe.wait_ge(v_out, NB)

                def scores(n):
                    b, j = divmod(n, 4)
                    slot = b % 4
                    dst = bank[n % 2]
                    if j == 0:
                        pe.wait_ge(stack_in[slot], 20 * batches0 + 80 * (b // 4 + 1))
                    if n >= 2:
                        pe.wait_ge(max_done, units0 + n - 1)
                    for g in range(NG):
                        cols = slice(P * g, P * (g + 1))
                        if L == 2:
                            pe.matmul(dst[:, cols], IDB[:], MB[:, b, :], start=True, stop=False)
                        mm = pe.matmul(dst[:, cols], SQ[:, slot, j, cols], SK[:, slot, cols], start=L != 2, stop=True)
                    mm.then_inc(s_done, 1)

                def shifted(n):
                    b, j = divmod(n, 4)
                    slot = b % 4
                    dst = bank[2 + n % 2]
                    if j == 0:
                        pe.wait_ge(nm_lo, batches0 + b + 1)
                    if n >= 2:
                        pe.wait_ge(exp_done, units0 + n - 1)
                    for g in range(NG):
                        cols = slice(P * g, P * (g + 1))
                        if L == 2:
                            pe.matmul(dst[:, cols], MB[:, b, :], IDB[:], start=True, stop=False)
                        pe.matmul(dst[:, cols], SK[:, slot, cols], SQ[:, slot, j, cols], start=L != 2, stop=False)
                        mm = pe.matmul(dst[:, cols], SEL[:, NG * j + g:NG * j + g + 1].to_broadcast((LO_AT + NH, P)),
                                       NHL[:, b % 2, :], start=False, stop=True)
                    mm.then_inc(st_done, 1)

                def values(n):
                    b, j = divmod(n, 4)
                    pe.wait_ge(exp_done, units0 + n + 1)
                    if j == 0 and b >= 2:
                        pe.wait_ge(oc_cp, batches0 + b - 1)
                    for g in range(NG):
                        at = ((b * NL + L) * NH + NG * g + j) * (DK + 1)
                        mm = pe.matmul(bank[4 + b % 2][32 * g:32 * (g + 1), P * j:P * (j + 1)],
                                       VAF[:, at:at + 32], PR[:, j, P * g:P * (g + 1)], start=True, stop=True)
                    mm.then_inc(pv_done, 1)

                for n in range(STEPS):
                    if n < UNITS:
                        scores(n)
                    if 0 <= n - ST_LAG < UNITS:
                        shifted(n - ST_LAG)
                    if n == PV_LAG:
                        pe.wait_ge(v_out, NB * min(L + 2, NL))
                    b = due(n, Y_LAG)
                    if b is not None:
                        pe.wait_ge(ot_cp, batches0 + b + 1)
                        pe.matmul(bank[7][:, 2 * P:3 * P], OT[:, b % 2, :], WO[:, L, :], start=True, stop=True
                                  ).then_inc(y_done, 1)
                    if 0 <= n - PV_LAG < UNITS:
                        values(n - PV_LAG)
                    b = due(n, T_LAG)
                    if b is not None:
                        pe.wait_ge(oc_cp, batches0 + b + 1)
                        if b >= 1:
                            pe.wait_ge(on_done, batches0 + b)
                        c = chunk_at(T_STEP, n - 2)
                        if c is not None:
                            pe.wait_ge(xt_lo[2 * L], c + 1)
                        c = chunk_at(Q_STEP, n - 2)
                        if c is not None:
                            pe.wait_ge(p_sum, query_job(L, c) + 1)
                        c = chunk_at(K_STEP, n - 2)
                        if c is not None and L < NL - 1:
                            pe.wait_ge(p_sum, key_job(L + 1, c) + 1)
                        for j in range(4):
                            mm = pe.transpose(bank[6][:, P * j:P * (j + 1)], OC[:, b % 2, P * j:P * (j + 1)], ID[:])
                        mm.then_inc(t_mm, 1)
                    b = due(n, NT_LAG)
                    if b is not None:
                        pe.wait_ge(max_done, units0 + b * 4 + 4)
                        if b >= 4:
                            pe.wait_ge(x_done, batches0 + b - 3)
                        pe.transpose(bank[7][0:NH, 0:P], NM[:, b % 2, :], ID[:]).then_inc(nt_done, 1)
                    b = due(n, OT_LAG)
                    if b is not None:
                        pe.wait_ge(on_done, batches0 + b + 1)
                        pe.wait_ge(nm_lo, batches0 + min(b + 4, NB))
                        if b >= 1:
                            pe.wait_ge(x_done, batches0 + b)
                        pe.transpose(bank[7][:, P:2 * P], ON[:, b % 2, :], ID[:]).then_inc(ot_done, 1)
                    c = chunk_at(V_STEP, n)
                    if c is not None and L < NL - 1:
                        if c >= 2:
                            pe.wait_ge(v_out, NB * (L + 1) + BC * (c - 1))
                        values_of(L + 1, c, bank[5 + c % 2])
                    c = chunk_at(T_STEP, n)
                    if c is not None:
                        if n > T_LAG:
                            pe.wait_ge(on_done, batches0 + (n - T_LAG) // 4 + 1)
                        elif L < NL - 1:
                            pe.wait_ge(v_out, NB * (L + 2))
                        transposes(c, bank[6])
                    c = chunk_at(Q_STEP, n)
                    if c is not None:
                        if n > T_LAG:
                            pe.wait_ge(on_done, batches0 + (n - T_LAG) // 4 + 1)
                        queries(c, bank[6])
                    c = chunk_at(K_STEP, n)
                    if c is not None and L < NL - 1:
                        pe.wait_ge(on_done, batches0 + (n - T_LAG) // 4 + 1)
                        keys(L + 1, c, bank[6])

            def experts():
                norm_transposes(1, XN)
                pe.wait_ge(moe_lo, 2 * NE + 1)
                pe.wait_ge(xt_lo[1], NC)
                for b in range(NB):
                    mm = product3(bank[5][:, 8 * b:8 * b + 8], XTH[:, b, :], XTL[:, b, :], GWH[:], GWL[:])
                mm.then_inc(gl_mm, 1)

                def up(e, n, c):
                    for i in range(NI):
                        if at_least(n, 1):
                            pe.wait_ge(gelu_done, n * 4 + (i - 3))
                        w = slice(P * i, P * (i + 1))
                        product3(bank[i][:], UPH[:, e, w], UPL[:, e, w],
                                 XTH[:, BC * c:BC * (c + 1), :], XTL[:, BC * c:BC * (c + 1), :]).then_inc(up_mm, 1)

                up(0, 0, 0)
                pe.wait_ge(w9_ready, 1)

                def routing_transposes(c):
                    if c >= 2:
                        pe.wait_ge(w9t_cp, c - 1)
                    for b in range(BC):
                        mm = pe.transpose(bank[6 + c % 2][0:NE, P * b:P * (b + 1)], W9[:, BC * c + b, :], ID[:])
                    mm.then_inc(w9t_mm, 1)

                routing_transposes(0)
                for c in range(NC):
                    if c < NC - 1:
                        routing_transposes(c + 1)
                    pe.wait_ge(w9t_cp, c + 1)
                    if c >= 2:
                        pe.wait_ge(acc_init, c - 1)
                    for b in range(BC):
                        mm = pe.matmul(bank[4 + c % 2][:, P * b:P * (b + 1)],
                                       W9T[0:NE, CT * (c % 2) + P * b:CT * (c % 2) + P * (b + 1)], DB[:],
                                       start=True, stop=True)
                    mm.then_inc(bias_mm, 1)

                def down(e, n, c):
                    pe.wait_ge(split_done, n * 4 + 4)
                    pe.wait_ge(acc_init, NC)
                    if at_least(n, 2):
                        pe.wait_ge(comb_done, n - 1)
                    s = c % 2
                    for t in range(BC):
                        tok = slice(P * t, P * (t + 1))
                        for i in range(NI):
                            w = slice(P * i, P * (i + 1))
                            mm = product3(bank[4 + s][:, tok], GH[:, s, i, tok], GL[:, s, i, tok],
                                          DNH[:, e, w], DNL[:, e, w], start=i == 0, stop=i == NI - 1)
                    mm.then_inc(dn_mm, 1)

                def turn(e, n0, last):
                    for c in range(NC):
                        if c < NC - 1:
                            up(e, n0 + (c + 1), c + 1)
                        elif not last:
                            up(e + 1, n0 + NC, 0)
                        down(e, n0 + c, c)

                turn(0, 0, False)
                with pe.Fori(1, NE - 1) as e:
                    turn(e, e * 4, False)
                turn(NE - 1, 4 * (NE - 1), True)

            def quantised_mlp():
                pe.wait_ge(x_done, 2 * NB)
                norm_transposes(8, XN2, range(2))
                pe.wait_ge(fc_ready, 2)
                for c in range(NC):
                    pe.wait_ge(xt_lo[8], c + 1)
                    for i in range(NI):
                        if c >= 1:
                            pe.wait_ge(silu_done, 4 * (c - 1) + i + 1)
                        w = FC1[:, P * i:P * (i + 1)]
                        pe.matmul(bank[i][:], w, XTH[:, BC * c:BC * (c + 1), :], start=True, stop=False)
                        pe.matmul(bank[i][:], w, XTL[:, BC * c:BC * (c + 1), :], start=False, stop=True
                                  ).then_inc(f1_mm, 1)
                    if c == 1:
                        norm_transposes(8, XN2, range(2, NC))
                    if c >= 1:
                        second(c - 1)
                second(NC - 1)
                pe.wait_ge(l2_deq, 1)
                for m in range(9):
                    if m >= 8:
                        pe.wait_ge(l2_cp, 1)
                    mm = pe.transpose(bank[6 + m // 4 % 2][:, P * (m % 4):P * (m % 4 + 1)],
                                      L2RAW[:, P * m:P * (m + 1)], ID[:])
                    if m % 4 == 3 or m == 8:
                        mm.then_inc(l2_tr, 1)

            def second(c):
                pe.wait_ge(silu_done, 4 * (c + 1))
                if c >= 2:
                    pe.wait_ge(f2_out, 4 * (c - 1))
                for t in range(BC):
                    for i in range(NI):
                        mm = pe.matmul(bank[4 + c % 2][:, P * t:P * (t + 1)], G[:, c % 2, i, P * t:P * (t + 1)],
                                       FC2[:, i, :], start=i == 0, stop=i == NI - 1)
                mm.then_inc(f2_mm, 1)

            def fixed_point_mlp():
                norm_transposes(5, XN)
                n = 0
                for m in range(6):
                    for c in range(NC):
                        pe.wait_ge(xt_lo[5], c + 1)
                        if n >= 4:
                            pe.wait_ge(gu_cp, n - 3)
                        pe.matmul(bank[n % 4][:], WL2T[:, m, :], XT32[:, CT * c:CT * (c + 1)], start=True, stop=True
                                  ).then_inc(gu_mm, 1)
                        n += 1
                for b in range(NB):
                    pe.wait_ge(o_q, b // BC + 1)
                    if b >= 2:
                        pe.wait_ge(d_out, b - 1)
                    for i in range(3):
                        mm = pe.matmul(bank[4 + b % 2][:, 0:P], GT[:, i, P * b:P * (b + 1)], WL2T[:, 6 + i, :],
                                       start=i == 0, stop=i == 2)
                    mm.then_inc(d_mm, 1)

            def int8_product():
                pe.wait_ge(r_q, 1)
                pe.transpose(bank[0][:].bitcast(F16)[:, 0:P], RQH, IDH[:]).then_inc(r_mm, 1)
                pe.matmul(bank[1][:, 0:P], SCAL[:, 20:21].to_broadcast((P, P)), ID[:], start=True, stop=True
                          ).then_inc(r_mm, 1)
                for c in range(NC):
                    pe.wait_ge(xn_ready[7], NB + c + 1)
                    if c >= 2:
                        pe.wait_ge(xt_hi[7], c - 1)
                    for b in range(BC):
                        mm = pe.transpose(bank[6 + c % 2][:].bitcast(F16)[:, P * b:P * (b + 1)], XQH[:, BC * c + b, :], IDH[:])
                    mm.then_inc(xt_mm[7], 1)
                pe.wait_ge(r_cp, 2)
                for c in range(NC):
                    pe.wait_ge(xt_hi[7], c + 1)
                    if c >= 2:
                        pe.wait_ge(z_cols, c - 1)
                    for i in range(BC):
                        mm = pe.matmul(bank[4 + c % 2][:, P * i:P * (i + 1)], XQT[:, BC * c + i, :], RQT, start=True, stop=True)
                    mm.then_inc(z_mm, 1)

            attention(0)
            experts()
            attention(1)
            quantised_mlp()
            attention(2)
            fixed_point_mlp()
            attention(3)
            int8_product()

        @block.scalar
        def _(act):
            act.wait_ge(scales, 1)
            for c in range(NC):
                act.activation(CTH[:, BC * c:BC * (c + 1), :].rearrange("p b t -> p (b t)"), CRAW[:, CT * c:CT * (c + 1)],
                               ACT.Identity, scale=SC[:, A_CTX:A_CTX + 1]).then_inc(ctx_hi, 1)
            for m in range(9):
                mats = slice(m, m + 1) if m < 8 else slice(8, 12)
                act.activation(WAH[:, mats, :], WRAW[:, mats, :], ACT.Identity, scale=SC[:, m:m + 1]).then_inc(w_hi, 1)
            act.wait_ge(ld_small, 48)
            act.activation(TG[:], ROWS[:, R_GATES:R_GATES + 8], ACT.Tanh).then_inc(tanh_done, 1)

            def projected(job, of, bias, scale):
                act.wait_ge(p_mm, job + 1)
                if job >= 2:
                    act.wait_ge(p_lo, job - 1)
                    act.wait_ge(p_put[job % 2], 48 * (job // 2))
                for dst in (PJH, PJ):
                    ins = act.activation(dst[:, job % 2, :], of[:], ACT.Identity, bias=bias, scale=scale)
                ins.then_inc(p_sum, 1)

            def keys(L, c, of):
                projected(key_job(L, c), of, COLS[:, C_BK + L:C_BK + L + 1], DK_[:, L:L + 1])

            def expert_weights(m):
                if m == 0:
                    act.wait_ge(scales, 2)
                    act.activation(GWH[:], COLS[:, C_GW:C_GW + 8], ACT.Identity, scale=SC[:, A_GW:A_GW + 1]
                                   ).then_inc(moe_hi, 1)
                    return
                e, down = divmod(m - 1, 2)
                dst, src, at = ((UPH, UPRAW, A_UP), (DNH, DNRAW, A_DN))[down]
                act.activation(dst[:, e, :], src[:, e, :], ACT.Identity, scale=SC[:, at + e:at + e + 1]).then_inc(moe_hi, 1)

            for c in range(NC):
                keys(0, c, bank[c])

            def norm_hi(i):
                for c in range(NC):
                    act.wait_ge(xt_mm[i], c + 1)
                    act.copy(XTH[:, BC * c:BC * (c + 1), :].rearrange("p b t -> p (b t)"), bank[6 + c % 2][:]
                             ).then_inc(xt_hi[i], 1)

            def attention(L):
                units0, batches0 = earlier(L)

                def hi_part(c, of):
                    act.wait_ge(xt_mm[2 * L], c + 1)
                    act.copy(XTH[:, BC * c:BC * (c + 1), :].rearrange("p b t -> p (b t)"), of[:]).then_inc(xt_hi[2 * L], 1)

                def query_sums(c, of):
                    projected(query_job(L, c), of, COLS[:, C_BQ + L:C_BQ + L + 1], DS[:, A_Q + L:A_Q + L + 1])

                for c in range(2):
                    hi_part(c, bank[6 + c])
                for c in range(2):
                    query_sums(c, bank[4 + c])

                for n in range(STEPS):
                    b = due(n, L_LAG)
                    if b is not None:
                        act.wait_ge(nt_done, batches0 + b + 1)
                        if b >= 2:
                            act.wait_ge(st_done, units0 + 4 * (b - 1))
                        act.activation(NHL[0:NH, b % 2, :], bank[7][0:NH, 0:P], ACT.Copy, scale=1.0 / BIG
                                       ).then_inc(nm_hi, 1)
                    b = due(n, OT_LAG + 1)
                    if b is not None:
                        act.wait_ge(ot_done, batches0 + b + 1)
                        if b >= 2:
                            act.wait_ge(y_done, batches0 + b - 1)
                        act.copy(OT[:, b % 2, :], bank[7][:, P:2 * P]).then_inc(ot_cp, 1)
                    c = chunk_at(T_STEP, n - 1)
                    if c is not None:
                        hi_part(c, bank[6])
                    c = chunk_at(Q_STEP, n - 1)
                    if c is not None:
                        query_sums(c, bank[6])
                    c = chunk_at(K_STEP, n - 1)
                    if c is not None and L < NL - 1:
                        keys(L + 1, c, bank[6])
                    if L == 0 and 30 <= n < 30 + 2 * (2 * NE + 1) and n % 2 == 0:
                        expert_weights((n - 30) // 2)
                    m = n - ST_LAG
                    if 0 <= m < UNITS:
                        act.wait_ge(st_done, units0 + m + 1)
                        if m >= 4:
                            act.wait_ge(pv_done, units0 + m - 3)
                        act.activation(PR[:, m % 4, :], bank[2 + m % 2][:], ACT.Exp, scale=float(DK) ** -0.5
                                       ).then_inc(exp_done, 1)
                    b = due(n, OC_LAG)
                    if b is not None:
                        act.wait_ge(pv_done, units0 + b * 4 + 4)
                        if b >= 2:
                            act.wait_ge(t_mm, batches0 + b - 1)
                        act.copy(OC[:, b % 2, :], bank[4 + b % 2][:]).then_inc(oc_cp, 1)

            def experts():
                norm_hi(1)
                act.wait_ge(lg_ready, 1)
                act.activation(SIG[:], LG[:], ACT.Sigmoid).then_inc(sig_done, 1)

                def turn(e, n0, slot, chunks=range(NC)):
                    if 0 in chunks:
                        act.copy(EXPERT[:, slot, :], EXPERTS[:, e, :]).then_inc(expert_cp, 1)
                        act.wait_ge(expert_cp, e + 1)
                    for c in chunks:
                        n = n0 + c
                        for i in range(NI + 1):
                            if i < NI:
                                act.wait_ge(up_mm, n * 4 + (i + 1))
                                if at_least(n, 2):
                                    act.wait_ge(split_done, n * 4 + (i - 7))
                                act.activation(G[:, c % 2, i, :], bank[i][:], ACT.Gelu, bias=EXPERT[:, slot, i:i + 1],
                                               scale=EXPERT[:, slot, NI:NI + 1]).then_inc(gelu_done, 1)
                            if i > 0:
                                act.wait_ge(gelu_done, n * 4 + i)
                                if at_least(n, 2):
                                    act.wait_ge(dn_mm, n - 1)
                                act.activation(GH[:, c % 2, i - 1, :], G[:, c % 2, i - 1, :], ACT.Identity,
                                               scale=EXPERT[:, slot, NI + 1:NI + 2]).then_inc(gh_done, 1)

                turn(0, 0, 0, range(1))
                for c in range(NC):
                    act.wait_ge(w9t_mm, c + 1)
                    if c >= 2:
                        act.wait_ge(bias_mm, c - 1)
                    act.copy(W9T[0:NE, CT * (c % 2):CT * (c % 2 + 1)], bank[6 + c % 2][0:NE, :]).then_inc(w9t_cp, 1)
                turn(0, 0, 0, range(1, NC))
                with act.Fori(0, NE // 2) as pair:
                    for slot in (1, 0):
                        e = 2 * pair + (2 - slot)
                        turn(e, e * 4, slot)

            def quantised_mlp():
                def norm_sums(c):
                    act.wait_ge(xt_mm[8], c + 1)
                    if c >= 2:
                        act.wait_ge(xt_lo[8], c - 1)
                    act.activation(H32[:, c % 2, :], bank[6 + c % 2][:], ACT.Identity, bias=COLS[:, C_BETA:C_BETA + 1],
                                   scale=COLS[:, C_GAMMA:C_GAMMA + 1]).then_inc(h_sum, 1)

                norm_sums(0)
                norm_sums(1)
                for c in range(NC):
                    for i in range(NI):
                        act.wait_ge(f1_mm, 4 * c + i + 1)
                        if c >= 2:
                            act.wait_ge(f2_mm, c - 1)
                        act.activation(G[:, c % 2, i, :], bank[i][:], ACT.Silu, bias=COLS[:, C_B1 + i:C_B1 + i + 1],
                                       scale=COLS[:, C_S1 + i:C_S1 + i + 1]).then_inc(silu_done, 1)
                    if c == 0:
                        norm_sums(2)
                        norm_sums(3)
                for i in range(3):
                    act.wait_ge(l2_tr, i + 1)
                    m = 4 * i
                    n = 4 if i < 2 else 1
                    act.copy(WL2T[:, m:m + n, :].rearrange("p m o -> p (m o)"), bank[6 + i % 2][:, 0:P * n]
                             ).then_inc(l2_cp, 1)

            def fixed_point_mlp():
                for c in range(NC):
                    act.wait_ge(xt_mm[5], c + 1)
                    act.copy(XT32[:, CT * c:CT * (c + 1)], bank[6 + c % 2][:]).then_inc(xt_lo[5], 1)
                for m in range(6):
                    dst = GT if m < 3 else UT
                    for c in range(NC):
                        n = 4 * m + c
                        act.wait_ge(gu_mm, n + 1)
                        act.copy(dst[:, m % 3, CT * c:CT * (c + 1)], bank[n % 4][:]).then_inc(gu_cp, 1)
                for o in range(3):
                    act.wait_ge(gate_r, o + 1)
                    act.activation(TT[o], GT[:, o, :], ACT.Sigmoid, scale=SCALE[:, 1:2]).then_inc(sig2, 1)
                act.wait_ge(act_go, 1)
                for o in range(3):
                    act.activation(GT[:, o, :], GT[:, o, :], ACT.Identity, bias=ROUNDS[:], scale=SCALE[:, 18:19]
                                   ).then_inc(act_shift, 1)
                act.wait_ge(act_go, 2)
                for c in range(NC):
                    gc = GT[:, :, CT * c:CT * (c + 1)]
                    act.activation(gc, gc, ACT.Identity, bias=ROUNDS[:], scale=SCALE[:, 19:20]).then_inc(act_shift, 1)

            def int8_product():
                act.wait_ge(r_mm, 1)
                act.copy(RQT, bank[0][:].bitcast(F16)[:, 0:P]).then_inc(r_cp, 1)
                for c in range(NC):
                    act.wait_ge(xt_mm[7], c + 1)
                    act.copy(XQT[:, BC * c:BC * (c + 1), :].rearrange("p b t -> p (b t)"), bank[6 + c % 2][:].bitcast(F16)[:, 0:CT]
                             ).then_inc(xt_hi[7], 1)

            attention(0)
            experts()
            attention(1)
            quantised_mlp()
            attention(2)
            fixed_point_mlp()
            attention(3)
            int8_product()

        @block.vector
        def _(dve):
            order = SelfOrder(dve, dve_self)

            def power_scales(lo, hi):
                p2 = SMALL[:, 0:hi - lo]
                order(dve.tensor_scalar(p2.bitcast(I32), AMR[:, lo:hi].bitcast(I32), 0x7F800000, None, ALU.bitwise_and))
                order(dve.tensor_scalar(p2, p2, 2.0 ** -100, None, ALU.max))
                order(dve.tensor_scalar(DS[:, lo:hi], p2, 2.0 ** -14, None, ALU.mult))
                order(dve.reciprocal(p2, p2))
                order(dve.tensor_scalar(SC[:, lo:hi], p2, 2.0 ** 14, None, ALU.mult))

            def flat(ap):
                return ap.rearrange("p b t -> p (b t)")

            dve.wait_ge(ld_w, 16)
            dve.tensor_reduce(AM[:, 0:8], WRAW[:, 0:8, :], AX.X, ALU.max, apply_absolute_value=True)
            dve.tensor_reduce(AM[:, A_V:A_V + 1], WRAW[:, 8:12, :], AX.XY, ALU.max, apply_absolute_value=True)
            dve.wait_ge(ld_ctx, 16)
            dve.tensor_reduce(AM[:, A_CTX:A_CTX + 1], CRAW, AX.X, ALU.max, apply_absolute_value=True).then_inc(am_local, 1)
            dve.wait_ge(am_all, 1)
            power_scales(0, A_UP)
            order(dve.tensor_scalar(DK_[:, 0:4], DS[:, A_K:A_K + 4], DS[:, A_CTX:A_CTX + 1], None, ALU.mult))
            dve.tensor_scalar(DK_[:, 4:5], DS[:, A_V:A_V + 1], DS[:, A_CTX:A_CTX + 1], None, ALU.mult).then_inc(scales, 1)
            for c in range(NC):
                dve.wait_ge(ctx_hi, c + 1)
                low(dve, flat(CTL[:, BC * c:BC * (c + 1), :]), CRAW[:, CT * c:CT * (c + 1)], SC[:, A_CTX:A_CTX + 1],
                    flat(CTH[:, BC * c:BC * (c + 1), :])).then_inc(ctx_lo, 1)
            for m in range(9):
                mats = slice(m, m + 1) if m < 8 else slice(8, 12)
                dve.wait_ge(w_hi, m + 1)
                low(dve, flat(WAL[:, mats, :]), flat(WRAW[:, mats, :]), SC[:, m:m + 1], flat(WAH[:, mats, :])).then_inc(w_lo, 1)

            def projection_lo(job):
                dve.wait_ge(p_sum, job + 1)
                dve.tensor_tensor(PJL[:, job % 2, :], PJ[:, job % 2, :], PJH[:, job % 2, :], ALU.subtract).then_inc(p_lo, 1)

            def values_out(L, c, of):
                dve.wait_ge(v_mm, NC * L + c + 1)
                for i in range(BC):
                    dve.scalar_tensor_tensor(out=VA[:, BC * c + i, NH * L:NH * (L + 1), 0:DK],
                                             in0=of[:, P * i:P * (i + 1)].rearrange("p (h d) -> p h d", d=DK),
                                             scalar=DK_[:, 4:5],
                                             in1=ROWS[:, R_BV + P * L:R_BV + P * (L + 1)].rearrange("p (h d) -> p h d", d=DK),
                                             op0=ALU.mult, op1=ALU.add).then_inc(v_out, 1)

            def masks():
                dve.wait_ge(ld_mask, 32)
                dve.tensor_scalar(MKH[:, 0, :], MKI[:], 0.0, -BIG, ALU.is_equal, ALU.mult).then_inc(mask_ready, 1)
                dve.tensor_scalar(MKH[:, 1, :], MK8, 0.0, -BIG, ALU.is_equal, ALU.mult).then_inc(mask_ready, 1)

            def expert_magnitudes(part):
                at, src = ((A_UP, UPRAW), (A_DN, DNRAW))[part % 2]
                e = part // 2 * 3
                dve.wait_ge(ld_moe[part], 16)
                dve.tensor_reduce(AM[:, at + e:at + e + 3], src[:, e:e + 3, :], AX.X, ALU.max, apply_absolute_value=True)
                if part == 5:
                    dve.tensor_reduce(AM[:, A_GW:A_GW + 1], COLS[:, C_GW:C_GW + 8], AX.X, ALU.max, apply_absolute_value=True)
                    dve.tensor_reduce(AM[:, A_UB:A_UB + NE], COLS[:, C_UB:C_UB + 36].rearrange("p (e i) -> p e i", e=NE),
                                            AX.X, ALU.max, apply_absolute_value=True).then_inc(am_local, 1)

            def expert_scales():
                dve.wait_ge(am_all, 2)
                power_scales(A_UP, A_N)
                order(dve.tensor_copy(EXPERTS[:, :, 0:NI], COLS[:, C_UB:C_UB + 36].rearrange("p (e i) -> p e i", e=NE)))
                order(dve.tensor_copy(EXPERTS[:, :, NI], DS[:, A_UP:A_UP + NE]))
                b = SMALL[:, 0:NE]
                order(dve.scalar_tensor_tensor(out=b, in0=AMR[:, A_UP:A_UP + NE], scalar=float(P),
                                               in1=AMR[:, A_UB:A_UB + NE], op0=ALU.mult, op1=ALU.add))
                order(dve.tensor_scalar(b.bitcast(I32), b.bitcast(I32), 0x7F800000, None, ALU.bitwise_and))
                order(dve.tensor_scalar(b, b, 2.0 ** -100, None, ALU.max))
                order(dve.tensor_scalar(HS[:, 1, :], b, 2.0 ** -14, None, ALU.mult))
                order(dve.reciprocal(b, b))
                order(dve.tensor_scalar(EXPERTS[:, :, NI + 1], b, 2.0 ** 14, None, ALU.mult))
                dve.tensor_scalar(HS[:, 0, :], b, 2.0 ** 14, None, ALU.mult).then_inc(scales, 1)

            def stats(src, mv, batches):
                for b in batches:
                    ins = dve.bn_stats(ST6[:, b, :], src[:, b, :])
                order(ins)
                for b in batches:
                    ins = dve.bn_aggr(mv[:, b, :], ST6[:, b, :])
                return ins

            def inverse_root(mv, batches=slice(0, NB)):
                n = batches.stop - batches.start
                v, y, t = SMALL[:, 0:n], RSTD[:, batches], SMALL[:, 32:32 + n]
                order(dve.tensor_scalar(v, mv[:, batches, 1], EPS, None, ALU.add))
                order(dve.tensor_scalar(y.bitcast(I32), v.bitcast(I32), 1, None, ALU.logical_shift_right))
                order(dve.tensor_scalar(y.bitcast(I32), y.bitcast(I32), -1.0, float(0x5F3759DF), ALU.mult, ALU.add))
                for _ in range(3):
                    order(dve.tensor_tensor(t, y, y, ALU.mult))
                    order(dve.scalar_tensor_tensor(out=t, in0=t, scalar=-0.5, in1=v, op0=ALU.mult, op1=ALU.mult))
                    order(dve.scalar_tensor_tensor(out=y, in0=t, scalar=1.5, in1=y, op0=ALU.add, op1=ALU.mult))

            def normalise(dst, src, mv, ready, batches=range(NB)):
                for b in batches:
                    dve.tensor_scalar(dst[:, b, :], src[:, b, :], mv[:, b, 0:1], RSTD[:, b:b + 1],
                                      ALU.subtract, ALU.mult).then_inc(ready, 1)

            def two_norms(lo, hi, part):
                if part == 0:
                    dve.wait_ge(mv_done, NB + hi)
                    inverse_root(MV, slice(lo, hi))
                elif part == 1:
                    dve.wait_ge(xt_mm[2], NC)
                    normalise(XN1, X, MV, xn_ready[3], range(lo, hi))
                elif part == 2:
                    dve.wait_ge(xn_ready[3], hi)
                    order(stats(XN1, MV2, range(lo, hi)))
                elif part == 3:
                    inverse_root(MV2, slice(lo, hi))
                else:
                    normalise(XN2, XN1, MV2, xn_ready[8], range(lo, hi))

            def block_scales():
                dve.wait_ge(ld_l2, 16)
                order(dve.tensor_reduce(BLK[:, 0], L2RAW.rearrange("p (k n) -> p k n", n=32), AX.X, ALU.max,
                                        apply_absolute_value=True))
                order(dve.tensor_scalar(BLK[:, 0], BLK[:, 0], 1.0 / 7.0, 1e-12, ALU.mult, ALU.max))
                dve.reciprocal(BLK[:, 1], BLK[:, 0]).then_inc(l2_inv, 1)

            def norm_lo(i):
                for c in range(NC):
                    dve.wait_ge(xt_hi[i], c + 1)
                    dve.tensor_tensor(flat(XTL[:, BC * c:BC * (c + 1), :]), bank[6 + c % 2][:],
                                      flat(XTH[:, BC * c:BC * (c + 1), :]), ALU.subtract).then_inc(xt_lo[i], 1)

            def attention(L):
                units0, batches0 = earlier(L)
                inverse_root(MV)
                if L == 2:
                    dve.wait_ge(fc_ready, 2)
                    keep = SMALL[:, 64:64 + NB]
                    order(dve.tensor_reduce(keep, MB, AX.X, ALU.max))
                    order(dve.tensor_scalar(keep, keep, 0.0, None, ALU.is_equal))
                    order(dve.tensor_tensor(RSTD[:], RSTD[:], keep, ALU.mult))

                def normed(b):
                    c, i = divmod(b, BC)
                    if c >= 2:
                        dve.wait_ge(xt_mm[2 * L], c - 1)
                    dve.tensor_scalar(XNC[L][:, c % 2, i, :], X[:, b, :], MV[:, b, 0:1], RSTD[:, b:b + 1], ALU.subtract, ALU.mult
                                      ).then_inc(xn_ready[2 * L], 1)

                def lo_part(c, of):
                    dve.wait_ge(xt_hi[2 * L], c + 1)
                    dve.tensor_tensor(flat(XTL[:, BC * c:BC * (c + 1), :]), of[:], flat(XTH[:, BC * c:BC * (c + 1), :]),
                                      ALU.subtract).then_inc(xt_lo[2 * L], 1)

                def query_lo(c):
                    projection_lo(query_job(L, c))

                for b in range(2 * BC):
                    normed(b)
                for c in range(2):
                    lo_part(c, bank[6 + c])
                for c in range(2):
                    query_lo(c)
                if L == 0:
                    dve.wait_ge(v_ones, 1)
                    dve.wait_ge(ld_small, 48)
                    for c in range(NC):
                        values_out(0, c, bank[c])
                if L == 0:
                    masks()

                heads = bank[6][:].rearrange("p (h d) -> p h d", d=32)
                for n in range(STEPS):
                    b = due(n, L_LAG)
                    if b is not None:
                        dve.wait_ge(nm_hi, batches0 + b + 1)
                        low(dve, NHL[LO_AT:LO_AT + NH, b % 2, :], bank[7][0:NH, 0:P], 1.0 / BIG, NHL[0:NH, b % 2, :]).then_inc(nm_lo, 1)
                    b = due(n, STAT_LAG)
                    if b is not None:
                        dve.wait_ge(x_done, batches0 + b + 1)
                        dve.bn_stats(ST6[:, b, :], X[:, b, :]).then_inc(st6_done, 1)
                    b = due(n, X_LAG)
                    if b is not None:
                        dve.wait_ge(y_done, batches0 + b + 1)
                        if L < 2:
                            dve.wait_ge(xb_done, NC * L + b // BC + 1)
                        dve.scalar_tensor_tensor(out=X[:, b, :], in0=bank[7][:, 2 * P:3 * P], scalar=TG[:, L:L + 1],
                                                 in1=X[:, b, :], op0=ALU.mult, op1=ALU.add).then_inc(x_done, 1)
                    if n < UNITS:
                        b, j = divmod(n, 4)
                        dve.wait_ge(s_done, units0 + n + 1)
                        if j == 0 and b >= 2:
                            dve.wait_ge(nt_done, batches0 + b - 1)
                        dve.tensor_reduce(NM[:, b % 2, 4 * j:4 * j + 4], bank[n % 2][:].rearrange("p (g t) -> p g t", g=NG),
                                          AX.X, ALU.max, negate=True).then_inc(max_done, 1)
                    b = due(n, STAT_LAG)
                    if b is not None:
                        dve.wait_ge(st6_done, batches0 + b + 1)
                        dve.bn_aggr(MV[:, b, :], ST6[:, b, :]).then_inc(mv_done, 1)
                    c = chunk_at(V_STEP, n - 1)
                    if c is not None and L < NL - 1:
                        values_out(L + 1, c, bank[5 + c % 2])
                    if L == 0 and n in EXPERT_STEPS:
                        expert_magnitudes(EXPERT_STEPS.index(n))
                    if L == 0 and n == 27:
                        expert_scales()
                    if L == 0 and n == 31:
                        dve.wait_ge(moe_hi, 1)
                        low(dve, GWL[:], COLS[:, C_GW:C_GW + 8], SC[:, A_GW:A_GW + 1], GWH[:]).then_inc(moe_lo, 1)
                    for c, at in T_STEP.items():
                        if 0 <= at - 1 - n < BC:
                            normed(BC * c + at - 1 - n)
                    c = chunk_at(T_STEP, n - 1)
                    if c is not None:
                        lo_part(c, bank[6])
                    c = chunk_at(Q_STEP, n - 1)
                    if c is not None:
                        query_lo(c)
                    c = chunk_at(K_STEP, n - 1)
                    if c is not None and L < NL - 1:
                        projection_lo(key_job(L + 1, c))
                    if L == 1 and n == BLOCK_STEP:
                        block_scales()
                    if L == 1 and n in NORM_STEPS:
                        two_norms(0, NB // 2, NORM_STEPS.index(n))
                    b = due(n, REC_LAG)
                    if b is not None:
                        dve.wait_ge(t_mm, batches0 + b + 1)
                        dve.reciprocal(REC[:, b % 2, :], heads[:, :, DK]).then_inc(rec_done, 1)
                    b = due(n, ON_LAG)
                    if b is not None:
                        dve.wait_ge(rec_done, batches0 + b + 1)
                        if b >= 2:
                            dve.wait_ge(ot_done, batches0 + b - 1)
                        dve.tensor_tensor(ON[:, b % 2, :].rearrange("p (h d) -> p h d", d=DK), heads[:, :, 0:DK],
                                          REC[:, b % 2, :].rearrange("p (h o) -> p h o", o=1).to_broadcast((P, NH, DK)),
                                          ALU.mult).then_inc(on_done, 1)
                dve.wait_ge(mv_done, batches0 + NB)

            def experts():
                inverse_root(MV)
                normalise(XN, X, MV, xn_ready[1])
                norm_lo(1)
                def each(ap, n=8):
                    return ap.rearrange("p (b o) -> p b o", o=1).to_broadcast((P, NB, n))

                lg, key, sel, m = (SMALL[:, 0:0 + 128], SMALL[:, 128:256], W9[:], SMALL[:, 256:256 + NB])
                lg, key = (v.rearrange("p (b e) -> p b e", e=8) for v in (lg, key))
                sel = W9[:, :, 0:8]
                prio = ROWS[:, R_PRIO:R_PRIO + 8].rearrange("p (o e) -> p o e", o=1).to_broadcast((P, NB, 8))
                bias = ROWS[:, R_GBIAS:R_GBIAS + 8].rearrange("p (o e) -> p o e", o=1).to_broadcast((P, NB, 8))
                dve.wait_ge(gl_mm, 1)
                order(dve.tensor_scalar(LG[:], bank[5][:, 0:128].rearrange("p (b e) -> p b e", e=8),
                                        DS[:, A_GW:A_GW + 1], None, ALU.mult))
                dve.tensor_tensor(LG[:], LG[:], bias, ALU.add).then_inc(lg_ready, 1)
                dve.wait_ge(lg_ready, 1)
                order(dve.tensor_scalar(lg, LG[:], 16.6, -88.0, ALU.min, ALU.max))
                order(dve.memset(W9[:], 0.0))
                for _ in range(2):
                    order(dve.tensor_reduce(m, lg, AX.X, ALU.max))
                    order(dve.tensor_tensor(key, lg, each(m), ALU.is_equal))
                    order(dve.tensor_tensor(key, key, prio, ALU.mult))
                    order(dve.tensor_reduce(m, key, AX.X, ALU.max))
                    order(dve.tensor_tensor(key, key, each(m), ALU.is_equal))
                    order(dve.tensor_tensor(sel, sel, key, ALU.add))
                    order(dve.scalar_tensor_tensor(out=SMALL[:, 0:128], in0=SMALL[:, 128:256], scalar=-1e4,
                                                   in1=SMALL[:, 0:128], op0=ALU.mult, op1=ALU.add))
                dve.wait_ge(sig_done, 1)
                order(dve.tensor_tensor(sel, sel, SIG[:], ALU.mult))
                order(dve.tensor_reduce(m, sel, AX.X, ALU.add))
                order(dve.tensor_scalar(m, m, 1e-6, None, ALU.add))
                order(dve.reciprocal(m, m))
                order(dve.tensor_tensor(sel, sel, each(m), ALU.mult))
                order(dve.memset(W9[:, :, 8:9], 1.0))
                f = SMALL[:, 288:288 + NE]
                order(dve.tensor_tensor(f, DS[:, A_DN:A_DN + NE], HS[:, 1, :], ALU.mult))
                order(dve.tensor_scalar(f, f, 0.1, None, ALU.mult))
                dve.tensor_tensor(WF[:], W9[:], f.rearrange("p (o e) -> p o e", o=1).to_broadcast((P, NB, NE)),
                                  ALU.mult).then_inc(w9_ready, 1)
                for c in range(NC):
                    dve.wait_ge(bias_mm, c + 1)
                    dve.tensor_scalar(flat(ACC[:, BC * c:BC * (c + 1), :]), bank[4 + c % 2][:], 0.1, None, ALU.mult
                                      ).then_inc(acc_init, 1)

                def split(e, n, c):
                    for i in range(NI):
                        dve.wait_ge(gh_done, n * 4 + (i + 1))
                        low(dve, GL[:, c % 2, i, :], G[:, c % 2, i, :], HS[:, 0, bass.ds(e, 1)], GH[:, c % 2, i, :]
                            ).then_inc(split_done, 1)

                def combine(e, n, c):
                    dve.wait_ge(dn_mm, n + 1)
                    dve.wait_ge(acc_init, NC)
                    if at_least(n, 4):
                        dve.wait_ge(comb_done, n - 3)
                    for t in range(BC):
                        b = BC * c + t
                        ins = dve.scalar_tensor_tensor(out=ACC[:, b, :], in0=bank[4 + c % 2][:, P * t:P * (t + 1)],
                                                       scalar=WF[:, b, bass.ds(e, 1)], in1=ACC[:, b, :],
                                                       op0=ALU.mult, op1=ALU.add)
                    ins.then_inc(comb_done, 1)

                def add(c):
                    batches = range(BC * c, BC * (c + 1))
                    top = SMALL[:, 256 + BC * c:256 + BC * (c + 1)]
                    dve.wait_ge(comb_done, NC * (NE - 1) + c + 1)
                    order(dve.tensor_reduce(top, ACC[:, BC * c:BC * (c + 1), :], AX.X, ALU.max, apply_absolute_value=True))
                    order(dve.tensor_scalar(top, top, 1e-6, None, ALU.add))
                    order(dve.reciprocal(top, top))
                    order(dve.tensor_scalar(top, top, TG[:, 4:5], None, ALU.mult))
                    for b in batches:
                        ins = dve.scalar_tensor_tensor(out=X[:, b, :], in0=ACC[:, b, :], scalar=SMALL[:, 256 + b:257 + b],
                                                       in1=X[:, b, :], op0=ALU.mult, op1=ALU.add)
                    order(ins)
                    order(stats(X, MV, batches))

                def turn(e, n0, last):
                    for c in range(NC):
                        if c < NC - 1:
                            split(e, n0 + (c + 1), c + 1)
                        elif not last:
                            split(e + 1, n0 + NC, 0)
                        combine(e, n0 + c, c)
                        if last:
                            add(c)

                split(0, 0, 0)
                turn(0, 0, False)
                with dve.Fori(1, NE - 1) as e:
                    turn(e, e * 4, False)
                turn(NE - 1, 4 * (NE - 1), True)
                dve.memset(SCAL[:, 30:31], 0.0).then_inc(moe_done, 1)

            def quantised_mlp():
                def parts(c):
                    dve.wait_ge(h_sum, c + 1)
                    hi = flat(XTH[:, BC * c:BC * (c + 1), :])
                    order(dve.tensor_copy(hi, H32[:, c % 2, :]))
                    dve.tensor_tensor(flat(XTL[:, BC * c:BC * (c + 1), :]), H32[:, c % 2, :], hi, ALU.subtract
                                      ).then_inc(xt_lo[8], 1)

                for part in range(5):
                    two_norms(NB // 2, NB, part)
                    if part == 0:
                        parts(0)
                        parts(1)
                for c in range(2, NC):
                    parts(c)
                order(dve.tensor_scalar(SCAL[:, 24:25], TG[:, 5:6], 0.5, None, ALU.mult))
                order(dve.scalar_tensor_tensor(out=flat(X[:]), in0=flat(XN1), scalar=TG[:, 5:6], in1=flat(X[:]),
                                               op0=ALU.mult, op1=ALU.add))
                order(dve.tensor_scalar(SMALL[:, 128:256], ROWS[:, R_B2:R_B2 + P], SCAL[:, 24:25], None, ALU.mult))
                order(dve.tensor_tensor(X[:], X[:],
                                        SMALL[:, 128:256].rearrange("p (o d) -> p o d", o=1).to_broadcast((P, NB, P)),
                                        ALU.add))
                for c in range(NC):
                    dve.wait_ge(f2_mm, c + 1)
                    for t in range(BC):
                        b = BC * c + t
                        ins = dve.scalar_tensor_tensor(out=X[:, b, :], in0=bank[4 + c % 2][:, P * t:P * (t + 1)],
                                                       scalar=SCAL[:, 24:25], in1=X[:, b, :], op0=ALU.mult, op1=ALU.add)
                        ins.then_inc(f2_out, 1)
                    dve.wait_ge(f2_out, BC * (c + 1))
                    order(stats(X, MV, range(BC * c, BC * (c + 1))))

            def fixed_point_mlp():

                def global_max(i, pieces, waits=None):
                    for n, piece in enumerate(pieces):
                        if waits is not None:
                            dve.wait_ge(gu_cp, waits + 4 * (n + 1))
                        order(dve.tensor_reduce(SCAL[:, 16 + n:17 + n], piece, AX.X, ALU.max, apply_absolute_value=True))
                    dve.tensor_reduce(SCAL[:, i:i + 1], SCAL[:, 16:16 + len(pieces)], AX.X, ALU.max).then_inc(gm_part, 1)

                def scale_of(i, unit=None):
                    dve.wait_ge(gm_all, i + 1)
                    top = SCAL[:, 8 + i:9 + i]
                    if unit is not None:
                        order(dve.tensor_tensor(top, top, unit, ALU.mult))
                    order(dve.tensor_scalar(SCALE[:, i:i + 1], top, 1.0 / 32767.0, 1e-12, ALU.mult, ALU.max))
                    ins = dve.reciprocal(SCALE[:, 8 + i:9 + i], SCALE[:, i:i + 1])
                    if unit is not None:
                        order(ins)
                        ins = dve.tensor_tensor(SCALE[:, 8 + i:9 + i], SCALE[:, 8 + i:9 + i], unit, ALU.mult)
                    return ins

                def shifted(ap, i):
                    return dve.tensor_scalar(ap, ap, SCALE[:, 8 + i:9 + i], ROUND, ALU.mult, ALU.add)

                inverse_root(MV)
                normalise(XN, X, MV, l2_norm)
                dve.wait_ge(l2_norm, NB)
                global_max(0, [flat(XN[:])])
                order(scale_of(0))
                for c in range(NC):
                    xc = flat(XN[:, BC * c:BC * (c + 1), :])
                    order(shifted(xc, 0))
                    dve.tensor_scalar(xc, xc, ROUND, SCALE[:, 0:1], ALU.subtract, ALU.mult).then_inc(xn_ready[5], BC)
                dve.wait_ge(gm_part, 1)
                global_max(1, [GT[:, o, :] for o in range(3)], waits=0)
                order(scale_of(1))
                for o in range(3):
                    order(shifted(GT[:, o, :], 1))
                    dve.tensor_scalar(GT[:, o, :], GT[:, o, :], ROUND, None, ALU.subtract).then_inc(gate_r, 1)
                global_max(2, [UT[:, o, :] for o in range(3)], waits=12)
                scale_of(2).then_inc(up_scale, 1)
                for o in range(3):
                    dve.wait_ge(sig2, o + 1)
                    order(dve.tensor_scalar(TT[o], TT[o], 65535.0 / 65536.0, 192.0, ALU.min, ALU.add))
                    order(dve.scalar_tensor_tensor(out=GT[:, o, :], in0=TT[o], scalar=-192.0, in1=GT[:, o, :],
                                                   op0=ALU.add, op1=ALU.mult))
                global_max(3, [GT[:, o, :] for o in range(3)])
                order(scale_of(3, SCALE[:, 1:2]))
                order(dve.tensor_tensor(SCALE[:, 16:17], SCALE[:, 3:4], SCALE[:, 2:3], ALU.mult))
                dve.tensor_copy(SCALE[:, 18:19], SCALE[:, 11:12]).then_inc(act_go, 1)
                for o in range(3):
                    dve.wait_ge(act_shift, o + 1)
                    dve.wait_ge(up_q, o + 1)
                    order(dve.scalar_tensor_tensor(out=GT[:, o, :], in0=GT[:, o, :], scalar=-ROUND, in1=UT[:, o, :],
                                                   op0=ALU.add, op1=ALU.mult))
                global_max(4, [GT[:, o, :] for o in range(3)])
                order(scale_of(4, SCALE[:, 16:17]))
                order(dve.tensor_tensor(SCALE[:, 17:18], SCALE[:, 4:5], TG[:, 6:7], ALU.mult))
                dve.tensor_copy(SCALE[:, 19:20], SCALE[:, 12:13]).then_inc(act_go, 1)
                for c in range(NC):
                    gc = GT[:, :, CT * c:CT * (c + 1)]
                    dve.wait_ge(act_shift, 3 + c + 1)
                    dve.tensor_scalar(gc, gc, ROUND, None, ALU.subtract).then_inc(o_q, 1)
                for c in range(NC):
                    for b in range(BC * c, BC * (c + 1)):
                        dve.wait_ge(d_mm, b + 1)
                        dve.scalar_tensor_tensor(out=X[:, b, :], in0=bank[4 + b % 2][:, 0:P], scalar=SCALE[:, 17:18],
                                                 in1=X[:, b, :], op0=ALU.mult, op1=ALU.add).then_inc(d_out, 1)
                    dve.wait_ge(d_out, BC * (c + 1))
                    order(stats(X, MV, range(BC * c, BC * (c + 1))))

            def int8_product():
                dve.wait_ge(ld_rhs, 16)
                order(dve.tensor_reduce(SCAL[:, 20:21], RT[:], AX.X, ALU.max, apply_absolute_value=True))
                order(dve.tensor_scalar(SCAL[:, 20:21], SCAL[:, 20:21], 1e-12, 1.0 / 127.0, ALU.max, ALU.mult))
                order(dve.reciprocal(SCAL[:, 21:22], SCAL[:, 20:21]))
                order(dve.tensor_scalar(RQ, RT[:], SCAL[:, 21:22], ROUND, ALU.mult, ALU.add))
                dve.tensor_scalar(RQH, RQ, ROUND, None, ALU.subtract).then_inc(r_q, 1)
                inverse_root(MV)
                normalise(XN, X, MV, xn_ready[7])
                dve.wait_ge(xn_ready[7], NB)
                ls, inv = SMALL[:, 64:64 + NB], SMALL[:, 96:96 + NB]
                order(dve.tensor_reduce(ls, XN[:], AX.X, ALU.max, apply_absolute_value=True))
                order(dve.tensor_scalar(ls, ls, 1e-12, 1.0 / 127.0, ALU.max, ALU.mult))
                order(dve.reciprocal(inv, ls))
                for c in range(NC):
                    for b in range(BC * c, BC * (c + 1)):
                        ins = dve.tensor_scalar(XN[:, b, :], XN[:, b, :], SMALL[:, 96 + b:97 + b], ROUND, ALU.mult, ALU.add)
                    order(ins)
                    dve.tensor_scalar(flat(XQH[:, BC * c:BC * (c + 1), :]), flat(XN[:, BC * c:BC * (c + 1), :]), ROUND,
                                      None, ALU.subtract).then_inc(xn_ready[7], 1)
                dve.wait_ge(r_mm, 2)
                dve.tensor_scalar(RSG, bank[1][:, 0:P], TG[:, 7:8], None, ALU.mult).then_inc(r_cp, 1)
                dve.wait_ge(r_cp, 2)
                rsg = RSG.rearrange("p (o d) -> p o d", o=1).to_broadcast((P, BC, P))
                for c in range(NC):
                    dve.wait_ge(z_mm, c + 1)
                    dve.tensor_tensor(OC[:, c % 2, :].rearrange("p (b d) -> p b d", b=BC),
                                      bank[4 + c % 2][:].rearrange("p (b d) -> p b d", b=BC), rsg, ALU.mult).then_inc(z_cols, 1)
                    dve.wait_ge(z_cols, c + 1)
                    for i in range(BC):
                        b = BC * c + i
                        dve.scalar_tensor_tensor(out=X[:, b, :], in0=OC[:, c % 2, P * i:P * (i + 1)],
                                                 scalar=SMALL[:, 64 + b:65 + b], in1=X[:, b, :], op0=ALU.mult, op1=ALU.add
                                                 ).then_inc(z_out, 1)

            for c in range(2):
                projection_lo(key_job(0, c))
            dve.wait_ge(ld_x, 16)
            for c in range(NC):
                order(stats(X, MV, range(BC * c, BC * (c + 1))))
            for c in range(2, NC):
                projection_lo(key_job(0, c))
            attention(0)
            experts()
            attention(1)
            quantised_mlp()
            attention(2)
            fixed_point_mlp()
            attention(3)
            int8_product()


def _laid_out(x):
    f = np.float32
    m = np.arange(P)
    perm = DK * (NG * (m % 4) + m // 32) + m // 4 % 8
    t = [True, False, True, True]

    def w(L, name):
        v = np.asarray(x[f"L{L}_xattn_W{name}"])
        return v.T if t[L] else v

    def b(L, name):
        return np.asarray(x[f"L{L}_xattn_b{name}"]) if L < 2 else np.zeros(P, f)

    def row(*parts):
        return np.concatenate([np.asarray(p).reshape(-1) for p in parts]).reshape(1, -1)

    qk = [w(L, n)[:, perm] for n in "qk" for L in range(NL)]
    v = [w(L, "v") for L in range(NL)]
    up = np.concatenate([x["L0_ffn_up_w"], x["L0_ffn_sw_up"][None]])
    dn = np.concatenate([x["L0_ffn_down_w"], x["L0_ffn_sw_down"][None]])
    ub = np.concatenate([x["L0_ffn_up_b"], x["L0_ffn_sb_up"][None]])
    cols = ([b(L, "q")[perm] for L in range(NL)] + [b(L, "k")[perm] for L in range(NL)]
            + list(ub.reshape(NE * NI, P)) + list(x["L1_ffn_fc1_scales"].reshape(NI, P))
            + list(x["L1_ffn_fc1_bias"].reshape(NI, P)) + [x["L1_ffn_ln_gamma"], x["L1_ffn_ln_beta"]]
            + list(np.asarray(x["L0_ffn_gate_w"]).T))
    const = {side: np.zeros((DK, NG * CT), np.float16) for side in "qk"}
    const["q"][0] = BIG
    select = np.zeros((LO_AT + NH, NH), np.float16)
    for h in range(NH):
        select[[h, LO_AT + h], h] = BIG
    return {
        "watt": np.stack(qk + v, 1),
        "ctx_t": x["ctx_1024"].transpose(2, 0, 1).reshape(P, NB * P),
        "x": x["x"].transpose(1, 0, 2),
        "cols": np.stack(cols, 1),
        "rows": row(x["g_xattn"], x["g_ffn"], x["L0_ffn_bias"], np.arange(8, 0, -1, dtype=f),
                    *[b(L, "v") for L in range(NL)], *[b(L, "o") for L in range(NL)],
                    x["L1_ffn_fc2_bias"], x["L1_ffn_fc2_scales"]),
        "down_b": np.concatenate([x["L0_ffn_down_b"], x["L0_ffn_sb_down"][None]]),
        "up_w": up.transpose(1, 0, 2),
        "down_w": dn.reshape(NE, NI, P, P).transpose(2, 0, 1, 3).reshape(P, NE, CT),
        "w_l2": np.concatenate([np.asarray(x[f"L2_ffn_w_{n}"]).reshape(3, P, P).transpose(1, 0, 2).reshape(P, 3 * P)
                                for n in ("gate", "up")] + [x["L2_ffn_w_down"]], 1),
        "wo": np.stack([w(L, "o").reshape(NG, 4, DK, P).transpose(1, 0, 2, 3).reshape(P, P) for L in range(NL)], 1),
        "rhs_t": x["L3_ffn_rhs"].T,
        "fc1_q": x["L1_ffn_fc1_q"],
        "fc2_q": x["L1_ffn_fc2_q"].reshape(NI, P, P).transpose(1, 0, 2).reshape(P, CT),
        "mask1": x["mask_BxS2_if1"],
        "mask2": x["mask_BxSxS2_if1"].transpose(1, 0, 2),
        "mask3": np.asarray(x["mask_BxS2_bk1"]).view(np.int32),
        "select": select,
        "q_const": const["q"],
        "k_const": const["k"],
    }


def kernel(**inputs):
    import concourse.bacc as bacc
    from concourse.bass_utils import run_bass_kernel_spmd

    nc = bacc.Bacc("TRN2", target_bir_lowering=False, num_devices=1)
    arrays = {k: np.ascontiguousarray(v) for k, v in _laid_out({k: np.asarray(v) for k, v in inputs.items()}).items()}
    aps = {k: nc.dram_tensor(f"{k}_in", v.shape, mybir.dt.from_np(v.dtype), kind="ExternalInput").ap()
           for k, v in arrays.items()}
    out = nc.dram_tensor("out", (NB, P, P), F32, kind="ExternalOutput").ap()
    flamingo(nc, aps, out)
    r = run_bass_kernel_spmd(nc, [{f"{k}_in": v for k, v in arrays.items()}], core_ids=[0])
    return r.results[0]["out"]
```
